# Optimizing a Trainium2 kernel written in Bass

```python
import numpy as np
import jax
import jax.numpy as jnp

def _softmax(x, axis=-1):
    return jax.nn.softmax(x, axis=axis)

def _gelu(x):
    return jax.nn.gelu(x, approximate=True)

def _silu(x):
    return jax.nn.silu(x)

def _sigmoid(x):
    return jax.nn.sigmoid(x)

def _layernorm(x, axis=-1, eps=1e-05):
    m = jnp.mean(x, axis=axis, keepdims=True)
    v = jnp.var(x, axis=axis, keepdims=True)
    return (x - m) / jnp.sqrt(v + eps)

def _scatter_add(tgt, idx, src, axis=0):
    return tgt.at[idx].add(src)

def _segment_sum(src, seg, n):
    return jax.ops.segment_sum(src, seg, n)
kernel_name = 'mk_flamingo_gated_d2_seqx_r8_f74f97'

def setup_inputs(seed: int=0):
    np.random.seed(seed)
    _w = jnp.asarray

    def _rec_inputs():
        import jax
        import jax.numpy as jnp
        _rk = jax.random.key(seed)
        x = -0.0003929 + 0.9999 * jax.random.normal(jax.random.fold_in(_rk, 1), (2, 512, 128), jnp.float32)
        _lenS = 512 - jax.random.randint(jax.random.fold_in(_rk, 7), (2,), 0, max(1, 512 // 4) + 1, jnp.int32)
        _lenS2 = 77 - jax.random.randint(jax.random.fold_in(_rk, 8), (2,), 0, max(1, 77 // 4) + 1, jnp.int32)
        _ctx_768P = jax.random.normal(jax.random.fold_in(_rk, 11), (2, 16, 96), jnp.float32)
        _ctx_768c = jax.random.dirichlet(jax.random.fold_in(_rk, 511), 0.3 * jnp.ones((16,), jnp.float32), (2, 77))
        _ctx_768t = jnp.einsum('bsk,bkd->bsd', _ctx_768c, _ctx_768P)
        _ctx_768t = _ctx_768t * jax.lax.rsqrt(jnp.mean(jnp.square(_ctx_768t)) + 1e-12) * 0.953939
        ctx_768 = -7.36909e-05 + 0.999899 * (_ctx_768t + 0.3 * jax.random.normal(jax.random.fold_in(_rk, 611), (2, 77, 96), jnp.float32))
        _g = jax.random.normal(jax.random.fold_in(_rk, 9001), (2, 2), jnp.float32)
        _g = jnp.sign(_g) * jnp.maximum(jnp.abs(_g), 1.0) + (_g == 0) * 1.0
        g_xattn = _g[0]
        g_ffn = _g[1]
        return (x, ctx_768, g_xattn, g_ffn)
    x, ctx_768, g_xattn, g_ffn = _rec_inputs()

    def _L0_xattn_setup():
        import jax, jax.numpy as jnp
        import numpy as np
        IMG_DIM, TXT_DIM, HID = (128, 96, 128)
        B, LQ, LK = (8, 256, 256)
        key = jax.random.key(seed)
        ks = jax.random.split(key, 8)
        s_img = 1.0 / np.sqrt(IMG_DIM)
        s_txt = 1.0 / np.sqrt(TXT_DIM)
        return {'image_features': jax.random.normal(ks[0], (B, LQ, IMG_DIM), jnp.float32), 'text_features': jax.random.normal(ks[1], (B, LK, TXT_DIM), jnp.float32), 'Wq': jax.random.uniform(ks[2], (IMG_DIM, HID), jnp.float32, -s_img, s_img), 'bq': jax.random.uniform(ks[3], (HID,), jnp.float32, -s_img, s_img), 'Wk': jax.random.uniform(ks[4], (TXT_DIM, HID), jnp.float32, -s_txt, s_txt), 'bk': jax.random.uniform(ks[5], (HID,), jnp.float32, -s_txt, s_txt), 'Wv': jax.random.uniform(ks[6], (TXT_DIM, HID), jnp.float32, -s_txt, s_txt), 'bv': jax.random.uniform(ks[7], (HID,), jnp.float32, -s_txt, s_txt)}
    _L0_xattn_all = _L0_xattn_setup()
    _L0_xattn_in = {k: v for k, v in _L0_xattn_all.items() if k in ('Wq', 'bq', 'Wk', 'bk', 'Wv', 'bv')}
    del _L0_xattn_all

    def _L0_ffn_setup():
        import jax, jax.numpy as jnp
        import numpy as np
        D_MODEL = 128
        D_HIDDEN = 512
        NUM_EXPERTS = 8
        B, T = (2, 256)
        key = jax.random.key(seed)
        ks = jax.random.split(key, 8)
        s = 0.02
        x = jax.random.normal(ks[0], (B, T, D_MODEL), dtype=jnp.float32)
        Wg = jax.random.normal(ks[1], (D_MODEL, NUM_EXPERTS), dtype=jnp.float32) * s
        bg = jnp.zeros((NUM_EXPERTS,), dtype=jnp.float32)
        W1 = jax.random.normal(ks[2], (NUM_EXPERTS, D_MODEL, D_HIDDEN), dtype=jnp.float32) * s
        b1 = jnp.zeros((NUM_EXPERTS, D_HIDDEN), dtype=jnp.float32)
        W2 = jax.random.normal(ks[3], (NUM_EXPERTS, D_HIDDEN, D_MODEL), dtype=jnp.float32) * s
        b2 = jnp.zeros((NUM_EXPERTS, D_MODEL), dtype=jnp.float32)
        return {'x': x, 'Wg': Wg, 'bg': bg, 'W1': W1, 'b1': b1, 'W2': W2, 'b2': b2}
    _L0_ffn_all = _L0_ffn_setup()
    _L0_ffn_in = {k: v for k, v in _L0_ffn_all.items() if k in ('Wg', 'bg', 'W1', 'b1', 'W2', 'b2')}
    del _L0_ffn_all

    def _L1_xattn_setup():
        import jax, jax.numpy as jnp
        import numpy as np
        import math
        B, L, E = (16, 512, 128)
        LC, EC = (77, 96)
        H = 16
        DH = E // H
        key = jax.random.key(seed)
        ks = jax.random.split(key, 10)
        s = 0.02
        return {'x': jax.random.normal(ks[0], (B, L, E), jnp.float32), 'cross': jax.random.normal(ks[1], (B, LC, EC), jnp.float32), 'q_w': jax.random.normal(ks[2], (E, E), jnp.float32) * s, 'q_b': jax.random.normal(ks[3], (E,), jnp.float32) * s, 'k_w': jax.random.normal(ks[4], (E, EC), jnp.float32) * s, 'k_b': jax.random.normal(ks[5], (E,), jnp.float32) * s, 'v_w': jax.random.normal(ks[6], (E, EC), jnp.float32) * s, 'v_b': jax.random.normal(ks[7], (E,), jnp.float32) * s, 'o_w': jax.random.normal(ks[8], (E, E), jnp.float32) * s, 'o_b': jax.random.normal(ks[9], (E,), jnp.float32) * s}
    _L1_xattn_all = _L1_xattn_setup()
    _L1_xattn_in = {k: v for k, v in _L1_xattn_all.items() if k in ('q_w', 'q_b', 'k_w', 'k_b', 'v_w', 'v_b', 'o_w', 'o_b')}
    del _L1_xattn_all

    def _L1_ffn_setup():
        import math
        import jax
        import jax.numpy as jnp
        import numpy as np
        B, T, D = (1, 256, 128)
        H, KV, DH = (16, 4, 64)
        E, TOPK, DFF = (32, 4, 128)
        WINDOW = 128
        EPS = 1e-05
        ROPE_BASE = 150000.0
        ROPE_SCALE = 32.0

        def _rmsnorm(x, w):
            rms = jax.lax.rsqrt(jnp.mean(x * x, axis=-1, keepdims=True) + EPS)
            return w * (x * rms)

        def _apply_rope(x, sin, cos):
            x1, x2 = (x[..., ::2], x[..., 1::2])
            out = jnp.stack([x1 * cos - x2 * sin, x1 * sin + x2 * cos], axis=-1)
            return out.reshape(x.shape)
        key = jax.random.key(seed)
        ks = jax.random.split(key, 12)
        s = 0.02
        return {'x': jax.random.normal(ks[0], (B, T, D), jnp.float32), 'attn_norm_w': 1.0 + 0.02 * jax.random.normal(ks[1], (D,), jnp.float32), 'ffn_norm_w': 1.0 + 0.02 * jax.random.normal(ks[2], (D,), jnp.float32), 'qkv_w': s * jax.random.normal(ks[3], (D, H * DH + 2 * KV * DH), jnp.float32), 'qkv_b': s * jax.random.normal(ks[4], (H * DH + 2 * KV * DH,), jnp.float32), 'proj_w': s * jax.random.normal(ks[5], (H * DH, D), jnp.float32), 'proj_b': s * jax.random.normal(ks[6], (D,), jnp.float32), 'attn_sink': 0.5 * jax.random.normal(ks[7], (H,), jnp.float32), 'gate_w': s * jax.random.normal(ks[8], (D, E), jnp.float32), 'gate_b': s * jax.random.normal(ks[9], (E,), jnp.float32), 'W_up': s * jax.random.normal(ks[10], (E, D, 2 * DFF), jnp.float32), 'W_down': s * jax.random.normal(ks[11], (E, DFF, D), jnp.float32)}
    _L1_ffn_all = _L1_ffn_setup()
    _L1_ffn_in = {k: v for k, v in _L1_ffn_all.items() if k in ('attn_norm_w', 'ffn_norm_w', 'qkv_w', 'qkv_b', 'proj_w', 'proj_b', 'attn_sink', 'gate_w', 'gate_b', 'W_up', 'W_down')}
    del _L1_ffn_all
    return {'x': x, 'ctx_768': ctx_768, 'g_xattn': g_xattn, 'g_ffn': g_ffn, 'L0_xattn_Wq': _L0_xattn_in['Wq'], 'L0_xattn_bq': _L0_xattn_in['bq'], 'L0_xattn_Wk': _L0_xattn_in['Wk'], 'L0_xattn_bk': _L0_xattn_in['bk'], 'L0_xattn_Wv': _L0_xattn_in['Wv'], 'L0_xattn_bv': _L0_xattn_in['bv'], 'L0_ffn_Wg': _L0_ffn_in['Wg'], 'L0_ffn_bg': _L0_ffn_in['bg'], 'L0_ffn_W1': _L0_ffn_in['W1'], 'L0_ffn_b1': _L0_ffn_in['b1'], 'L0_ffn_W2': _L0_ffn_in['W2'], 'L0_ffn_b2': _L0_ffn_in['b2'], 'L1_xattn_q_w': _L1_xattn_in['q_w'], 'L1_xattn_q_b': _L1_xattn_in['q_b'], 'L1_xattn_k_w': _L1_xattn_in['k_w'], 'L1_xattn_k_b': _L1_xattn_in['k_b'], 'L1_xattn_v_w': _L1_xattn_in['v_w'], 'L1_xattn_v_b': _L1_xattn_in['v_b'], 'L1_xattn_o_w': _L1_xattn_in['o_w'], 'L1_xattn_o_b': _L1_xattn_in['o_b'], 'L1_ffn_attn_norm_w': _L1_ffn_in['attn_norm_w'], 'L1_ffn_ffn_norm_w': _L1_ffn_in['ffn_norm_w'], 'L1_ffn_qkv_w': _L1_ffn_in['qkv_w'], 'L1_ffn_qkv_b': _L1_ffn_in['qkv_b'], 'L1_ffn_proj_w': _L1_ffn_in['proj_w'], 'L1_ffn_proj_b': _L1_ffn_in['proj_b'], 'L1_ffn_attn_sink': _L1_ffn_in['attn_sink'], 'L1_ffn_gate_w': _L1_ffn_in['gate_w'], 'L1_ffn_gate_b': _L1_ffn_in['gate_b'], 'L1_ffn_W_up': _L1_ffn_in['W_up'], 'L1_ffn_W_down': _L1_ffn_in['W_down']}

def reference(x, ctx_768, g_xattn, g_ffn, L0_xattn_Wq, L0_xattn_bq, L0_xattn_Wk, L0_xattn_bk, L0_xattn_Wv, L0_xattn_bv, L0_ffn_Wg, L0_ffn_bg, L0_ffn_W1, L0_ffn_b1, L0_ffn_W2, L0_ffn_b2, L1_xattn_q_w, L1_xattn_q_b, L1_xattn_k_w, L1_xattn_k_b, L1_xattn_v_w, L1_xattn_v_b, L1_xattn_o_w, L1_xattn_o_b, L1_ffn_attn_norm_w, L1_ffn_ffn_norm_w, L1_ffn_qkv_w, L1_ffn_qkv_b, L1_ffn_proj_w, L1_ffn_proj_b, L1_ffn_attn_sink, L1_ffn_gate_w, L1_ffn_gate_b, L1_ffn_W_up, L1_ffn_W_down):
    import jax
    import jax.numpy as jnp

    def _L0_xattn_ref(image_features, text_features, Wq, bq, Wk, bk, Wv, bv):
        import jax, jax.numpy as jnp
        import numpy as np
        IMG_DIM, TXT_DIM, HID = (128, 96, 128)
        B, LQ, LK = (8, 256, 256)
        query = jnp.einsum('bqi,ih->bqh', image_features, Wq) + bq
        key = jnp.einsum('bkt,th->bkh', text_features, Wk) + bk
        value = jnp.einsum('bkt,th->bkh', text_features, Wv) + bv
        scale = 1.0 / jnp.sqrt(jnp.asarray(HID, query.dtype))
        scores = jnp.einsum('bqh,bkh->bqk', query, key) * scale
        weights = jax.nn.softmax(scores, axis=-1)
        attended = jnp.einsum('bqk,bkh->bqh', weights, value)
        return attended

    def _L0_ffn_ref(x, Wg, bg, W1, b1, W2, b2):
        import jax, jax.numpy as jnp
        import numpy as np
        D_MODEL = 128
        D_HIDDEN = 512
        NUM_EXPERTS = 8
        B, T = (2, 256)
        gate_logits = jnp.einsum('btd,de->bte', x, Wg) + bg
        gate_scores = jax.nn.softmax(gate_logits, axis=-1)
        top1_idx = jnp.argmax(gate_scores, axis=-1)
        top1_mask = jax.nn.one_hot(top1_idx, NUM_EXPERTS, dtype=x.dtype)
        top1_weight = jnp.sum(gate_scores * top1_mask, axis=-1, keepdims=True)
        h = jax.nn.silu(jnp.einsum('btd,edh->bteh', x, W1) + b1)
        o = jnp.einsum('bteh,ehd->bted', h, W2) + b2
        y = jnp.sum(o * top1_mask[..., None], axis=2) * top1_weight
        return y

    def _L1_xattn_ref(x, cross, q_w, q_b, k_w, k_b, v_w, v_b, o_w, o_b):
        import jax, jax.numpy as jnp
        import numpy as np
        import math
        B, L, E = (16, 512, 128)
        LC, EC = (77, 96)
        H = 16
        DH = E // H
        b, l, e = x.shape
        q = jnp.einsum('ble,fe->blf', x, q_w) + q_b
        k = jnp.einsum('bce,fe->bcf', cross, k_w) + k_b
        v = jnp.einsum('bce,fe->bcf', cross, v_w) + v_b
        q = q.reshape(b, l, H, DH).transpose(0, 2, 1, 3)
        v = v.reshape(b, -1, H, DH).transpose(0, 2, 1, 3)
        scores = jnp.einsum('bhld,bhcd->bhlc', q, v) / math.sqrt(DH)
        attn = jax.nn.softmax(scores, axis=-1)
        qkv = jnp.einsum('bhlc,bhcd->bhld', attn, v)
        qkv = qkv.reshape(b, l, e)
        out = jnp.einsum('ble,fe->blf', qkv, o_w) + o_b
        return out

    def _L1_ffn_ref(x, attn_norm_w, ffn_norm_w, qkv_w, qkv_b, proj_w, proj_b, attn_sink, gate_w, gate_b, W_up, W_down):
        import math
        import jax
        import jax.numpy as jnp
        import numpy as np
        B, T, D = (1, 256, 128)
        H, KV, DH = (16, 4, 64)
        E, TOPK, DFF = (32, 4, 128)
        WINDOW = 128
        EPS = 1e-05
        ROPE_BASE = 150000.0
        ROPE_SCALE = 32.0

        def _rmsnorm(x, w):
            rms = jax.lax.rsqrt(jnp.mean(x * x, axis=-1, keepdims=True) + EPS)
            return w * (x * rms)

        def _apply_rope(x, sin, cos):
            x1, x2 = (x[..., ::2], x[..., 1::2])
            out = jnp.stack([x1 * cos - x2 * sin, x1 * sin + x2 * cos], axis=-1)
            return out.reshape(x.shape)
        Bx, Tx, Dx = x.shape
        h = _rmsnorm(x, attn_norm_w)
        qkv = h @ qkv_w + qkv_b
        q = qkv[..., :H * DH].reshape(Bx, Tx, H, DH).transpose(0, 2, 1, 3)
        k = qkv[..., H * DH:H * DH + KV * DH].reshape(Bx, Tx, KV, DH).transpose(0, 2, 1, 3)
        v = qkv[..., H * DH + KV * DH:].reshape(Bx, Tx, KV, DH).transpose(0, 2, 1, 3)
        pos = jnp.arange(Tx, dtype=jnp.float32) / ROPE_SCALE
        inv_freq = 1.0 / ROPE_BASE ** (jnp.arange(0, DH, 2, dtype=jnp.float32) / DH)
        freqs = pos[:, None] * inv_freq[None, :]
        sin, cos = (jnp.sin(freqs), jnp.cos(freqs))
        q = _apply_rope(q, sin, cos)
        k = _apply_rope(k, sin, cos)
        rep = H // KV
        k = jnp.repeat(k, rep, axis=1)
        v = jnp.repeat(v, rep, axis=1)
        logits = jnp.einsum('bhqd,bhkd->bhqk', q, k) / math.sqrt(DH)
        i = jnp.arange(Tx)[:, None]
        j = jnp.arange(Tx)[None, :]
        mask = (j > i) | (i - j > WINDOW)
        logits = jnp.where(mask, -jnp.inf, logits)
        lse = jax.nn.logsumexp(logits, axis=-1, keepdims=True)
        denom_log = jnp.logaddexp(lse, attn_sink.reshape(1, H, 1, 1))
        attn = jnp.exp(logits - denom_log)
        y = jnp.einsum('bhqk,bhkd->bhqd', attn, v)
        y = y.transpose(0, 2, 1, 3).reshape(Bx, Tx, H * DH)
        x = x + (y @ proj_w + proj_b)
        h2 = _rmsnorm(x, ffn_norm_w).reshape(Bx * Tx, Dx)
        glogits = h2 @ gate_w + gate_b
        topv, topi = jax.lax.top_k(glogits, TOPK)
        gw = jax.nn.softmax(topv, axis=-1)
        N = Bx * Tx
        combine = jnp.zeros((N, E), x.dtype).at[jnp.arange(N)[:, None], topi].add(gw)

        def body(acc, we):
            wu, wd, ce = we
            ug = h2 @ wu
            u, g = (ug[:, :DFF], ug[:, DFF:])
            return (acc + ce[:, None] * (jax.nn.silu(g) * u @ wd), None)
        y2, _ = jax.lax.scan(body, jnp.zeros_like(h2), (W_up, W_down, combine.T))
        return x + y2.reshape(Bx, Tx, Dx)
    x = x + jnp.tanh(g_xattn[0]) * _L0_xattn_ref(_layernorm(x, axis=-1), ctx_768, L0_xattn_Wq, L0_xattn_bq, L0_xattn_Wk, L0_xattn_bk, L0_xattn_Wv, L0_xattn_bv)
    x = x + jnp.tanh(g_ffn[0]) * _L0_ffn_ref(_layernorm(x, axis=-1), L0_ffn_Wg, L0_ffn_bg, L0_ffn_W1, L0_ffn_b1, L0_ffn_W2, L0_ffn_b2)
    x = x + jnp.tanh(g_xattn[1]) * _L1_xattn_ref(_layernorm(x, axis=-1), ctx_768, L1_xattn_q_w, L1_xattn_q_b, L1_xattn_k_w, L1_xattn_k_b, L1_xattn_v_w, L1_xattn_v_b, L1_xattn_o_w, L1_xattn_o_b)
    x = x + jnp.tanh(g_ffn[1]) * _L1_ffn_ref(_layernorm(x, axis=-1), L1_ffn_attn_norm_w, L1_ffn_ffn_norm_w, L1_ffn_qkv_w, L1_ffn_qkv_b, L1_ffn_proj_w, L1_ffn_proj_b, L1_ffn_attn_sink, L1_ffn_gate_w, L1_ffn_gate_b, L1_ffn_W_up, L1_ffn_W_down)
    return x

_drawn_inputs = setup_inputs


def setup_inputs(seed=0):
    import zlib

    import numpy as np

    out = dict(_drawn_inputs(seed))
    spreads = {'g_ffn': (-1.0, 0.2),
     'L0_ffn_bg': (0.0, 0.8),
     'L0_ffn_b1': (0.0, 0.8),
     'L0_ffn_b2': (0.0, 0.565)}
    factors = {'L0_xattn_bq': 8.0,
     'L0_xattn_bk': 200.0,
     'L0_ffn_Wg': 3.871,
     'L0_ffn_W1': 8.0,
     'L0_ffn_W2': 7.27,
     'L1_xattn_q_w': 31.725,
     'L1_xattn_q_b': 200.0,
     'L1_xattn_v_b': 8.0,
     'L1_ffn_attn_norm_w': 8.0,
     'L1_ffn_ffn_norm_w': 8.0,
     'L1_ffn_attn_sink': 8.0,
     'L1_ffn_gate_w': 5.657,
     'L1_ffn_gate_b': 8.0,
     'L1_ffn_W_up': 5.3,
     'L1_ffn_W_down': 5.274}
    for name, (base, spread) in spreads.items():
        noise = np.random.default_rng([zlib.crc32(name.encode()), seed]).standard_normal(out[name].shape)
        drawn = base * np.exp(spread * noise) if base else spread * noise
        out[name] = jnp.asarray(drawn.astype(out[name].dtype))
    for name, factor in factors.items():
        out[name] = (out[name] * factor).astype(out[name].dtype)
    return out
```

```python
from contextlib import ExitStack

import numpy as np

import concourse.bass as bass
from concourse import mybir
from concourse.alu_op_type import AluOpType as ALU

F32 = mybir.dt.float32
F32R = mybir.dt.float32r
U32 = mybir.dt.uint32
ACT = mybir.ActivationFunctionType
AX = mybir.AxisListType

P = 128
EPS = 1e-5


def constants():
    lc, heads, d, chunks = 77, 16, 128, 10
    flat = np.arange(chunks * P)
    head = np.where(flat < heads * lc, flat // lc, -1)
    token = np.where(flat < heads * lc, flat % lc, -1)
    own = np.concatenate([head[:, None] == np.arange(d)[None] // (d // heads),
                          head[:, None] == np.arange(heads)[None]], axis=1).astype(np.float32)
    seq, window, dh = 512, 128, 64
    inv_freq = (1.0 / np.float32(150000.0) ** (np.arange(0, dh, 2, dtype=np.float32) / np.float32(dh))).astype(np.float32)
    pos = np.arange(seq, dtype=np.float32) / np.float32(32.0)
    angle = (inv_freq[:, None] * pos[None, :]).astype(np.float32)[(np.arange(P) % dh) // 2]
    sign = np.where(np.arange(P) % 2 == 0, -1.0, 1.0)[:, None]
    r, c = np.arange(P)[:, None], np.arange(P)[None]
    masked = np.concatenate([r - c > 0, c > r], axis=1)
    return {
        "c_ident": np.eye(P, dtype=np.float32),
        "c_rev": np.arange(8, 0, -1).astype(np.float32),
        "c_head_cols": (np.arange(d)[:, None] // (d // heads) == np.arange(heads)[None]).astype(np.float32),
        "c_repeat_ctx": (np.arange(lc)[:, None] == token[None]).astype(np.float32),
        "c_own_head": own.reshape(chunks, P, d + heads).transpose(1, 0, 2).copy(),
        "c_cos": np.cos(angle.astype(np.float64)).astype(np.float32),
        "c_sin": (sign * np.sin(angle.astype(np.float64))).astype(np.float32),
        "c_window": np.where(masked, np.float32(-1e30), np.float32(0)).astype(np.float32),
        "c_experts": np.arange(32).astype(np.float32),
    }


def qkv_by_group(w, b):
    heads, kv, dh = 16, 4, 64
    columns = []
    for g in range(kv):
        q = np.arange(g * (heads // kv) * dh, (g + 1) * (heads // kv) * dh)
        k = np.tile(heads * dh + np.arange(g * dh, (g + 1) * dh), 2)
        columns.append(np.concatenate([q, q ^ 1, k, k ^ 1]))
    columns = np.stack(columns)
    return {"qkv_w_groups": np.ascontiguousarray(w[:, columns].transpose(1, 0, 2)),
            "qkv_b_groups": np.ascontiguousarray(b[columns].reshape(-1, P).T)}


def spread(ap, axis, n):
    wide = ap.unsqueeze(axis)
    shape = list(wide.shape)
    shape[axis] = n
    return wide.broadcast_to(shape)


def flamingo_two_layers(nc, t, out):
    NB, SEQ, D = t["x"].shape
    LC, DC = t["ctx_768"].shape[1:]
    TPB = SEQ // P
    NT = NB * TPB
    T = NB * SEQ
    E0, _, F0 = t["L0_ffn_W1"].shape
    C0 = F0 // P
    E1, _, F1x2 = t["L1_ffn_W_up"].shape
    TOPK = 4
    H1 = 16
    DH1 = D // H1
    HK = H1 * LC
    HEADS, KV, DH, WINDOW = 16, 4, 64, 128
    QD, KD = HEADS * DH, KV * DH
    PAIRS = HEADS // 2
    HALVES = T // 512
    assert D == P and WINDOW == P and SEQ == 512 and F1x2 == 2 * P

    ctx = ExitStack()
    with ctx:
        def sb(name, shape, dt=F32):
            return ctx.enter_context(nc.sbuf_tensor(name, list(shape), dt))

        def sem(name):
            return ctx.enter_context(nc.semaphore(name))

        bank = [ctx.enter_context(nc.psum_tensor(f"bank{i}", [P, 512], F32)) for i in range(2)]
        mid3 = ctx.enter_context(nc.psum_tensor("mid3", [P, 3, 512], F32))
        bank += [mid3[:, i, :] for i in range(3)]
        bank += [ctx.enter_context(nc.psum_tensor(f"bank{i}", [P, 512], F32)) for i in range(5, 6)]
        top2 = ctx.enter_context(nc.psum_tensor("top2", [P, 2, 512], F32))
        bank += [top2[:, i, :] for i in range(2)]

        ident = sb("ident", [P, P])
        X = sb("X", [P, NT, D])
        XN = sb("XN", [P, NT, D])
        XR = sb("XR", [P, NT, D])
        X1 = sb("X1", [P, NT, D])
        XT = sb("XT", [P, T])
        XTH = sb("XTH", [P, T], F32R)
        XTL = sb("XTL", [P, T], F32R)
        stats = sb("stats", [P, NT, 6])
        mv = sb("mv", [P, NT, 2])
        ve = sb("ve", [P, NT])
        rstd = sb("rstd", [P, NT])
        minus_half = sb("minus_half", [P, NT])

        ctx_rows = sb("ctx_rows", [LC, NB, DC])
        wk0 = sb("wk0", [DC, D])
        wv0 = sb("wv0", [DC, D])
        wq0 = sb("wq0", [P, D])
        qw1 = sb("qw1", [P, D])
        ow1 = sb("ow1", [P, D])
        vw1 = sb("vw1", [P, DC])
        NROWS = 6
        rows = sb("rows", [NROWS, P])
        cols = sb("cols", [P, NROWS])
        BQ, BK, QB, VB, ATTN_W, FFN_W = range(NROWS)
        bias_v = sb("bias_v", [LC, 4, D])
        gate_in = sb("gate_in", [P, 4])
        gate = sb("gate", [P, 4])
        ctxT = sb("ctxT", [DC, NB * LC])
        WT = sb("WT", [P, 4, D])
        KT0 = sb("KT0", [P, NB * LC])
        KA = sb("KA", [P, NB * LC])
        BQW = sb("BQW", [P, P])
        VV = sb("VV", [LC, 2, NB, D])
        V1T = sb("V1T", [P, NB * LC])
        SA = sb("SA", [P, NT, LC])
        mA = sb("mA", [P, NT])
        lA = sb("lA", [P, NT])
        rA = sb("rA", [P, NT])
        PTA = sb("PTA", [LC, NT, P])

        UP_RING, H_RING, LEAD0, LEAD1 = 4, 4, 5, 3
        NP0, NP1 = E0 // 2, E1 // 2
        BLK0 = C0 * HALVES
        b1 = sb("b1", [P, 2, C0])
        wg0 = sb("wg0", [P, E0])
        bg0 = sb("bg0", [P, E0])
        rev0 = sb("rev0", [P, E0])
        b2 = sb("b2", [E0, D])
        GL = sb("GL", [P, NT, E0])
        EQ = sb("EQ", [P, NT, E0])
        gm = sb("gm", [P, NT])
        gs = sb("gs", [P, NT])
        CM = sb("CM", [P, NT, E0])
        CT8 = sb("CT8", [E0, T])
        CE = sb("CE", [P, 2, T])
        W1 = sb("W1", [P, 2, F0])
        W1H = sb("W1H", [P, 2, F0], F32R)
        W1L = sb("W1L", [P, 2, F0], F32R)
        W2 = sb("W2", [P, 2, C0, D])
        W2H = sb("W2H", [P, 2, C0, D], F32R)
        W2L = sb("W2L", [P, 2, C0, D], F32R)
        HA = sb("HA", [P, H_RING, 512])
        HC = sb("HC", [P, H_RING, 512])
        HH = sb("HH", [P, H_RING, 512], F32R)
        HL = sb("HL", [P, H_RING, 512], F32R)
        YT = sb("YT", [P, T])
        c0_dram = nc.dram_tensor("c0_dram", [E0, T], F32).ap()

        NCH = (HK + P - 1) // P
        DEN = D + H1
        GROUPS = ((0, 6), (6, 6), (12, 4))
        head_cols = sb("head_cols", [P, H1])
        repeat_ctx = sb("repeat_ctx", [LC, NCH * P])
        own_head = sb("own_head", [P, NCH, DEN])
        VTH = sb("VTH", [P, NB, HK], F32R)
        VTL = sb("VTL", [P, NB, HK], F32R)
        V1TH = sb("V1TH", [P, NB * LC], F32R)
        V1TL = sb("V1TL", [P, NB * LC])
        VBD = sb("VBD", [P, NB, NCH, DEN])
        SC = sb("SC", [P, 2, HK])
        PTC = sb("PTC", [P, NCH, P])
        mC = sb("mC", [P, 2, H1])
        rC = sb("rC", [P, 2, H1])
        STR = D // DH1
        AA = SEQ // STR
        OA = sb("OA", [AA, NB, H1, STR, DH1])
        OT = sb("OT", [P, NB, SEQ])
        ob = sb("ob", [P, D])


        NG = NB * KV
        NU = NB * PAIRS
        NQ = NU * TPB
        GW = 6 * P
        flat = "p a b -> p (a b)"
        w_raw = W1[:].rearrange(flat)
        WH, WL = W1H[:].rearrange(flat), W1L[:].rearrange(flat)
        proj_w = W2[:].rearrange("p a c d -> p (a c) d")
        QH = HH
        QL = W2H[:].rearrange("p a c d -> p a (c d)")
        KHH = W2L[:].rearrange("p a c d -> p a (c d)")
        KL = (HL[:, 0:2, :], HL[:, 2:4, :])
        UQ = [v[:].rearrange("p b k -> p (b k)")[:, s * 1024:(s + 1) * 1024].rearrange("p (h t) -> p h t", h=2)
              for v in (VTH, VTL) for s in range(2)]
        SM = HA
        T1, T2 = HC[:, 0:2, :], HC[:, 2:4, :]
        VS = CE[:].rearrange("p j (i d) -> p (j i) d", d=KD)
        sc_flat = SC[:].rearrange("p s k -> p (s k)")
        TS = sc_flat[:, 0:1024].rearrange("p (s k) -> p s k", s=2)
        YS = sc_flat[:, 1024:2048].rearrange("p (s k) -> p s k", s=2)
        PT = PTC[:].rearrange("p c k -> p (c k)")[:, 0:1024].rearrange("p (s k) -> p s k", s=2)
        YTC = VBD[:].rearrange("p b c k -> p (b c k)")[:, 0:1024].rearrange("p (s k) -> p s k", s=2)
        own_flat = own_head[:].rearrange("p c k -> p (c k)")
        cosT, sinT, window = own_flat[:, 0:SEQ], own_flat[:, SEQ:2 * SEQ], own_flat[:, 2 * SEQ:2 * SEQ + 2 * P]
        qkv_bias = sb("qkv_bias", [P, KV * 6])
        v_bias = sb("v_bias", [P, KD])
        proj_b = sb("proj_b", [P, D])
        sink = sb("sink", [P, HEADS])
        nsink = sb("nsink", [P, HEADS])
        rms = sb("rms", [P, NT])
        mD = sb("mD", [P, 4, 2])
        nm = sb("nm", [P, 2, TPB, 2])
        zs = sb("zs", [P, 2, TPB, 2])
        lD = sb("lD", [P, 2, TPB, 2])
        den = sb("den", [P, 2, TPB, 2])

        def rope_block(r):
            if r == 0:
                return "k", 0
            if r < 3:
                return "q", r - 1
            g = r // 3 - 1
            return (("q", 2 * g + 2), ("k", g + 1), ("q", 2 * g + 3))[r % 3]

        BLOCK_OF = {rope_block(r): r for r in range(3 * NG)}
        ROPE_AT = {8 * g + s: 3 * g + 3 + k for g in range(NG - 1) for k, s in enumerate((3, 5, 7))}

        NB1 = E1 * HALVES
        QUAD = 4
        ZU, ZD = [[w[:].rearrange(pat)[:, 0:QUAD * n].rearrange("p (s f) -> p s f", s=QUAD)
                   for w in ws] for ws, pat, n in (((W1, W1H, W1L), "p a b -> p (a b)", F1x2),
                                                   ((W2, W2H, W2L), "p a c d -> p (a c d)", D))]
        CZ = [CE[:, 0, :], CE[:, 1, :], sc_flat[:, 0:T], sc_flat[:, T:2 * T]]
        CT1 = YT[0:E1, :]
        EQ4 = XN[:].rearrange("p u d -> p (u d)").rearrange("p (u e k) -> p u e k", u=NT, k=TOPK)
        gate_w = sb("gate_w", [P, E1])
        gate_b = sb("gate_b", [P, E1])
        experts = sb("experts", [P, E1])
        GZ = sb("GZ", [P, NT, E1])
        m8 = sb("m8", [P, NT, 8])
        i8 = sb("i8", [P, NT, 8], U32)
        if8 = sb("if8", [P, NT, TOPK])
        wt = sb("wt", [P, NT, TOPK])
        wsum = sb("wsum", [P, NT])
        c1_dram = nc.dram_tensor("c1_dram", [E1, T], F32).ap()

        s_id = sem("ident_loaded")
        s_x = [sem(f"x_loaded{b}") for b in range(NB)]
        s_w0 = sem("setup_weights_loaded")
        s_b0 = sem("setup_biases_loaded")
        s_st = sem("row_stats")
        s_mv = sem("row_mean_var")
        s_ve = sem("var_eps")
        s_rs = sem("rstd")
        s_xn = sem("xn")
        s_xu = sem("x_updated")
        s_xtp = sem("xt_in_psum")
        s_xt = sem("xt")
        s_mh = sem("minus_half_set")
        s_g = sem("gate_tanh")
        s_p1 = sem("setup_transposes")
        s_e1 = sem("setup_evacuated")
        s_bq = sem("bq_spread")
        s_kt = sem("kt0_out")
        s_vw = sem("v_w_transposed")
        s_p2 = sem("setup_products")
        s_e2 = sem("setup_products_out")
        s_p3 = sem("ka_product")
        s_e3 = sem("ka_out")
        sa_s = sem("a_scores")
        sa_m = sem("a_max")
        sa_c = sem("a_centred")
        sa_e = sem("a_exp")
        sa_l = sem("a_sum")
        sa_r = sem("a_recip")
        sa_g = sem("a_recip_gate")
        sa_t = sem("a_pT_in_psum")
        sa_p = sem("a_pT")
        sa_o = sem("a_out")
        s_st1 = sem("stored")
        s_xth = sem("xt_high")
        s_xtl = sem("xt_low")
        s_rl = sem("router_inputs_loaded")
        b_lg = sem("b_logits")
        b_d = sem("b_router_vector_steps")
        b_ex = sem("b_router_exp")
        b_cm = sem("b_weights")
        b_ctp = sem("b_weights_transposed")
        b_ct = sem("b_weights_T")
        b_cs = sem("b_weights_stored")
        b_ce = [sem(f"b_weights_spread{i}") for i in range(2)]
        b_b1 = [sem(f"b_biases_loaded{i}") for i in range(2)]
        b_w1 = [sem(f"b_w1_loaded{i}") for i in range(2)]
        b_w2 = [sem(f"b_w2_loaded{i}") for i in range(2)]
        b_w1h = sem("b_w1_high")
        b_w1l = sem("b_w1_low")
        b_w2h = sem("b_w2_high")
        b_w2l = sem("b_w2_low")
        b_up = sem("b_up_products")
        b_si = sem("b_silu")
        b_mv = sem("b_weighted_by_vector")
        b_mp = sem("b_weighted_by_gpsimd")
        b_hh = sem("b_hidden_high")
        b_hl = sem("b_hidden_low")
        b_dn = sem("b_down_products")
        b_yt = sem("b_y_out")
        b_yp = sem("b_y_transposed")
        s_cc = sem("c_constants_loaded")
        c_vh = sem("c_values_split")
        c_vt = sem("c_values_by_head")
        c_vp = sem("c_values_repeated")
        c_vb = sem("c_values_block_diagonal")
        c_q = sem("c_queries")
        c_qh = sem("c_queries_high")
        c_qt = sem("c_queries_out")
        c_ql = sem("c_queries_low")
        c_s = sem("c_scores")
        c_m = sem("c_max")
        c_c = sem("c_centred")
        c_e = sem("c_exp")
        c_tp = sem("c_pT_in_psum")
        c_p = sem("c_pT")
        c_o = sem("c_out")
        c_r = sem("c_recip")
        c_n = sem("c_normed")
        c_otp = sem("c_outT_in_psum")
        c_ot = sem("c_outT")
        c_y = sem("c_projected")
        c_ob = sem("c_bias_gated")
        c_xb = sem("c_bias_added")
        s_rr = sem("rms_steps")
        s_xr = sem("xr")
        d_cl = sem("d_constants_loaded")
        d_ns = sem("d_sink_negated")
        d_wg = sem("d_group_weights_loaded")
        d_vw = sem("d_value_weights_high")
        d_vl = sem("d_value_weights_low")
        d_wh = sem("d_group_weights_high")
        d_wl = sem("d_group_weights_low")
        d_vp = sem("d_value_products")
        d_v = sem("d_values")
        d_kz = sem("d_key_zeros")
        d_x0 = sem("d_residual_started")
        d_qp = sem("d_qk_products")
        d_t = sem("d_rope_terms")
        d_ts = sem("d_rope_sum")
        d_hi = sem("d_qk_high")
        d_lo = sem("d_qk_low")
        d_u = [sem(f"d_queries_stacked{i}") for i in range(2)]
        d_s = sem("d_scores")
        d_m = sem("d_max")
        d_nm = sem("d_minus_max")
        d_e = sem("d_exp")
        d_tp = sem("d_pT_in_psum")
        d_pt = sem("d_pT")
        d_y = sem("d_attended")
        d_zs = sem("d_sink_minus_max")
        d_es = sem("d_sink_exp")
        d_dn = sem("d_denominator")
        d_rc = sem("d_recip")
        d_ys = sem("d_normed")
        d_yt = sem("d_yT_in_psum")
        d_yc = sem("d_yT")
        d_pr = sem("d_projected")
        d_x1 = sem("d_residual")
        e_cl = sem("e_constants_loaded")
        e_sq = sem("e_squares")
        e_lg = sem("e_logits")
        e_r = sem("e_router_vector_steps")
        e_cm = sem("e_router_top")
        e_ex = sem("e_router_exp")
        e_ctp = sem("e_weights_transposed")
        e_ct = sem("e_weights_T")
        e_cs = sem("e_weights_stored")
        e_ce = [sem(f"e_weights_spread{s}") for s in range(QUAD)]
        e_w = [sem(f"e_expert_loaded{s}") for s in range(QUAD)]
        e_wh = sem("e_expert_high")
        e_wl = sem("e_expert_low")
        e_g = sem("e_gate_products")
        e_u = sem("e_up_products")
        e_si = sem("e_silu")
        e_mu = sem("e_hidden")
        e_c = sem("e_weighted")
        e_hh = sem("e_hidden_high")
        e_hl = sem("e_hidden_low")
        e_dn = sem("e_down_products")

        POOL0 = (3, 7)
        VEC0 = tuple(i for i in range(BLK0) if i not in POOL0)

        def over_pairs(eng, pairs, body):
            body(0, True, False)
            with eng.Fori(1, pairs - 1) as p:
                body(p, False, False)
            body(pairs - 1, False, True)

        def rows_of(b):
            return t["x"][b].rearrange("(t p) d -> p t d", p=P)

        block = ctx.enter_context(nc.Block())

        def load_mixture0(sp):
            def weights(e, j, first):
                if not first:
                    sp.wait_ge(b_w1h, e - 1)
                    sp.wait_ge(b_w1l, e - 1)
                sp.dma_start(W1[:, j, :], t["L0_ffn_W1"][bass.ds(e, 1), :, :].squeeze(0)).then_inc(b_w1[j], 16)
                if not first:
                    sp.wait_ge(b_w2h, e - 1)
                    sp.wait_ge(b_w2l, e - 1)
                sp.dma_start(W2[:, j], t["L0_ffn_W2"][bass.ds(e, 1), :, :].squeeze(0).rearrange("(c p) d -> p c d", p=P))\
                  .then_inc(b_w2[j], 16)

            def biases(e, j):
                sp.dma_start(b1[:, j, :], t["L0_ffn_b1_columns"][bass.ds(e, 1), :, :].squeeze(0)).then_inc(b_b1[j], 16)

            for j in range(2):
                weights(j, j, True)
                biases(j, j)
            sp.wait_ge(b_ct, HALVES)
            sp.dma_start(c0_dram, CT8[:]).then_inc(b_cs, 16)
            sp.wait_ge(b_cs, 16)

            def pair(p, first, last):
                for j in range(2):
                    e = p * 2 + j
                    if not first:
                        sp.wait_ge(b_hl, (e - 1) * BLK0)
                    sp.dma_start(CE[:, j, :], c0_dram[bass.ds(e, 1), :].squeeze(0).partition_broadcast(P))\
                      .then_inc(b_ce[j], 16)
                    if not first:
                        biases(e, j)
                    if not last:
                        weights(e + 2, j, False)

            over_pairs(sp, NP0, pair)

        @block.sync
        def _(sp):
            sp.dma_start(ident[:], t["c_ident"]).then_inc(s_id, 16)
            for b in range(NB):
                sp.dma_start(X[:, b * TPB:(b + 1) * TPB, :], rows_of(b)).then_inc(s_x[b], 16)
            sp.dma_start(ctx_rows[:], t["ctx_768"].rearrange("b c d -> c b d")).then_inc(s_w0, 16)
            for dst, name in ((wk0, "L0_xattn_Wk"), (wq0, "L0_xattn_Wq"), (wv0, "L0_xattn_Wv"),
                              (qw1, "L1_xattn_q_w"), (ow1, "L1_xattn_o_w"), (vw1, "L1_xattn_v_w")):
                sp.dma_start(dst[:], t[name]).then_inc(s_w0, 16)
            for r, name in enumerate(("L0_xattn_bq", "L0_xattn_bk", "L1_xattn_q_b", "L1_xattn_v_b",
                                      "L1_ffn_attn_norm_w", "L1_ffn_ffn_norm_w")):
                sp.dma_start(rows[r:r + 1, :], t[name].unsqueeze(0)).then_inc(s_w0, 16)
            for i, name in enumerate(("L0_xattn_bv", "L0_xattn_bv", "L1_xattn_v_b", "L1_xattn_v_b")):
                sp.dma_start(bias_v[:, i, :], t[name].partition_broadcast(LC)).then_inc(s_b0, 16)
            sp.dma_start(gate_in[:, 0:2], t["g_xattn"].partition_broadcast(P)).then_inc(s_b0, 16)
            sp.dma_start(gate_in[:, 2:4], t["g_ffn"].partition_broadcast(P)).then_inc(s_b0, 16)

            for dst, src in ((wg0[:], t["L0_ffn_Wg"]), (bg0[:], t["L0_ffn_bg"].partition_broadcast(P)),
                             (rev0[:], t["c_rev"].partition_broadcast(P)), (b2[:], t["L0_ffn_b2"])):
                sp.dma_start(dst, src).then_inc(s_rl, 16)
            for dst, src in ((head_cols[:], t["c_head_cols"]), (repeat_ctx[:], t["c_repeat_ctx"]),
                             (own_head[:], t["c_own_head"]), (ob[:], t["L1_xattn_o_b"].partition_broadcast(P))):
                sp.dma_start(dst, src).then_inc(s_cc, 16)
            load_mixture0(sp)

            sp.wait_ge(b_dn, E0 * BLK0)
            sp.wait_ge(c_vb, 4 * NB)
            for dst, src in ((cosT, t["c_cos"]), (sinT, t["c_sin"]), (window, t["c_window"]),
                             (w_raw[:, GW:], t["L1_ffn_qkv_w"][:, QD + KD:]),
                             (proj_w, t["L1_ffn_proj_w"].rearrange("(c p) d -> p c d", p=P)),
                             (qkv_bias[:], t["qkv_b_groups"]),
                             (v_bias[:], t["L1_ffn_qkv_b"][QD + KD:].partition_broadcast(P)),
                             (proj_b[:], t["L1_ffn_proj_b"].partition_broadcast(P)),
                             (sink[:], t["L1_ffn_attn_sink"].partition_broadcast(P))):
                sp.dma_start(dst, src).then_inc(d_cl, 16)

            def group_weights(G):
                if G:
                    sp.wait_ge(d_wh, G)
                    sp.wait_ge(d_wl, G)
                sp.dma_start(w_raw[:, 0:GW], t["qkv_w_groups"][G % KV]).then_inc(d_wg, 16)

            def stack_queries(n):
                r = BLOCK_OF["q", n]
                sp.wait_ge(d_hi, r + 1)
                sp.wait_ge(d_lo, r + 1)
                if n >= 4:
                    sp.wait_ge(d_s, TPB * (n - 3))
                h = DH
                for dst, src in ((UQ[n % 4][0:h, 0, :], QH[0:h, n % 4, :]), (UQ[n % 4][h:P, 0, :], QL[0:h, n % 2, :]),
                                 (UQ[n % 4][h:P, 1, :], QH[h:P, n % 4, :]), (UQ[n % 4][0:h, 1, :], QL[h:P, n % 2, :])):
                    sp.dma_start(dst.bitcast(F32), src.bitcast(F32)).then_inc(d_u[n % 2], 16)

            group_weights(0)
            sp.wait_ge(c_n, NT)
            for r in range(3 * NG):
                kind, n = rope_block(r)
                if kind == "q":
                    if n % 2 and n // 2 + 1 < NG:
                        group_weights(n // 2 + 1)
                    stack_queries(n)

            for dst, src in ((gate_w[:], t["L1_ffn_gate_w"]), (gate_b[:], t["L1_ffn_gate_b"].partition_broadcast(P)),
                             (experts[:], t["c_experts"].partition_broadcast(P))):
                sp.dma_start(dst, src).then_inc(e_cl, 16)

            def expert(e, s, first):
                if not first:
                    sp.wait_ge(e_wh, 2 * (e - 3))
                    sp.wait_ge(e_wl, 2 * (e - 3))
                sp.dma_start(ZU[0][:, s, :], t["L1_ffn_W_up"][bass.ds(e, 1), :, :].squeeze(0)).then_inc(e_w[s], 16)
                sp.dma_start(ZD[0][:, s, :], t["L1_ffn_W_down"][bass.ds(e, 1), :, :].squeeze(0)).then_inc(e_w[s], 16)

            sp.wait_ge(d_x1, NB)
            for s in range(QUAD):
                expert(s, s, True)
            sp.wait_ge(e_ct, HALVES)
            sp.dma_start(c1_dram, CT1).then_inc(e_cs, 16)
            sp.wait_ge(e_cs, 16)

            def quad_loads(p, first, last):
                for s in range(QUAD):
                    e = p * QUAD + s
                    if not first:
                        sp.wait_ge(e_c, (e - 3) * HALVES)
                    sp.dma_start(CZ[s], c1_dram[bass.ds(e, 1), :].squeeze(0).partition_broadcast(P))\
                      .then_inc(e_ce[s], 16)
                    if not last:
                        expert(e + QUAD, s, False)

            over_pairs(sp, E1 // QUAD, quad_loads)

            for b in range(NB):
                sp.wait_ge(s_xu, NT * 3 + TPB * (b + 1))
                sp.dma_start(out[b].rearrange("(t p) d -> p t d", p=P),
                             X[:, b * TPB:(b + 1) * TPB, :]).then_inc(s_st1, 16)
            sp.wait_ge(s_st1, 16 * NB)

        SETUP_W = 16 * 13
        SETUP_B = 16 * 6

        @block.gpsimd
        def _(pool):
            pool.memset(minus_half[:], -0.5).then_inc(s_mh, 1)

            def inverse_roots(stage, b, src):
                u = slice(b * TPB, (b + 1) * TPB)
                pool.wait_ge(s_mv, NT * stage + TPB * (b + 1))
                pool.tensor_scalar(ve[:, u], src, EPS, None, ALU.add).then_inc(s_ve, 1)
                pool.wait_ge(s_ve, NB * stage + b + 1)
                pool.tensor_tensor(rstd[:, u], ve[:, u], minus_half[:, u], ALU.pow).then_inc(s_rs, 1)

            pool.wait_ge(s_mh, 1)
            for b in range(NB):
                inverse_roots(0, b, mv[:, b * TPB:(b + 1) * TPB, 1])

            def low1(e, j, first):
                pool.wait_ge(b_w1h, e + 1)
                if not first:
                    pool.wait_ge(b_up, (e - 1) * BLK0)
                pool.tensor_tensor(W1L[:, j, :], W1[:, j, :], W1H[:, j, :].bitcast(F32), ALU.subtract)\
                    .then_inc(b_w1l, 1)

            def low2(e, j, first):
                pool.wait_ge(b_w2h, e + 1)
                if not first:
                    pool.wait_ge(b_dn, (e - 1) * BLK0)
                pool.tensor_tensor(W2L[:, j], W2[:, j], W2H[:, j].bitcast(F32), ALU.subtract).then_inc(b_w2l, 1)

            def values_by_head(b):
                for part in range(2):
                    src = (V1TH[:, b * LC:(b + 1) * LC].bitcast(F32), V1TL[:, b * LC:(b + 1) * LC])[part]
                    pool.tensor_tensor((VTH, VTL)[part][:, b, :].rearrange("p (h k) -> p h k", k=LC),
                                       spread(src, 1, H1), spread(head_cols[:], 2, LC), ALU.mult).then_inc(c_vt, 1)

            low1(0, 0, True)
            low2(0, 0, True)
            pool.wait_ge(s_cc, 64)
            pool.wait_ge(c_vh, 2)
            values_by_head(0)
            for b in range(NB):
                inverse_roots(1, b, mv[:, b * TPB:(b + 1) * TPB, 1])

            def pair(p, first, last):
                for j in range(2):
                    e = p * 2 + j
                    for k, i in enumerate(POOL0):
                        if not (last and j == 1):
                            (low1, low2)[k](e + 1, 1 - j, first and j == 0)
                        n = e * BLK0 + i
                        pool.wait_ge(b_si, n + 1)
                        pool.wait_ge(b_ce[j], 16 * (p + 1))
                        if not (first and j * BLK0 + i < H_RING):
                            pool.wait_ge(b_hl, n + 1 - H_RING)
                        pool.tensor_tensor(HC[:, i % H_RING, :], HA[:, i % H_RING, :],
                                           CE[:, j, (i % HALVES) * 512:(i % HALVES + 1) * 512], ALU.mult)\
                            .then_inc(b_mp, 1)

            over_pairs(pool, NP0, pair)
            values_by_head(1)
            pool.wait_ge(s_g, 1)
            pool.tensor_scalar(ob[:], ob[:], gate[:, 1:2], None, ALU.mult).then_inc(c_ob, 1)
            for b in range(NB):
                inverse_roots(2, b, mv[:, b * TPB:(b + 1) * TPB, 1])
            pool.wait_ge(c_ob, 1)
            for u in range(NT):
                pool.wait_ge(s_xn, 2 * NT + u + 1)
                pool.tensor_tensor(X[:, u, :], X[:, u, :], ob[:], ALU.add).then_inc(c_xb, 1)

            def rms_roots(before, b, mean_square):
                u = slice(b * TPB, (b + 1) * TPB)
                steps = mean_square(u)
                pool.tensor_scalar(rms[:, u], rms[:, u], EPS, None, ALU.add).then_inc(s_rr, 1)
                pool.wait_ge(s_rr, before + steps + 1)
                pool.tensor_tensor(rms[:, u], rms[:, u], minus_half[:, u], ALU.pow).then_inc(s_rr, 1)

            pool.wait_ge(b_dn, E0 * BLK0)
            pool.wait_ge(c_xb, NT)
            pool.memset(KL[0][DH:P].bitcast(F32), 0.0)
            pool.memset(KL[1][0:DH].bitcast(F32), 0.0).then_inc(d_kz, 1)
            pool.wait_ge(d_kz, 1)
            pool.wait_ge(d_cl, 16 * 9)
            pool.wait_ge(d_vw, 1)
            pool.tensor_tensor(WL[:, GW:], w_raw[:, GW:], WH[:, GW:].bitcast(F32), ALU.subtract).then_inc(d_vl, 1)
            pool.tensor_scalar(nsink[:], sink[:], -1.0, None, ALU.mult).then_inc(d_ns, 1)
            for b in range(NB):
                inverse_roots(3, b, mv[:, b * TPB:(b + 1) * TPB, 1])

                def of_normed(u):
                    pool.wait_ge(s_rs, NB * 3 + b + 1)
                    pool.tensor_tensor(rms[:, u], mv[:, u, 1], rstd[:, u], ALU.mult).then_inc(s_rr, 1)
                    pool.wait_ge(s_rr, 4 * b + 1)
                    pool.tensor_tensor(rms[:, u], rms[:, u], rstd[:, u], ALU.mult).then_inc(s_rr, 1)
                    pool.wait_ge(s_rr, 4 * b + 2)
                    return 2

                rms_roots(4 * b, b, of_normed)

            def low_group(G):
                pool.wait_ge(d_wh, G + 1)
                if G:
                    pool.wait_ge(d_qp, 2 * 3 * G)
                pool.tensor_tensor(WL[:, 0:GW], w_raw[:, 0:GW], WH[:, 0:GW].bitcast(F32), ALU.subtract)\
                    .then_inc(d_wl, 1)

            low_group(0)
            for r in range(3 * NG):
                kind, n = rope_block(r)
                pool.wait_ge(d_t, 2 * r + 2)
                if r >= 2:
                    pool.wait_ge(d_hi, r - 1)
                    pool.wait_ge(d_lo, r - 1)
                pool.tensor_tensor(TS[:, r % 2], T1[:, r % 2], T2[:, r % 2], ALU.add).then_inc(d_ts, 1)
                pool.wait_ge(d_hi, r + 1)
                if kind == "q":
                    if n >= 2:
                        pool.wait_ge(d_u[n % 2], 64 * (n // 2))
                    pool.tensor_tensor(QL[:, n % 2], TS[:, r % 2], QH[:, n % 4].bitcast(F32), ALU.subtract)\
                        .then_inc(d_lo, 1)
                else:
                    if n >= 2:
                        pool.wait_ge(d_s, 8 * (n - 1))
                    for q in range(2):
                        rows_ = slice(q * DH, (q + 1) * DH)
                        ins = pool.tensor_tensor(KL[q][rows_, n % 2], TS[rows_, r % 2],
                                                 KHH[rows_, n % 2].bitcast(F32), ALU.subtract)
                    ins.then_inc(d_lo, 1)
                    pool.wait_ge(d_lo, r + 1)
                if kind == "q" and n % 2 and n // 2 + 1 < NG:
                    low_group(n // 2 + 1)
                if r == 2:
                    for b in range(NB):
                        pool.wait_ge(s_xn, NT * 3 + TPB * (b + 1))
                        u = slice(b * TPB, (b + 1) * TPB)
                        pool.tensor_tensor(X1[:, u, :], XN[:, u, :], spread(proj_b[:], 1, TPB), ALU.add)\
                            .then_inc(d_x0, 1)

            for b in range(NB):
                def of_squares(u):
                    pool.wait_ge(e_sq, TPB * (b + 1))
                    pool.tensor_scalar(rms[:, u], rms[:, u], 1.0 / D, None, ALU.mult).then_inc(s_rr, 1)
                    pool.wait_ge(s_rr, 4 * NB + 3 * b + 1)
                    return 1

                rms_roots(4 * NB + 3 * b, b, of_squares)

            def quad(p, first, last):
                for k in range(QUAD * HALVES):
                    n, s, h = p * QUAD * HALVES + k, k // HALVES, k % HALVES
                    pool.wait_ge(e_mu, n + 1)
                    if h == 0:
                        pool.wait_ge(e_ce[s], 16 * (p + 1))
                    if not (first and k < H_RING):
                        pool.wait_ge(e_hl, n + 1 - H_RING)
                    pool.tensor_tensor(HC[:, k % H_RING, :], HA[:, k % H_RING, :], CZ[s][:, h * 512:(h + 1) * 512],
                                       ALU.mult).then_inc(e_c, 1)

            over_pairs(pool, E1 // QUAD, quad)

        @block.tensor
        def _(pe):
            pe.wait_ge(s_id, 16)
            pe.wait_ge(s_w0, SETUP_W)
            for b in range(NB):
                pe.transpose(bank[2][0:DC, b * LC:(b + 1) * LC], ctx_rows[:, b, :], ident[0:LC, 0:LC])
            pe.transpose(bank[2][:, 256:256 + NROWS], rows[:], ident[0:NROWS, 0:NROWS]).then_inc(s_p1, 1)
            for i, w in enumerate((wq0, qw1, ow1)):
                pe.transpose(bank[3][:, i * D:(i + 1) * D], w[:], ident[:])
            pe.transpose(bank[3][0:DC, 3 * D:4 * D], vw1[:], ident[:]).then_inc(s_p1, 1)
            pe.wait_ge(s_e1, 3)
            pe.wait_ge(s_vw, 1)
            pe.matmul(bank[4][:, 0:NB * LC], wk0[:], ctxT[:], start=True, stop=True).then_inc(s_p2, 1)
            pe.matmul(bank[5][:, 0:NB * LC], WT[0:DC, 3, :], ctxT[:], start=True, stop=True).then_inc(s_p2, 1)
            for b in range(NB):
                cb = ctxT[:, b * LC:(b + 1) * LC]
                pe.matmul(bank[6][0:LC, b * D:(b + 1) * D], cb, wv0[:], start=True, stop=True)
            for b in range(NB):
                cb = ctxT[:, b * LC:(b + 1) * LC]
                mm = pe.matmul(bank[6][0:LC, (2 + b) * D:(3 + b) * D], cb, WT[0:DC, 3, :], start=True, stop=True)
            mm.then_inc(s_p2, 1)
            pe.wait_ge(s_kt, 1)
            pe.matmul(bank[7][:, 0:NB * LC], WT[:, 0, :], KT0[:], start=True, stop=True).then_inc(s_p3, 1)

            def transpose_tokens(ready, before, src, dst):
                for b in range(NB):
                    for i in range(TPB):
                        u = b * TPB + i
                        pe.wait_ge(ready, NT * before + u + 1)
                        mm = pe.transpose(dst[b][:, i * P:(i + 1) * P], src[:, u, :], ident[:])
                    mm.then_inc(s_xtp, 1)

            transpose_tokens(s_xn, 0, XN, bank)
            pe.wait_ge(s_bq, 1)
            pe.wait_ge(s_e3, 1)
            pe.wait_ge(s_e2, 2)
            for b in range(NB):
                pe.wait_ge(s_xt, b + 1)
                cb = slice(b * LC, (b + 1) * LC)
                for i in range(TPB):
                    o = bank[2 + b][:, i * LC:(i + 1) * LC]
                    u = b * TPB + i
                    pe.matmul(o, BQW[:], KT0[:, cb], start=True, stop=False)
                    mm = pe.matmul(o, XT[:, u * P:(u + 1) * P], KA[:, cb], start=False, stop=True)
                mm.then_inc(sa_s, 1)
            for b in range(NB):
                pe.wait_ge(sa_e, b + 1)
                for i in range(TPB):
                    mm = pe.transpose(bank[4 + b][0:LC, i * P:(i + 1) * P], SA[:, b * TPB + i, :], ident[:])
                mm.then_inc(sa_t, 1)
            for b in range(NB):
                pe.wait_ge(sa_p, b + 1)
                for i in range(TPB):
                    mm = pe.matmul(bank[6 + b][:, i * D:(i + 1) * D], PTA[:, b * TPB + i, :],
                                   VV[:, 0, b, :], start=True, stop=True)
                mm.then_inc(sa_o, 1)

            pe.wait_ge(s_xt, NB)
            transpose_tokens(s_xn, 1, XN, bank)
            pe.wait_ge(s_rl, 64)
            for b in range(NB):
                pe.wait_ge(s_xt, NB + b + 1)
                for i in range(TPB):
                    u = b * TPB + i
                    mm = pe.matmul(bank[6][:, u * E0:(u + 1) * E0], XT[:, u * P:(u + 1) * P], wg0[:],
                                   start=True, stop=True)
            mm.then_inc(b_lg, 1)
            pe.wait_ge(s_xtl, NB)

            def up(e, j, i, first):
                n = e * BLK0 + i
                if i == 0:
                    pe.wait_ge(b_w1l, e + 1)
                if not first:
                    pe.wait_ge(b_si, n + 1 - UP_RING)
                c, h = i // HALVES, i % HALVES
                o = bank[2 + i % UP_RING][:, :]
                wc, tk = slice(c * P, (c + 1) * P), slice(h * 512, (h + 1) * 512)
                pe.matmul(o, W1H[:, j, wc], XTH[:, tk], start=True, stop=False)
                pe.matmul(o, W1H[:, j, wc], XTL[:, tk], start=False, stop=False)
                pe.matmul(o, W1L[:, j, wc], XTH[:, tk], start=False, stop=True).then_inc(b_up, 1)

            def down(e, j, i):
                n = e * BLK0 + i
                if i == 0:
                    pe.wait_ge(b_w2l, e + 1)
                pe.wait_ge(b_hl, n + 1)
                c, h = i // HALVES, i % HALVES
                o, r = bank[6 + h][:, :], i % H_RING
                pe.matmul(o, W2H[:, j, c], HH[:, r, :], start=False, stop=False, skip_group_check=True)
                pe.matmul(o, W2H[:, j, c], HL[:, r, :], start=False, stop=False, skip_group_check=True)
                pe.matmul(o, W2L[:, j, c], HH[:, r, :], start=False, stop=True, skip_group_check=True)\
                    .then_inc(b_dn, 1)

            for i in range(LEAD0):
                up(0, 0, i, i < UP_RING)
            pe.wait_ge(b_cm, 1)
            for b in range(NB):
                for i in range(TPB):
                    mm = pe.transpose(bank[b][0:E0, i * P:(i + 1) * P], CM[:, b * TPB + i, :], ident[:])
                mm.then_inc(b_ctp, 1)
            for h in range(HALVES):
                pe.wait_ge(b_ct, h + 1)
                pe.matmul(bank[6 + h][:, :], b2[:], CT8[:, h * 512:(h + 1) * 512], start=True, stop=False,
                          skip_group_check=True)

            pe.wait_ge(s_cc, 64)
            for q in range(NB * 3):
                b, g = q // 3, q % 3
                if q >= 2:
                    pe.wait_ge(c_vb, q - 1)
                for j in range(4 * g, min(4 * g + 4, NCH)):
                    mm = pe.matmul(bank[q % 2][:, (j - 4 * g) * D:(j - 4 * g + 1) * D],
                                   repeat_ctx[:, j * P:(j + 1) * P], VV[:, 1, b, :], start=True, stop=True)
                mm.then_inc(c_vp, 1)

            def pair0(p, first, last):
                for k in range(2 * BLK0):
                    j, i = k // BLK0, k % BLK0
                    m = k + LEAD0
                    if not (last and m >= 2 * BLK0):
                        up(p * 2 + m // BLK0, m // BLK0 % 2, m % BLK0, False)
                    down(p * 2 + j, j, i)

            over_pairs(pe, NP0, pair0)

            def transpose_back(done, count):
                for b in range(NB):
                    pe.wait_ge(done, count + b + 1)
                    for i in range(TPB):
                        u = b * TPB + i
                        mm = pe.transpose(bank[b][:, i * P:(i + 1) * P], YT[:, u * P:(u + 1) * P], ident[:])
                    mm.then_inc(b_yp, 1)

            transpose_back(b_yt, 0)

            pe.wait_ge(s_xu, 2 * NT)
            transpose_tokens(s_xn, 2, XN, bank)
            for b in range(NB):
                pe.wait_ge(s_xt, 2 * NB + b + 1)
                pe.matmul(bank[5 + b][:, :], WT[:, 1, :], XT[:, b * 512:(b + 1) * 512], start=True, stop=True)\
                    .then_inc(c_q, 1)

            def scores(u):
                b = u // TPB
                pe.wait_ge(c_ql, b + 1)
                pe.wait_ge(c_vt, 2 * (b + 1))
                tk = slice(u * P, (u + 1) * P)
                for g, (h0, n) in enumerate(GROUPS):
                    if u:
                        pe.wait_ge(c_c, 3 * (u - 1) + g + 1)
                    o, hk = bank[2 + g][:, 0:n * LC], slice(h0 * LC, (h0 + n) * LC)
                    pe.matmul(o, XTH[:, tk], VTH[:, b, hk], start=True, stop=False)
                    pe.matmul(o, XTH[:, tk], VTL[:, b, hk], start=False, stop=False)
                    pe.matmul(o, XTL[:, tk], VTH[:, b, hk], start=False, stop=True).then_inc(c_s, 1)

            def chunk_rows(j):
                return min(P, HK - j * P)

            def probs_transposed(u):
                pe.wait_ge(c_e, u + 1)
                for g in range(3):
                    if u:
                        pe.wait_ge(c_p, 3 * (u - 1) + g + 1)
                    for j in range(4 * g, min(4 * g + 4, NCH)):
                        mm = pe.transpose(bank[5 + g][0:chunk_rows(j), (j - 4 * g) * P:(j - 4 * g + 1) * P],
                                          SC[:, u % 2, j * P:j * P + chunk_rows(j)], ident[:])
                    mm.then_inc(c_tp, 1)

            def attend(u):
                pe.wait_ge(c_p, 3 * (u + 1))
                if u:
                    pe.wait_ge(c_n, u)
                for j in range(NCH):
                    mm = pe.matmul(bank[0][:, 0:DEN], PTC[0:chunk_rows(j), j, :],
                                   VBD[0:chunk_rows(j), u // TPB, j, :], start=(j == 0), stop=(j == NCH - 1))
                mm.then_inc(c_o, 1)

            def rows_transposed(b):
                pe.wait_ge(c_n, TPB * (b + 1))
                if b:
                    pe.wait_ge(s_xu, 2 * NT + TPB * b)
                for h in range(H1):
                    mm = pe.transpose(bank[1][:, h * AA:(h + 1) * AA], OA[:, b, h].rearrange("a s d -> a (s d)"),
                                      ident[0:AA, 0:AA])
                mm.then_inc(c_otp, 1)

            def project(b):
                pe.wait_ge(c_ot, b + 1)
                for i in range(TPB):
                    mm = pe.matmul(bank[1][:, i * P:(i + 1) * P], OT[:, b, i * P:(i + 1) * P], WT[:, 2, :],
                                   start=True, stop=True)
                mm.then_inc(c_y, 1)

            scores(0)
            for u in range(NT):
                if u + 1 < NT:
                    scores(u + 1)
                if u and u % TPB == 0:
                    rows_transposed(u // TPB - 1)
                probs_transposed(u)
                if u and u % TPB == 0:
                    project(u // TPB - 1)
                attend(u)
            rows_transposed(NB - 1)
            project(NB - 1)

            pe.wait_ge(s_xu, 3 * NT)
            transpose_tokens(s_xr, 0, XR, bank)
            pe.wait_ge(s_xtl, 2 * NB)
            pe.wait_ge(d_vl, 1)
            for u in range(NT):
                o, tk = bank[2 + u // 2][:, u % 2 * KD:(u % 2 + 1) * KD], slice(u * P, (u + 1) * P)
                pe.matmul(o, XTH[:, tk], WH[:, GW:], start=True, stop=False)
                pe.matmul(o, XTL[:, tk], WH[:, GW:], start=False, stop=False)
                mm = pe.matmul(o, XTH[:, tk], WL[:, GW:], start=False, stop=True)
                if u % 2:
                    mm.then_inc(d_vp, 1)

            def rope_products(r, outT):
                kind, n = rope_block(r)
                G = n if kind == "k" else n // 2
                b = G // KV
                tk = slice(b * 512, (b + 1) * 512)
                pe.wait_ge(d_wl, G + 1)
                if r:
                    pe.wait_ge(d_t, 2 * r)
                if outT:
                    pe.wait_ge(d_yc, outT)
                for swap in range(2):
                    w0 = (4 + swap) * P if kind == "k" else (2 * swap + n % 2) * P
                    wc = slice(w0, w0 + P)
                    pe.matmul(bank[swap][:, :], WH[:, wc], XTH[:, tk], start=True, stop=False)
                    pe.matmul(bank[swap][:, :], WH[:, wc], XTL[:, tk], start=False, stop=False)
                    pe.matmul(bank[swap][:, :], WL[:, wc], XTH[:, tk], start=False, stop=True).then_inc(d_qp, 1)

            def scores_d(q):
                n, i = q // TPB, q % TPB
                G = n // 2
                if i == 0:
                    pe.wait_ge(d_u[n % 2], 64 * (n // 2 + 1))
                    pe.wait_ge(d_lo, BLOCK_OF["k", G] + 1)
                    if q == 0:
                        pe.wait_ge(d_kz, 1)
                if q < 2:
                    pe.wait_ge(d_v, q + 1)
                else:
                    pe.wait_ge(d_m, q - 1)
                k0 = max(i - 1, 0)
                keys, tk = slice(k0 * P, (i + 1) * P), slice(i * P, (i + 1) * P)
                for hd in range(2):
                    o = bank[2 + q % 2][:, hd * 256 + (128 if i == 0 else 0):(hd + 1) * 256]
                    pe.matmul(o, UQ[n % 4][:, hd, tk], KHH[:, G % 2, keys], start=True, stop=False)
                    mm = pe.matmul(o, QH[:, n % 4, tk], KL[hd][:, G % 2, keys], start=False, stop=True)
                mm.then_inc(d_s, 1)

            def probs_transposed_d(q):
                pe.wait_ge(d_e, q + 1)
                if q < 2:
                    pe.wait_ge(d_v, 3 + q)
                else:
                    pe.wait_ge(d_pt, q - 1)
                for hd in range(2):
                    for kb in range(2):
                        if q % TPB or kb:
                            at = slice((2 * hd + kb) * P, (2 * hd + kb + 1) * P)
                            mm = pe.transpose(bank[4 + q % 2][:, at], SM[:, q % 4, at], ident[:])
                mm.then_inc(d_tp, 1)

            def attend_d(q):
                n, i = q // TPB, q % TPB
                b, g = n // PAIRS, n % PAIRS // 2
                pe.wait_ge(d_pt, q + 1)
                if i == 0 and n:
                    pe.wait_ge(d_ys, n)
                for hd in range(2):
                    o = bank[6][:, i * P + hd * DH:i * P + (hd + 1) * DH]
                    for kb in range(2):
                        if i or kb:
                            mm = pe.matmul(o, PT[:, q % 2, (2 * hd + kb) * P:(2 * hd + kb + 1) * P],
                                           VS[:, b * TPB + i - 1 + kb, g * DH:(g + 1) * DH],
                                           start=(kb == 0 or i == 0), stop=(kb == 1))
                mm.then_inc(d_y, 1)

            def out_transposed(m, ropes):
                pe.wait_ge(d_ys, m + 1)
                pe.wait_ge(d_t, 2 * ropes)
                if m:
                    pe.wait_ge(d_yc, m)
                for i in range(TPB):
                    mm = pe.transpose(bank[0][:, i * P:(i + 1) * P], YS[:, m % 2, i * P:(i + 1) * P], ident[:])
                mm.then_inc(d_yt, 1)

            def project_d(m):
                b, c = m // PAIRS, m % PAIRS
                pe.wait_ge(d_yc, m + 1)
                if b and c == 0:
                    pe.wait_ge(d_x1, b)
                for i in range(TPB):
                    mm = pe.matmul(bank[7][:, i * P:(i + 1) * P], YTC[:, m % 2, i * P:(i + 1) * P], proj_w[:, c, :],
                                   start=(c == 0 and i == 0), stop=(c == PAIRS - 1), skip_group_check=True)
                mm.then_inc(d_pr, 1)

            for r in range(3):
                rope_products(r, 0)
            ropes = 3
            for q in range(NQ + TPB + 3):
                if q < NQ:
                    scores_d(q)
                if 2 <= q < NQ + 2:
                    probs_transposed_d(q - 2)
                if q in ROPE_AT:
                    rope_products(ropes, max(0, (q - 4) // 4))
                    ropes += 1
                if 3 <= q < NQ + 3:
                    attend_d(q - 3)
                m, k = (q - 4) // 4 - 1, (q - 4) % 4
                if 0 <= m < NU and k == 0:
                    out_transposed(m, ropes)
                if 0 <= m < NU and k == 2:
                    project_d(m)

            transpose_tokens(s_xr, 1, XR, bank)
            pe.wait_ge(e_cl, 48)
            for b in range(NB):
                pe.wait_ge(s_xt, 4 * NB + b + 1)
                for i in range(TPB):
                    u = b * TPB + i
                    mm = pe.matmul(bank[5][:, u * E1:(u + 1) * E1], XT[:, u * P:(u + 1) * P], gate_w[:],
                                   start=True, stop=True)
            mm.then_inc(e_lg, 1)
            for u in range(NT):
                pe.matmul(bank[6 + u // TPB][:, u % TPB * P:(u % TPB + 1) * P], X1[:, u, :], ident[:],
                          start=(u % TPB == 0), stop=False, skip_group_check=True)
            pe.wait_ge(s_xtl, 3 * NB)

            def three_passes(o, wh, wl, xh, xl, start):
                pe.matmul(o, wh, xh, start=start, stop=False, skip_group_check=not start)
                pe.matmul(o, wh, xl, start=False, stop=False, skip_group_check=not start)
                return pe.matmul(o, wl, xh, start=False, stop=True, skip_group_check=not start)

            def gate_block(n, k, first):
                s, tk = k // HALVES % QUAD, slice(k % HALVES * 512, (k % HALVES + 1) * 512)
                if k % HALVES == 0:
                    pe.wait_ge(e_wl, n + 2)
                if not first:
                    pe.wait_ge(e_si, n - 3)
                three_passes(bank[k % 4][:, :], ZU[1][:, s, P:2 * P], ZU[2][:, s, P:2 * P], XTH[:, tk], XTL[:, tk],
                             True).then_inc(e_g, 1)

            def up_block(n, k, first):
                s, tk = k // HALVES % QUAD, slice(k % HALVES * 512, (k % HALVES + 1) * 512)
                if not first:
                    pe.wait_ge(e_mu, n - 1)
                three_passes(bank[4 + k % 2][:, :], ZU[1][:, s, 0:P], ZU[2][:, s, 0:P], XTH[:, tk], XTL[:, tk],
                             True).then_inc(e_u, 1)

            def down_block(n, k):
                s, r = k // HALVES, k % H_RING
                pe.wait_ge(e_hl, n + 1)
                three_passes(bank[6 + k % HALVES][:, :], ZD[1][:, s, :], ZD[2][:, s, :], HH[:, r, :], HL[:, r, :],
                             False).then_inc(e_dn, 1)

            gate_block(0, 0, True)
            pe.wait_ge(e_r, 10)
            up_block(0, 0, True)
            gate_block(1, 1, True)
            up_block(1, 1, True)
            for b in range(NB):
                for i in range(TPB):
                    mm = pe.transpose(bank[2 + b][0:E1, i * P:(i + 1) * P], GZ[:, b * TPB + i, :], ident[:])
                mm.then_inc(e_ctp, 1)
            pe.wait_ge(e_ct, NB)
            gate_block(2, 2, True)

            def quad(p, first, last):
                for k in range(QUAD * HALVES):
                    n = p * QUAD * HALVES + k
                    if not (last and k + 2 >= QUAD * HALVES):
                        up_block(n + 2, k + 2, False)
                    if not (last and k + 3 >= QUAD * HALVES):
                        gate_block(n + 3, k + 3, first and k + 3 < 4)
                    down_block(n, k)

            over_pairs(pe, E1 // QUAD, quad)
            transpose_back(b_yt, NB)

        @block.scalar
        def _(act):
            act.wait_ge(s_p1, 1)
            act.copy(ctxT[:], bank[2][0:DC, 0:NB * LC]).then_inc(s_e1, 1)
            act.copy(cols[:], bank[2][:, 256:256 + NROWS]).then_inc(s_e1, 1)
            act.wait_ge(s_p1, 2)
            act.copy(WT[:, 0:3, :], bank[3][:, 0:3 * D]).then_inc(s_e1, 1)
            act.wait_ge(s_p2, 1)
            act.wait_ge(s_e1, 3)
            act.activation(KT0[:], bank[4][:, 0:NB * LC], ACT.Identity, bias=cols[:, BK:BK + 1]).then_inc(s_kt, 1)
            act.wait_ge(s_p3, 1)
            act.copy(KA[:], bank[7][:, 0:NB * LC]).then_inc(s_e3, 1)
            for b in range(NB):
                act.wait_ge(s_xtp, b + 1)
                act.copy(XT[:, b * 512:(b + 1) * 512], bank[b][:, :]).then_inc(s_xt, 1)
            act.wait_ge(s_b0, SETUP_B)
            act.activation(gate[:], gate_in[:], ACT.Tanh).then_inc(s_g, 1)
            for b in range(NB):
                act.wait_ge(sa_c, b + 1)
                sc = SA[:, b * TPB:(b + 1) * TPB, :]
                act.activation(sc, sc, ACT.Exp, scale=float(D) ** -0.5).then_inc(sa_e, 1)
            for b in range(NB):
                act.wait_ge(sa_t, b + 1)
                act.copy(PTA[:, b * TPB:(b + 1) * TPB, :], bank[4 + b][0:LC, :]).then_inc(sa_p, 1)


            def split_tokens(kth, hi_kth, scale):
                for b in range(NB):
                    act.wait_ge(s_xtp, NB * kth + b + 1)
                    tk = slice(b * 512, (b + 1) * 512)
                    act.activation(XTH[:, tk], bank[b][:, :], ACT.Copy, scale=scale).then_inc(s_xth, 1)
                    act.activation(XT[:, tk], bank[b][:, :], ACT.Copy, scale=scale).then_inc(s_xt, 1)

            def high1(e, j, first, p):
                act.wait_ge(b_w1[j], 16 * (p + 1))
                if not first:
                    act.wait_ge(b_up, (e - 1) * BLK0)
                act.copy(W1H[:, j, :], W1[:, j, :]).then_inc(b_w1h, 1)

            def high2(e, j, first, p):
                act.wait_ge(b_w2[j], 16 * (p + 1))
                if not first:
                    act.wait_ge(b_dn, (e - 1) * BLK0)
                act.copy(W2H[:, j], W2[:, j]).then_inc(b_w2h, 1)

            high1(0, 0, True, 0)
            high2(0, 0, True, 0)
            split_tokens(1, 0, 1.0)
            act.wait_ge(b_d, 3)
            act.activation(GL[:], GL[:], ACT.Exp).then_inc(b_ex, 1)

            HI_LAG = 2

            def high(e, i, k, first):
                n = e * BLK0 + i
                if i in POOL0:
                    act.wait_ge(b_mp, e * len(POOL0) + POOL0.index(i) + 1)
                else:
                    act.wait_ge(b_mv, e * len(VEC0) + VEC0.index(i) + 1)
                if not first:
                    act.wait_ge(b_dn, n + 1 - H_RING)
                act.copy(HH[:, i % H_RING, :], HC[:, i % H_RING, :]).then_inc(b_hh, 1)

            def pair0(p, first, last):
                for k in range(2 * BLK0):
                    j, i = k // BLK0, k % BLK0
                    e = p * 2 + j
                    n = e * BLK0 + i
                    act.wait_ge(b_up, n + 1)
                    if not (first and k < H_RING):
                        act.wait_ge(b_hl, n + 1 - H_RING)
                    if i == 0:
                        act.wait_ge(b_b1[j], 16 * (p + 1))
                    act.activation(HA[:, i % H_RING, :], bank[2 + i % UP_RING][:, :], ACT.Silu,
                                   bias=b1[:, j, i // HALVES:i // HALVES + 1]).then_inc(b_si, 1)
                    if not (last and j == 1):
                        if i == 0:
                            high1(e + 1, 1 - j, first and j == 0, p + j)
                        if i == BLK0 - 2:
                            high2(e + 1, 1 - j, first and j == 0, p + j)
                    if k >= HI_LAG or not first:
                        m = k - HI_LAG
                        high(p * 2 + m // BLK0, m % BLK0, m, first and m < H_RING)
                if last:
                    for m in range(2 * BLK0 - HI_LAG, 2 * BLK0):
                        high(p * 2 + m // BLK0, m % BLK0, m, False)

            over_pairs(act, NP0, pair0)
            for h in range(HALVES):
                act.wait_ge(b_dn, E0 * BLK0 - HALVES + h + 1)
                act.copy(YT[:, h * 512:(h + 1) * 512], bank[6 + h][:, :]).then_inc(b_yt, 1)

            for b in range(NB):
                act.wait_ge(s_xtp, 2 * NB + b + 1)
                act.copy(XT[:, b * 512:(b + 1) * 512], bank[b][:, :]).then_inc(s_xt, 1)
            for b in range(NB):
                tk = slice(b * 512, (b + 1) * 512)
                act.wait_ge(c_q, b + 1)
                by_s = bank[5 + b][:, :].rearrange("p (a s) -> p s a", s=STR)
                for dst, done in ((XTH, c_qh), (YT, c_qt)):
                    act.activation(dst[:, tk].rearrange("p (s a) -> p s a", s=STR), by_s, ACT.Identity,
                                   bias=cols[:, QB:QB + 1]).then_inc(done, 1)

            def exp_c(u):
                act.wait_ge(c_c, 3 * (u + 1))
                act.activation(SC[:, u % 2, :], SC[:, u % 2, :], ACT.Exp, scale=float(DH1) ** -0.5).then_inc(c_e, 1)

            def out_c(b):
                act.wait_ge(c_otp, b + 1)
                act.copy(OT[:, b, :], bank[1][:, :]).then_inc(c_ot, 1)

            exp_c(0)
            for u in range(NT):
                if u and u % TPB == 0:
                    out_c(u // TPB - 1)
                for g in range(3):
                    act.wait_ge(c_tp, 3 * u + g + 1)
                    if u and g == 0:
                        act.wait_ge(c_o, u)
                    nj = min(4, NCH - 4 * g)
                    full = nj if g < 2 else nj - 1
                    act.copy(PTC[:, 4 * g:4 * g + nj, :], bank[5 + g][:, 0:nj * P]).then_inc(c_p, 1)
                if u + 1 < NT:
                    exp_c(u + 1)
            out_c(NB - 1)

            act.wait_ge(d_cl, 16 * 9)
            act.copy(WH[:, GW:], w_raw[:, GW:]).then_inc(d_vw, 1)

            def high_group(G):
                act.wait_ge(d_wg, 16 * (G + 1))
                if G:
                    act.wait_ge(d_qp, 2 * 3 * G)
                act.copy(WH[:, 0:GW], w_raw[:, 0:GW]).then_inc(d_wh, 1)

            high_group(0)
            split_tokens(3, 1, cols[:, ATTN_W:ATTN_W + 1])

            def high_qk(r):
                kind, n = rope_block(r)
                act.wait_ge(d_ts, r + 1)
                if kind == "q":
                    if n >= 4:
                        act.wait_ge(d_s, TPB * (n - 3))
                        act.wait_ge(d_u[n % 2], 64 * ((n - 4) // 2 + 1))
                    act.copy(QH[:, n % 4], TS[:, r % 2]).then_inc(d_hi, 1)
                else:
                    if n >= 2:
                        act.wait_ge(d_s, 8 * (n - 1))
                    act.copy(KHH[:, n % 2], TS[:, r % 2]).then_inc(d_hi, 1)
                if kind == "q" and n % 2 and n // 2 + 1 < NG:
                    high_group(n // 2 + 1)

            for r in range(3):
                high_qk(r)
            highs = 3
            for q in range(NQ + TPB + 4):
                if 2 <= q < NQ + 2:
                    act.wait_ge(d_tp, q - 1)
                    if q >= 4:
                        act.wait_ge(d_y, q - 3)
                    h = slice(0, 2) if (q - 2) % TPB else slice(1, 2)
                    act.copy(PT[:, q % 2].rearrange("p (h k j) -> p h k j", h=2, k=2)[:, :, h, :],
                             bank[4 + q % 2][:, :].rearrange("p (h k j) -> p h k j", h=2, k=2)[:, :, h, :])\
                       .then_inc(d_pt, 1)
                if q < NQ:
                    n, i = q // TPB, q % TPB
                    act.wait_ge(d_nm, q + 1)
                    if n >= 2 and i == 0:
                        act.wait_ge(d_dn, n - 1)
                    for hd in range(2):
                        pr = SM[:, q % 4, hd * 256 + (128 if i == 0 else 0):(hd + 1) * 256]
                        ins = act.activation(pr, pr, ACT.Exp, bias=nm[:, n % 2, i, hd:hd + 1], scale=DH ** -0.5,
                                             accum_out=lD[:, n % 2, i, hd:hd + 1])
                    ins.then_inc(d_e, 1)
                m, k = q // 4 - 1, q % 4
                if k == 0 and 0 <= m < NU:
                    act.wait_ge(d_zs, m + 1)
                    act.activation(den[:, m % 2], zs[:, m % 2], ACT.Exp).then_inc(d_es, 1)
                m, k = (q - 5) // 4 - 1, (q - 5) % 4
                if k == 0 and 0 <= m < NU:
                    act.wait_ge(d_yt, m + 1)
                    if m >= 2:
                        act.wait_ge(d_pr, m - 1)
                    act.copy(YTC[:, m % 2], bank[0][:, :]).then_inc(d_yc, 1)
                if q - 1 in ROPE_AT:
                    high_qk(highs)
                    highs += 1

            for b in range(NB):
                act.wait_ge(d_x1, b + 1)
                for i in range(TPB):
                    u = b * TPB + i
                    act.activation(XR[:, u, :], X1[:, u, :], ACT.Square, accum_out=rms[:, u:u + 1]).then_inc(e_sq, 1)

            def high_expert(e, s, p):
                act.wait_ge(e_w[s], 32 * (p + 1))
                act.copy(ZU[1][:, s, :], ZU[0][:, s, :]).then_inc(e_wh, 1)
                act.copy(ZD[1][:, s, :], ZD[0][:, s, :]).then_inc(e_wh, 1)

            for s in range(2):
                high_expert(s, s, 0)
            split_tokens(4, 2, cols[:, FFN_W:FFN_W + 1])
            act.wait_ge(e_r, 2)
            act.activation(wt[:], wt[:], ACT.Exp).then_inc(e_ex, 1)

            def high_e(n, k, first):
                act.wait_ge(e_c, n + 1)
                if not first:
                    act.wait_ge(e_dn, n + 1 - H_RING)
                act.copy(HH[:, k % H_RING, :], HC[:, k % H_RING, :]).then_inc(e_hh, 1)

            HI1 = 3

            def quad(p, first, last):
                for k in range(QUAD * HALVES):
                    n, s, h = p * QUAD * HALVES + k, k // HALVES, k % HALVES
                    if not first or k >= HI1:
                        high_e(n - HI1, (k - HI1) % H_RING, first and k - HI1 < H_RING)
                    act.wait_ge(e_g, n + 1)
                    if not (first and k < H_RING):
                        act.wait_ge(e_c, n + 1 - H_RING)
                    act.activation(HA[:, k % H_RING, :], bank[k % 4][:, :], ACT.Silu).then_inc(e_si, 1)
                    if h == 0 and not (last and s >= 2):
                        if not (first and s < 2):
                            act.wait_ge(e_dn, n + (3 - QUAD) * HALVES)
                        high_expert(p * QUAD + s + 2, (s + 2) % QUAD, p + (s + 2) // QUAD)
                if last:
                    for k in range(QUAD * HALVES - HI1, QUAD * HALVES):
                        high_e(p * QUAD * HALVES + k, k, False)

            over_pairs(act, E1 // QUAD, quad)
            for h in range(HALVES):
                act.wait_ge(e_dn, NB1 - HALVES + h + 1)
                act.copy(YT[:, h * 512:(h + 1) * 512], bank[6 + h][:, :]).then_inc(b_yt, 1)

        @block.vector
        def _(dve):
            def row_means(stage, b):
                for i in range(TPB):
                    u = b * TPB + i
                    if stage:
                        dve.wait_ge(s_xu, NT * (stage - 1) + u + 1)
                    dve.bn_stats(stats[:, u, :], X[:, u, :]).then_inc(s_st, 1)
                for i in range(TPB):
                    u = b * TPB + i
                    dve.wait_ge(s_st, NT * stage + u + 1)
                    dve.bn_aggr(mv[:, u, :], stats[:, u, :]).then_inc(s_mv, 1)

            def normalise(stage, b):
                dve.wait_ge(s_rs, NB * stage + b + 1)
                for i in range(TPB):
                    u = b * TPB + i
                    dve.tensor_scalar(XN[:, u, :], X[:, u, :], mv[:, u, 0:1], rstd[:, u:u + 1],
                                      ALU.subtract, ALU.mult).then_inc(s_xn, 1)

            for b in range(NB):
                dve.wait_ge(s_x[b], 16)
                row_means(0, b)
            for b in range(NB):
                normalise(0, b)
            dve.wait_ge(s_e1, 3)
            dve.tensor_copy(WT[0:DC, 3, :], bank[3][0:DC, 3 * D:4 * D]).then_inc(s_vw, 1)
            dve.tensor_copy(BQW[:], cols[:, BQ:BQ + 1].broadcast_to([P, P])).then_inc(s_bq, 1)
            dve.wait_ge(s_p2, 2)
            dve.tensor_scalar(V1T[:], bank[5][:, 0:NB * LC], cols[:, VB:VB + 1], None, ALU.add).then_inc(s_e2, 1)
            dve.wait_ge(s_p2, 3)
            dve.wait_ge(s_b0, SETUP_B)
            dve.tensor_tensor(VV[:].rearrange("k l b d -> k (l b d)"), bank[6][0:LC, :],
                              bias_v[:].rearrange("k l d -> k (l d)"), ALU.add).then_inc(s_e2, 1)

            dve.wait_ge(s_e2, 1)
            dve.tensor_copy(V1TH[:], V1T[:]).then_inc(c_vh, 1)
            dve.wait_ge(c_vh, 1)
            dve.tensor_tensor(V1TL[:], V1T[:], V1TH[:].bitcast(F32), ALU.subtract).then_inc(c_vh, 1)

            for b in range(NB):
                u = slice(b * TPB, (b + 1) * TPB)
                sc = bank[2 + b][:, 0:TPB * LC].rearrange("p (i k) -> p i k", k=LC)
                dve.wait_ge(sa_s, b + 1)
                dve.tensor_reduce(mA[:, u], sc, AX.X, ALU.max).then_inc(sa_m, 1)
                dve.wait_ge(sa_m, b + 1)
                dve.tensor_tensor(SA[:, u, :], sc, spread(mA[:, u], 2, LC), ALU.subtract).then_inc(sa_c, 1)
            for b in range(NB):
                u = slice(b * TPB, (b + 1) * TPB)
                dve.wait_ge(sa_e, b + 1)
                dve.tensor_reduce(lA[:, u], SA[:, u, :], AX.X, ALU.add).then_inc(sa_l, 1)
                dve.wait_ge(sa_l, b + 1)
                dve.reciprocal(rA[:, u], lA[:, u]).then_inc(sa_r, 1)
                dve.wait_ge(sa_r, b + 1)
                dve.wait_ge(s_g, 1)
                dve.tensor_scalar(rA[:, u], rA[:, u], gate[:, 0:1], None, ALU.mult).then_inc(sa_g, 1)
            for b in range(NB):
                dve.wait_ge(sa_o, b + 1)
                dve.wait_ge(sa_g, b + 1)
                for i in range(TPB):
                    u = b * TPB + i
                    dve.scalar_tensor_tensor(X[:, u, :], bank[6 + b][:, i * D:(i + 1) * D], rA[:, u:u + 1],
                                             X[:, u, :], ALU.mult, ALU.add).then_inc(s_xu, 1)


            def low_tokens(kth, hi_kth):
                for b in range(NB):
                    dve.wait_ge(s_xt, NB * kth + b + 1)
                    tk = slice(b * 512, (b + 1) * 512)
                    dve.tensor_tensor(XTL[:, tk], XT[:, tk], XTH[:, tk].bitcast(F32), ALU.subtract).then_inc(s_xtl, 1)

            for b in range(NB):
                row_means(1, b)
            for b in range(NB):
                normalise(1, b)
            low_tokens(1, 0)
            dve.wait_ge(b_lg, 1)
            dve.tensor_tensor(GL[:], bank[6][:, 0:NT * E0].rearrange("p (u e) -> p u e", e=E0),
                              spread(bg0[:], 1, NT), ALU.add).then_inc(b_d, 1)
            dve.wait_ge(b_d, 1)
            dve.tensor_reduce(gm[:], GL[:], AX.X, ALU.max).then_inc(b_d, 1)
            dve.wait_ge(b_d, 2)
            dve.tensor_tensor(GL[:], GL[:], spread(gm[:], 2, E0), ALU.subtract).then_inc(b_d, 1)
            dve.wait_ge(b_ex, 1)
            dve.tensor_reduce(gs[:], GL[:], AX.X, ALU.add).then_inc(b_d, 1)
            dve.wait_ge(b_d, 4)
            dve.reciprocal(gs[:], gs[:]).then_inc(b_d, 1)
            dve.wait_ge(b_d, 5)
            dve.tensor_tensor(GL[:], GL[:], spread(gs[:], 2, E0), ALU.mult).then_inc(b_d, 1)
            dve.wait_ge(b_d, 6)
            dve.tensor_reduce(gm[:], GL[:], AX.X, ALU.max).then_inc(b_d, 1)
            dve.wait_ge(b_d, 7)
            dve.tensor_tensor(EQ[:], GL[:], spread(gm[:], 2, E0), ALU.is_equal).then_inc(b_d, 1)
            dve.wait_ge(b_d, 8)
            dve.tensor_tensor(EQ[:], EQ[:], spread(rev0[:], 1, NT), ALU.mult).then_inc(b_d, 1)
            dve.wait_ge(b_d, 9)
            dve.tensor_reduce(gm[:], EQ[:], AX.X, ALU.max).then_inc(b_d, 1)
            dve.wait_ge(b_d, 10)
            dve.tensor_tensor(EQ[:], EQ[:], spread(gm[:], 2, E0), ALU.is_equal).then_inc(b_d, 1)
            dve.wait_ge(b_d, 11)
            dve.tensor_tensor(CM[:], EQ[:], GL[:], ALU.mult).then_inc(b_cm, 1)

            for b in range(NB):
                dve.wait_ge(b_ctp, b + 1)
                dve.tensor_copy(CT8[:, b * 512:(b + 1) * 512], bank[b][0:E0, :]).then_inc(b_ct, 1)

            dve.wait_ge(s_cc, 64)
            for q in range(NB * 3):
                b, g = q // 3, q % 3
                n = min(4, NCH - 4 * g)
                dve.wait_ge(c_vp, q + 1)
                dve.tensor_tensor(VBD[:, b, 4 * g:4 * g + n, 0:D],
                                  bank[q % 2][:, 0:n * D].rearrange("p (j d) -> p j d", d=D),
                                  own_head[:, 4 * g:4 * g + n, 0:D], ALU.mult).then_inc(c_vb, 1)
            for b in range(NB):
                dve.tensor_copy(VBD[:, b, :, D:DEN], own_head[:, :, D:DEN]).then_inc(c_vb, 1)

            LO_LAG = 2

            def low(e, i, first):
                n = e * BLK0 + i
                dve.wait_ge(b_hh, n + 1)
                if not first:
                    dve.wait_ge(b_dn, n + 1 - H_RING)
                r = i % H_RING
                dve.tensor_tensor(HL[:, r, :], HC[:, r, :], HH[:, r, :].bitcast(F32), ALU.subtract).then_inc(b_hl, 1)

            def pair0(p, first, last):
                for k in range(2 * BLK0):
                    j, i = k // BLK0, k % BLK0
                    n = (p * 2 + j) * BLK0 + i
                    if i in VEC0:
                        dve.wait_ge(b_si, n + 1)
                        dve.wait_ge(b_ce[j], 16 * (p + 1))
                        if not (first and k < H_RING):
                            dve.wait_ge(b_hl, n + 1 - H_RING)
                        dve.tensor_tensor(HC[:, i % H_RING, :], HA[:, i % H_RING, :],
                                          CE[:, j, (i % HALVES) * 512:(i % HALVES + 1) * 512], ALU.mult)\
                            .then_inc(b_mv, 1)
                    if k >= LO_LAG or not first:
                        m = k - LO_LAG
                        low(p * 2 + m // BLK0, m % BLK0, first and m < H_RING)
                if last:
                    for m in range(2 * BLK0 - LO_LAG, 2 * BLK0):
                        low(p * 2 + m // BLK0, m % BLK0, False)

            over_pairs(dve, NP0, pair0)

            def add_back(kth, g):
                for b in range(NB):
                    dve.wait_ge(b_yp, NB * kth + b + 1)
                    for i in range(TPB):
                        u = b * TPB + i
                        dve.scalar_tensor_tensor(X[:, u, :], bank[b][:, i * P:(i + 1) * P], gate[:, g:g + 1],
                                                 X[:, u, :], ALU.mult, ALU.add).then_inc(s_xu, 1)

            add_back(0, 2)

            for b in range(NB):
                row_means(2, b)
            for b in range(NB):
                normalise(2, b)
            for b in range(NB):
                tk = slice(b * 512, (b + 1) * 512)
                dve.wait_ge(c_qt, b + 1)
                dve.tensor_tensor(XTL[:, tk], YT[:, tk], XTH[:, tk].bitcast(F32), ALU.subtract).then_inc(c_ql, 1)

            def centre(u):
                for g, (h0, n) in enumerate(GROUPS):
                    sc = bank[2 + g][:, 0:n * LC].rearrange("p (h k) -> p h k", k=LC)
                    m = mC[:, u % 2, h0:h0 + n]
                    dve.wait_ge(c_s, 3 * u + g + 1)
                    dve.tensor_reduce(m, sc, AX.X, ALU.max).then_inc(c_m, 1)
                    dve.wait_ge(c_m, 3 * u + g + 1)
                    if u >= 2 and g == 0:
                        dve.wait_ge(c_tp, 3 * (u - 1))
                    dve.tensor_tensor(SC[:, u % 2, h0 * LC:(h0 + n) * LC].rearrange("p (h k) -> p h k", k=LC),
                                      sc, spread(m, 2, LC), ALU.subtract).then_inc(c_c, 1)

            def update(b):
                dve.wait_ge(c_y, b + 1)
                for i in range(TPB):
                    u = b * TPB + i
                    dve.wait_ge(c_xb, u + 1)
                    dve.scalar_tensor_tensor(X[:, u, :], bank[1][:, i * P:(i + 1) * P], gate[:, 1:2], X[:, u, :],
                                             ALU.mult, ALU.add).then_inc(s_xu, 1)

            centre(0)
            for u in range(NT):
                if u + 1 < NT:
                    centre(u + 1)
                dve.wait_ge(c_o, u + 1)
                dve.reciprocal(rC[:, u % 2, :], bank[0][:, D:DEN]).then_inc(c_r, 1)
                dve.wait_ge(c_r, u + 1)
                b, i = u // TPB, u % TPB
                for k in range(P // AA):
                    q = slice(k * AA, (k + 1) * AA)
                    ins = dve.tensor_tensor(OA[:, b, :, i * (P // AA) + k, :],
                                            bank[0][q, 0:D].rearrange("p (h d) -> p h d", d=DH1),
                                            spread(rC[q, u % 2, :], 2, DH1), ALU.mult)
                ins.then_inc(c_n, 1)
                if u and i == 0:
                    update(b - 1)
            update(NB - 1)

            for b in range(NB):
                row_means(3, b)
            for b in range(NB):
                normalise(3, b)
                dve.wait_ge(s_rr, 4 * (b + 1))
                for i in range(TPB):
                    u = b * TPB + i
                    dve.wait_ge(s_xn, NT * 3 + u + 1)
                    dve.tensor_scalar(XR[:, u, :], XN[:, u, :], rms[:, u:u + 1], None, ALU.mult).then_inc(s_xr, 1)
            low_tokens(3, 1)

            def rope_terms(r):
                kind, n = rope_block(r)
                G = n if kind == "k" else n // 2
                for swap, (dst, table) in enumerate(((T1, cosT), (T2, sinT))):
                    col = G % KV * 6 + (4 + swap if kind == "k" else 2 * swap + n % 2)
                    dve.wait_ge(d_qp, 2 * r + swap + 1)
                    if r >= 2 and swap == 0:
                        dve.wait_ge(d_ts, r - 1)
                    dve.scalar_tensor_tensor(dst[:, r % 2], bank[swap][:, :], qkv_bias[:, col:col + 1], table,
                                             ALU.add, ALU.mult).then_inc(d_t, 1)

            dve.wait_ge(d_cl, 16 * 9)
            dve.wait_ge(d_vl, 1)
            for k in range(NT // 2):
                dve.wait_ge(d_vp, k + 1)
                dve.tensor_tensor(VS[:, 2 * k:2 * k + 2], bank[2 + k][:, :].rearrange("p (u d) -> p u d", u=2),
                                  spread(v_bias[:], 1, 2), ALU.add).then_inc(d_v, 1)
            for r in range(3):
                rope_terms(r)
            ropes = 3
            dve.wait_ge(d_ns, 1)
            for q in range(NQ + 3):
                if q < NQ:
                    n, i = q // TPB, q % TPB
                    dve.wait_ge(d_s, q + 1)
                    if q >= 4:
                        dve.wait_ge(d_tp, q - 3)
                    k0 = 128 if i == 0 else 0
                    for hd in range(2):
                        at = slice(hd * 256 + k0, (hd + 1) * 256)
                        ins = dve.tensor_tensor_reduce(SM[:, q % 4, at], bank[2 + q % 2][:, at], window[:, k0:256],
                                                       1.0, -3e38, ALU.add, ALU.max, mD[:, q % 4, hd:hd + 1])
                    ins.then_inc(d_m, 1)
                    c = n % PAIRS
                    dve.wait_ge(d_m, q + 1)
                    dve.scalar_tensor_tensor(nm[:, n % 2, i, :], mD[:, q % 4, :], -DH ** -0.5,
                                             nsink[:, 2 * c:2 * c + 2], ALU.mult, ALU.min).then_inc(d_nm, 1)
                if q in ROPE_AT:
                    rope_terms(ropes)
                    ropes += 1
                if q < NQ and i == TPB - 1:
                    if n >= 2:
                        dve.wait_ge(d_es, n - 1)
                    dve.wait_ge(d_nm, q + 1)
                    dve.tensor_tensor(zs[:, n % 2], nm[:, n % 2], spread(sink[:, 2 * c:2 * c + 2], 1, TPB), ALU.add)\
                        .then_inc(d_zs, 1)
                m, k = q // 4 - 1, q % 4
                if k == 2 and 0 <= m < NU:
                    dve.wait_ge(d_es, m + 1)
                    dve.wait_ge(d_e, TPB * (m + 1))
                    dve.tensor_tensor(den[:, m % 2], den[:, m % 2], lD[:, m % 2], ALU.add).then_inc(d_dn, 1)
                    dve.wait_ge(d_dn, m + 1)
                    dve.reciprocal(den[:, m % 2], den[:, m % 2]).then_inc(d_rc, 1)
                    dve.wait_ge(d_rc, m + 1)
                    dve.wait_ge(d_y, TPB * (m + 1))
                    if m >= 2:
                        dve.wait_ge(d_yt, m - 1)
                    dve.tensor_tensor(YS[:, m % 2].rearrange("p (x d) -> p x d", d=DH),
                                      bank[6][:, :].rearrange("p (x d) -> p x d", d=DH),
                                      spread(den[:, m % 2].rearrange("p i h -> p (i h)"), 2, DH), ALU.mult)\
                        .then_inc(d_ys, 1)
                if q == TPB * (PAIRS + 2):
                    dve.wait_ge(d_x0, NB)
                    dve.wait_ge(d_pr, PAIRS)
                    dve.tensor_tensor(X1[:, 0:TPB, :].rearrange("p i d -> p (i d)"),
                                      X1[:, 0:TPB, :].rearrange("p i d -> p (i d)"), bank[7][:, :], ALU.add)\
                        .then_inc(d_x1, 1)
            dve.wait_ge(d_pr, NU)
            dve.tensor_tensor(X1[:, TPB:, :].rearrange("p i d -> p (i d)"),
                              X1[:, TPB:, :].rearrange("p i d -> p (i d)"), bank[7][:, :], ALU.add).then_inc(d_x1, 1)

            for b in range(NB):
                dve.wait_ge(s_rr, 4 * NB + 3 * (b + 1))
                for i in range(TPB):
                    u = b * TPB + i
                    dve.tensor_scalar(XR[:, u, :], X1[:, u, :], rms[:, u:u + 1], None, ALU.mult).then_inc(s_xr, 1)

            def low_expert(e, s):
                dve.wait_ge(e_wh, 2 * e + 2)
                dve.tensor_tensor(ZU[2][:, s, :], ZU[0][:, s, :], ZU[1][:, s, :].bitcast(F32), ALU.subtract)\
                   .then_inc(e_wl, 1)
                dve.tensor_tensor(ZD[2][:, s, :], ZD[0][:, s, :], ZD[1][:, s, :].bitcast(F32), ALU.subtract)\
                   .then_inc(e_wl, 1)

            for s in range(2):
                low_expert(s, s)
            low_tokens(4, 2)
            dve.wait_ge(e_lg, 1)
            dve.wait_ge(e_cl, 48)
            dve.tensor_tensor(GZ[:], bank[5][:, 0:NT * E1].rearrange("p (u e) -> p u e", e=E1),
                              spread(gate_b[:], 1, NT), ALU.add).then_inc(e_r, 1)
            dve.wait_ge(e_r, 1)
            for u in range(NT):
                ins = dve.max(m8[:, u, :], GZ[:, u, :])
            ins.then_inc(e_cm, 1)
            dve.wait_ge(e_cm, 1)
            dve.tensor_tensor(wt[:], m8[:, :, 0:TOPK], m8[:, :, 0:1].broadcast_to([P, NT, TOPK]), ALU.subtract)\
               .then_inc(e_r, 1)
            for u in range(NT):
                ins = dve.max_index(i8[:, u, :], m8[:, u, :], GZ[:, u, :])
            ins.then_inc(e_r, 1)
            dve.wait_ge(e_r, 3)
            dve.tensor_copy(if8[:], i8[:, :, 0:TOPK]).then_inc(e_r, 1)
            dve.wait_ge(e_ex, 1)
            dve.tensor_reduce(wsum[:], wt[:], AX.X, ALU.add).then_inc(e_r, 1)
            dve.wait_ge(e_r, 5)
            dve.reciprocal(wsum[:], wsum[:]).then_inc(e_r, 1)
            dve.wait_ge(e_r, 6)
            dve.tensor_tensor(wt[:], wt[:], spread(wsum[:], 2, TOPK), ALU.mult).then_inc(e_r, 1)
            dve.tensor_tensor(EQ4, spread(spread(experts[:], 1, NT), 3, TOPK), spread(if8[:], 2, E1), ALU.is_equal)\
               .then_inc(e_r, 1)
            dve.wait_ge(e_r, 8)
            dve.tensor_tensor(EQ4, EQ4, spread(wt[:], 2, E1), ALU.mult).then_inc(e_r, 1)
            dve.wait_ge(e_r, 9)
            dve.tensor_reduce(GZ[:], EQ4, AX.X, ALU.add).then_inc(e_r, 1)
            for b in range(NB):
                dve.wait_ge(e_ctp, b + 1)
                dve.tensor_copy(CT1[:, b * 512:(b + 1) * 512], bank[2 + b][0:E1, :]).then_inc(e_ct, 1)

            def low_e(n, k, first):
                dve.wait_ge(e_hh, n + 1)
                if not first:
                    dve.wait_ge(e_dn, n + 1 - H_RING)
                r = k % H_RING
                dve.tensor_tensor(HL[:, r, :], HC[:, r, :], HH[:, r, :].bitcast(F32), ALU.subtract).then_inc(e_hl, 1)

            LO1 = 2

            def quad(p, first, last):
                for k in range(QUAD * HALVES):
                    n, s, h = p * QUAD * HALVES + k, k // HALVES, k % HALVES
                    if not first or k >= LO1:
                        low_e(n - LO1, (k - LO1) % H_RING, first and k - LO1 < H_RING)
                    dve.wait_ge(e_u, n + 1)
                    dve.wait_ge(e_si, n + 1)
                    dve.tensor_tensor(HA[:, k % H_RING, :], bank[4 + k % 2][:, :], HA[:, k % H_RING, :], ALU.mult)\
                       .then_inc(e_mu, 1)
                    if h == 1 and not (last and s >= 2):
                        low_expert(p * QUAD + s + 2, (s + 2) % QUAD)
                if last:
                    for k in range(QUAD * HALVES - LO1, QUAD * HALVES):
                        low_e(p * QUAD * HALVES + k, k, False)

            over_pairs(dve, E1 // QUAD, quad)
            add_back(1, 3)


_NAMES = ("x", "ctx_768", "g_xattn", "g_ffn", "L0_xattn_Wq", "L0_xattn_bq", "L0_xattn_Wk", "L0_xattn_bk",
          "L0_xattn_Wv", "L0_xattn_bv", "L0_ffn_Wg", "L0_ffn_bg", "L0_ffn_W1", "L0_ffn_b1", "L0_ffn_W2", "L0_ffn_b2",
          "L1_xattn_q_w", "L1_xattn_q_b", "L1_xattn_k_w", "L1_xattn_k_b", "L1_xattn_v_w", "L1_xattn_v_b",
          "L1_xattn_o_w", "L1_xattn_o_b", "L1_ffn_attn_norm_w", "L1_ffn_ffn_norm_w", "L1_ffn_qkv_w", "L1_ffn_qkv_b",
          "L1_ffn_proj_w", "L1_ffn_proj_b", "L1_ffn_attn_sink", "L1_ffn_gate_w", "L1_ffn_gate_b", "L1_ffn_W_up",
          "L1_ffn_W_down")
_UNUSED = ("L1_xattn_k_w", "L1_xattn_k_b")


def kernel(**inputs):
    import concourse.bacc as bacc
    from concourse.bass_utils import run_bass_kernel_spmd

    nc = bacc.Bacc("TRN2", target_bir_lowering=False, num_devices=1)
    arrays = {name: np.ascontiguousarray(inputs[name]) for name in _NAMES if name not in _UNUSED}
    arrays.update(constants())
    arrays.update(qkv_by_group(arrays["L1_ffn_qkv_w"], arrays["L1_ffn_qkv_b"]))
    b1 = arrays.pop("L0_ffn_b1")
    arrays["L0_ffn_b1_columns"] = np.ascontiguousarray(b1.reshape(len(b1), -1, P).transpose(0, 2, 1))
    t, named = {}, {}
    for name, a in arrays.items():
        named[f"in_{name}_dram"] = a
        t[name] = nc.dram_tensor(f"in_{name}_dram", a.shape, mybir.dt.from_np(a.dtype), kind="ExternalInput").ap()
    out = nc.dram_tensor("out_0_dram", arrays["x"].shape, F32, kind="ExternalOutput").ap()
    flamingo_two_layers(nc, t, out)
    r = run_bass_kernel_spmd(nc, [named], core_ids=[0])
    return r.results[0]["out_0_dram"]
```

```python
from contextlib import ExitStack

import numpy as np

import concourse.bass as bass
from concourse import mybir
from concourse.alu_op_type import AluOpType as ALU

F32 = mybir.dt.float32
F32R = mybir.dt.float32r
U32 = mybir.dt.uint32
ACT = mybir.ActivationFunctionType
AX = mybir.AxisListType

P = 128
EPS = 1e-5


def constants():
    lc, heads, d, chunks = 77, 16, 128, 10
    flat = np.arange(chunks * P)
    head = np.where(flat < heads * lc, flat // lc, -1)
    token = np.where(flat < heads * lc, flat % lc, -1)
    own = np.concatenate([head[:, None] == np.arange(d)[None] // (d // heads),
                          head[:, None] == np.arange(heads)[None]], axis=1).astype(np.float32)
    seq, window, dh = 512, 128, 64
    inv_freq = (1.0 / np.float32(150000.0) ** (np.arange(0, dh, 2, dtype=np.float32) / np.float32(dh))).astype(np.float32)
    pos = np.arange(seq, dtype=np.float32) / np.float32(32.0)
    angle = (inv_freq[:, None] * pos[None, :]).astype(np.float32)[(np.arange(P) % dh) // 2]
    sign = np.where(np.arange(P) % 2 == 0, -1.0, 1.0)[:, None]
    r, c = np.arange(P)[:, None], np.arange(P)[None]
    masked = np.concatenate([r - c > 0, c > r], axis=1)
    return {
        "c_ident": np.eye(P, dtype=np.float32),
        "c_rev": np.arange(8, 0, -1).astype(np.float32),
        "c_head_cols": (np.arange(d)[:, None] // (d // heads) == np.arange(heads)[None]).astype(np.float32),
        "c_repeat_ctx": (np.arange(lc)[:, None] == token[None]).astype(np.float32),
        "c_own_head": own.reshape(chunks, P, d + heads).transpose(1, 0, 2).copy(),
        "c_cos": np.cos(angle.astype(np.float64)).astype(np.float32),
        "c_sin": (sign * np.sin(angle.astype(np.float64))).astype(np.float32),
        "c_window": np.where(masked, np.float32(-1e30), np.float32(0)).astype(np.float32),
        "c_experts": np.arange(32).astype(np.float32),
    }


def qkv_by_group(w, b):
    heads, kv, dh = 16, 4, 64
    columns = []
    for g in range(kv):
        q = np.arange(g * (heads // kv) * dh, (g + 1) * (heads // kv) * dh)
        k = np.tile(heads * dh + np.arange(g * dh, (g + 1) * dh), 2)
        columns.append(np.concatenate([q, k]))
    columns = np.stack(columns)
    pairs = np.stack([columns.reshape(kv, 3, P), columns.reshape(kv, 3, P) ^ 1], axis=2)
    return {"qkv_w_groups": np.ascontiguousarray(w[:, columns].transpose(1, 0, 2)),
            "qkv_b_groups": np.ascontiguousarray(b[pairs].reshape(-1, P).T)}


def spread(ap, axis, n):
    wide = ap.unsqueeze(axis)
    shape = list(wide.shape)
    shape[axis] = n
    return wide.broadcast_to(shape)


def flamingo_two_layers(nc, t, out):
    NB, SEQ, D = t["x"].shape
    LC, DC = t["ctx_768"].shape[1:]
    TPB = SEQ // P
    NT = NB * TPB
    T = NB * SEQ
    E0, _, F0 = t["L0_ffn_W1"].shape
    C0 = F0 // P
    E1, _, F1x2 = t["L1_ffn_W_up"].shape
    TOPK = 4
    H1 = 16
    DH1 = D // H1
    HK = H1 * LC
    HEADS, KV, DH, WINDOW = 16, 4, 64, 128
    QD, KD = HEADS * DH, KV * DH
    PAIRS = HEADS // 2
    HALVES = T // 512
    assert D == P and WINDOW == P and SEQ == 512 and F1x2 == 2 * P

    ctx = ExitStack()
    with ctx:
        def sb(name, shape, dt=F32):
            return ctx.enter_context(nc.sbuf_tensor(name, list(shape), dt))

        def sem(name):
            return ctx.enter_context(nc.semaphore(name))

        bank = [ctx.enter_context(nc.psum_tensor(f"bank{i}", [P, 512], F32)) for i in range(2)]
        mid3 = ctx.enter_context(nc.psum_tensor("mid3", [P, 3, 512], F32))
        bank += [mid3[:, i, :] for i in range(3)]
        bank += [ctx.enter_context(nc.psum_tensor(f"bank{i}", [P, 512], F32)) for i in range(5, 6)]
        top2 = ctx.enter_context(nc.psum_tensor("top2", [P, 2, 512], F32))
        bank += [top2[:, i, :] for i in range(2)]

        ident = sb("ident", [P, P])
        X = sb("X", [P, NT, D])
        XN = sb("XN", [P, NT, D])
        XR = sb("XR", [P, NT, D])
        X1 = sb("X1", [P, NT, D])
        XT = sb("XT", [P, T])
        XTH = sb("XTH", [P, T], F32R)
        XTL = sb("XTL", [P, T], F32R)
        stats = sb("stats", [P, NT, 6])
        mv = sb("mv", [P, NT, 2])
        ve = sb("ve", [P, NT])
        rstd = sb("rstd", [P, NT])
        minus_half = sb("minus_half", [P, NT])

        ctx_rows = sb("ctx_rows", [LC, NB, DC])
        wk0 = sb("wk0", [DC, D])
        wv0 = sb("wv0", [DC, D])
        wq0 = sb("wq0", [P, D])
        qw1 = sb("qw1", [P, D])
        ow1 = sb("ow1", [P, D])
        vw1 = sb("vw1", [P, DC])
        NROWS = 6
        rows = sb("rows", [NROWS, P])
        cols = sb("cols", [P, NROWS])
        BQ, BK, QB, VB, ATTN_W, FFN_W = range(NROWS)
        bias_v = sb("bias_v", [LC, 4, D])
        gate_in = sb("gate_in", [P, 4])
        gate = sb("gate", [P, 4])
        ctxT = sb("ctxT", [DC, NB * LC])
        WT = sb("WT", [P, 4, D])
        KT0 = sb("KT0", [P, NB * LC])
        KA = sb("KA", [P, NB * LC])
        BQW = sb("BQW", [P, P])
        VV = sb("VV", [LC, 2, NB, D])
        V1T = sb("V1T", [P, NB * LC])
        SA = sb("SA", [P, NT, LC])
        mA = sb("mA", [P, NT])
        lA = sb("lA", [P, NT])
        rA = sb("rA", [P, NT])
        PTA = sb("PTA", [LC, NT, P])

        UP_RING, H_RING, LEAD0 = 4, 4, 5
        NP0, NP1 = E0 // 2, E1 // 2
        BLK0 = C0 * HALVES
        b1 = sb("b1", [P, 2, C0])
        wg0 = sb("wg0", [P, E0])
        bg0 = sb("bg0", [P, E0])
        rev0 = sb("rev0", [P, E0])
        b2 = sb("b2", [E0, D])
        GL = sb("GL", [P, NT, E0])
        EQ = sb("EQ", [P, NT, E0])
        gm = sb("gm", [P, NT])
        gs = sb("gs", [P, NT])
        CM = sb("CM", [P, NT, E0])
        CT8 = sb("CT8", [E0, T])
        CE = sb("CE", [P, 2, T])
        W1 = sb("W1", [P, 2, F0])
        W1H = sb("W1H", [P, 2, F0], F32R)
        W1L = sb("W1L", [P, 2, F0], F32R)
        W2 = sb("W2", [P, 2, C0, D])
        W2H = sb("W2H", [P, 2, C0, D], F32R)
        W2L = sb("W2L", [P, 2, C0, D], F32R)
        HA = sb("HA", [P, H_RING, 512])
        HC = sb("HC", [P, H_RING, 512])
        HH = sb("HH", [P, H_RING, 512], F32R)
        HL = sb("HL", [P, H_RING, 512], F32R)
        YT = sb("YT", [P, T])
        c0_dram = nc.dram_tensor("c0_dram", [E0, T], F32).ap()

        NCH = (HK + P - 1) // P
        DEN = D + H1
        GROUPS = ((0, 6), (6, 6), (12, 4))
        head_cols = sb("head_cols", [P, H1])
        repeat_ctx = sb("repeat_ctx", [LC, NCH * P])
        own_head = sb("own_head", [P, NCH, DEN])
        VTH = sb("VTH", [P, NB, HK], F32R)
        VTL = sb("VTL", [P, NB, HK], F32R)
        V1TH = sb("V1TH", [P, NB * LC], F32R)
        V1TL = sb("V1TL", [P, NB * LC])
        VBD = sb("VBD", [P, NB, NCH, DEN])
        SC = sb("SC", [P, 2, HK])
        SCS = [SC[:, 0, :], SC[:, 1, :], HC[:].rearrange("p r k -> p (r k)")[:, 0:HK]]
        PTC = sb("PTC", [P, NCH, P])
        mC = sb("mC", [P, 2, H1])
        rC = sb("rC", [P, 2, H1])
        STR = D // DH1
        AA = SEQ // STR
        OA = sb("OA", [AA, NB, H1, STR, DH1])
        OT = sb("OT", [P, NB, SEQ])
        ob = sb("ob", [P, D])


        NG = NB * KV
        NU = NB * PAIRS
        NQ = NU * TPB
        GW = 3 * P
        flat = "p a b -> p (a b)"
        w_raw = W1[:].rearrange(flat)
        WH, WL = W1H[:].rearrange(flat), W1L[:].rearrange(flat)
        proj_w = W2[:].rearrange("p a c d -> p (a c) d")
        QH = HH
        QL = W2H[:].rearrange("p a c d -> p a (c d)")
        KHH = W2L[:].rearrange("p a c d -> p a (c d)")
        KL = (HL[:, 0:2, :], HL[:, 2:4, :])
        UQ = [v[:].rearrange("p b k -> p (b k)")[:, s * 1024:(s + 1) * 1024].rearrange("p (h t) -> p h t", h=2)
              for v in (VTH, VTL) for s in range(2)]
        SM = HA
        T1, T2 = HC[:, 0:2, :], HC[:, 2:4, :]
        VS = CE[:].rearrange("p j (i d) -> p (j i) d", d=KD)
        sc_flat = SC[:].rearrange("p s k -> p (s k)")
        TS = sc_flat[:, 0:1024].rearrange("p (s k) -> p s k", s=2)
        YS = sc_flat[:, 1024:2048].rearrange("p (s k) -> p s k", s=2)
        PT = PTC[:].rearrange("p c k -> p (c k)")[:, 0:1024].rearrange("p (s k) -> p s k", s=2)
        YTC = VBD[:].rearrange("p b c k -> p (b c k)")[:, 0:1024].rearrange("p (s k) -> p s k", s=2)
        own_flat = own_head[:].rearrange("p c k -> p (c k)")
        cosT, sinT, window = own_flat[:, 0:SEQ], own_flat[:, SEQ:2 * SEQ], own_flat[:, 2 * SEQ:2 * SEQ + 2 * P]
        qkv_bias = sb("qkv_bias", [P, KV * 6])
        v_bias = sb("v_bias", [P, KD])
        proj_b = sb("proj_b", [P, D])
        sink = sb("sink", [P, HEADS])
        nsink = sb("nsink", [P, HEADS])
        rms = sb("rms", [P, NT])
        mD = sb("mD", [P, 4, 2])
        nm = sb("nm", [P, 2, TPB, 2])
        zs = sb("zs", [P, 2, TPB, 2])
        lD = sb("lD", [P, 2, TPB, 2])
        den = sb("den", [P, 2, TPB, 2])

        def rope_block(r):
            if r == 0:
                return "k", 0
            if r < 3:
                return "q", r - 1
            g = r // 3 - 1
            return (("q", 2 * g + 2), ("k", g + 1), ("q", 2 * g + 3))[r % 3]

        V_BANK = (bank[2], bank[3], bank[7], bank[7])
        ROOTS_AT = 1
        SQ_AT = 45
        T_LAG = 3
        NDVE = 3
        BLOCK_OF = {rope_block(r): r for r in range(3 * NG)}
        ROPE_AT = {8 * g + s: 3 * g + 3 + k for g in range(NG - 1) for k, s in enumerate((1, 3, 5))}

        NB1 = E1 * HALVES
        QUAD = 4
        ZU, ZD = [[w[:].rearrange(pat)[:, 0:QUAD * n].rearrange("p (s f) -> p s f", s=QUAD)
                   for w in ws] for ws, pat, n in (((W1, W1H, W1L), "p a b -> p (a b)", F1x2),
                                                   ((W2, W2H, W2L), "p a c d -> p (a c d)", D))]
        CZ = [CE[:, 0, :], CE[:, 1, :], sc_flat[:, 0:T], sc_flat[:, T:2 * T]]
        CT1 = YT[0:E1, :]
        row0 = sb("row0", [E1, P])
        EQ4 = XN[:].rearrange("p u d -> p (u d)").rearrange("p (u e k) -> p u e k", u=NT, k=TOPK)
        gate_w = sb("gate_w", [P, E1])
        gate_b = sb("gate_b", [P, E1])
        experts = sb("experts", [P, E1])
        GZ = sb("GZ", [P, NT, E1])
        m8 = sb("m8", [P, NT, 8])
        i8 = sb("i8", [P, NT, 8], U32)
        if8 = sb("if8", [P, NT, TOPK])
        wt = sb("wt", [P, NT, TOPK])
        wsum = sb("wsum", [P, NT])
        c1_dram = nc.dram_tensor("c1_dram", [E1, T], F32).ap()

        s_id = sem("ident_loaded")
        s_x = [sem(f"x_loaded{b}") for b in range(NB)]
        s_w0 = sem("setup_rows_loaded")
        s_w2 = sem("second_layer_weights_loaded")
        s_w1 = sem("setup_weights_loaded")
        s_b0 = sem("setup_biases_loaded")
        s_st = sem("row_stats")
        s_mv = sem("row_mean_var")
        s_ve = sem("var_eps")
        s_rs = sem("rstd")
        s_xn = sem("xn")
        s_xu = sem("x_updated")
        s_xtp = sem("xt_in_psum")
        s_xt = sem("xt")
        s_mh = sem("minus_half_set")
        s_g = sem("gate_tanh")
        s_p1 = sem("setup_transposes")
        s_e1 = sem("setup_evacuated")
        s_bq = sem("bq_spread")
        s_kt = sem("kt0_out")
        s_vw = sem("v_w_transposed")
        s_p2 = sem("setup_products")
        s_e2 = sem("setup_products_out")
        s_p3 = sem("ka_product")
        s_e3 = sem("ka_out")
        sa_s = sem("a_scores")
        sa_m = sem("a_max")
        sa_c = sem("a_centred")
        sa_e = sem("a_exp")
        sa_l = sem("a_sum")
        sa_r = sem("a_recip")
        sa_g = sem("a_recip_gate")
        sa_t = sem("a_pT_in_psum")
        sa_p = sem("a_pT")
        sa_o = sem("a_out")
        s_st1 = sem("stored")
        s_xth = sem("xt_high")
        s_xtl = sem("xt_low")
        s_rl = sem("router_inputs_loaded")
        b_lg = sem("b_logits")
        b_d = sem("b_router_vector_steps")
        b_ex = sem("b_router_exp")
        b_cm = sem("b_weights")
        b_ctp = sem("b_weights_transposed")
        b_ct = sem("b_weights_T")
        b_cs = sem("b_weights_stored")
        b_ce = [sem(f"b_weights_spread{i}") for i in range(2)]
        b_b1 = [sem(f"b_biases_loaded{i}") for i in range(2)]
        b_w1 = [sem(f"b_w1_loaded{i}") for i in range(2)]
        b_w2 = [sem(f"b_w2_loaded{i}") for i in range(2)]
        b_w1h = sem("b_w1_high")
        b_w1l = sem("b_w1_low")
        b_w2h = sem("b_w2_high")
        b_w2l = sem("b_w2_low")
        b_up = sem("b_up_products")
        b_si = sem("b_silu")
        b_mv = sem("b_weighted_by_vector")
        b_mp = sem("b_weighted_by_gpsimd")
        b_hh = sem("b_hidden_high")
        b_hl = sem("b_hidden_low")
        b_dn = sem("b_down_products")
        b_yt = sem("b_y_out")
        b_yp = sem("b_y_transposed")
        s_cc = sem("c_constants_loaded")
        c_vh = sem("c_values_split")
        c_vt = sem("c_values_by_head")
        c_vp = sem("c_values_repeated")
        c_vb = sem("c_values_block_diagonal")
        c_q = sem("c_queries")
        c_qh = sem("c_queries_high")
        c_qt = sem("c_queries_out")
        c_ql = sem("c_queries_low")
        c_s = sem("c_scores")
        c_m = sem("c_max")
        c_c = sem("c_centred")
        c_e = sem("c_exp")
        c_tp = sem("c_pT_in_psum")
        c_p = sem("c_pT")
        c_o = sem("c_out")
        c_r = sem("c_recip")
        c_n = sem("c_normed")
        c_otp = sem("c_outT_in_psum")
        c_ot = sem("c_outT")
        c_y = sem("c_projected")
        c_ob = sem("c_bias_gated")
        c_xb = sem("c_bias_added")
        s_rr = sem("rms_steps")
        s_xr = sem("xr")
        d_cl = sem("d_constants_loaded")
        d_ns = sem("d_sink_negated")
        d_wg = sem("d_group_weights_loaded")
        d_vw = sem("d_value_weights_high")
        d_vl = sem("d_value_weights_low")
        d_wh = sem("d_group_weights_high")
        d_wl = sem("d_group_weights_low")
        d_vp = sem("d_value_products")
        d_v = sem("d_values")
        d_kz = sem("d_key_zeros")
        d_x0 = sem("d_residual_started")
        d_qp = sem("d_qk_products")
        d_sh = sem("d_rope_exchanged")
        d_t = sem("d_rope_terms")
        d_ts = sem("d_rope_sum")
        d_ts0 = sem("d_rope_sum_by_vector")
        d_hi = sem("d_qk_high")
        d_lo = sem("d_qk_low")
        d_u = [sem(f"d_queries_stacked{i}") for i in range(2)]
        d_s = sem("d_scores")
        d_m = sem("d_max")
        d_nm = sem("d_minus_max")
        d_e = sem("d_exp")
        d_tp = sem("d_pT_in_psum")
        d_pt = sem("d_pT")
        d_y = sem("d_attended")
        d_zs = sem("d_sink_minus_max")
        d_es = sem("d_sink_exp")
        d_dn = sem("d_denominator")
        d_rc = sem("d_recip")
        d_ys = sem("d_normed")
        d_yt = sem("d_yT_in_psum")
        d_yc = sem("d_yT")
        d_pr = sem("d_projected")
        d_x1 = sem("d_residual")
        e_cl = sem("e_constants_loaded")
        e_sq = sem("e_squares")
        e_lg = sem("e_logits")
        e_r = sem("e_router_vector_steps")
        e_cm = sem("e_router_top")
        e_ex = sem("e_router_exp")
        e_ctp = sem("e_weights_transposed")
        e_ct = sem("e_weights_T")
        e_r0 = sem("e_row0")
        e_z0p = sem("e_first_weights_in_psum")
        e_z0 = sem("e_first_weights_spread")
        e_cs = sem("e_weights_stored")
        e_ce = [sem(f"e_weights_spread{s}") for s in range(QUAD)]
        e_wu, e_wd = b_w1 + b_b1, b_w2 + b_ce
        LOADS0 = (16 * NP0,) * 4
        LOADS1 = (16 * NP0, 16 * NP0, 16 * (NP0 - 1), 16 * NP0)
        e_uh = sem("e_w_up_high")
        e_ul = sem("e_w_up_low")
        e_wh = sem("e_w_down_high")
        e_wl = sem("e_w_down_low")
        e_g = sem("e_gate_products")
        e_u = sem("e_up_products")
        e_si = sem("e_silu")
        e_mu = sem("e_hidden")
        e_c = sem("e_weighted")
        e_hh = sem("e_hidden_high")
        e_hl = sem("e_hidden_low")
        e_dn = sem("e_down_products")

        POOL0 = (3, 7)
        VEC0 = tuple(i for i in range(BLK0) if i not in POOL0)

        def over_pairs(eng, pairs, body):
            body(0, True, False)
            with eng.Fori(1, pairs - 1) as p:
                body(p, False, False)
            body(pairs - 1, False, True)

        def wait_weights0(eng, p, j, i, first):
            if first and j == 0:
                eng.wait_ge(e_z0, i % HALVES + 1)
            else:
                eng.wait_ge(b_ce[j], 16 * (p + j))

        def rope_bank(r):
            return bank[4] if r == 1 else bank[r % 2]

        def wait_rope_sum(eng, r):
            if r < NDVE:
                eng.wait_ge(d_ts0, r + 1)
            else:
                eng.wait_ge(d_ts, r + 1 - NDVE)

        def rows_of(b):
            return t["x"][b].rearrange("(t p) d -> p t d", p=P)

        block = ctx.enter_context(nc.Block())

        def load_mixture0(sp):
            def weights(e, j, first):
                if not first:
                    sp.wait_ge(b_w1h, e - 1)
                    sp.wait_ge(b_w1l, e - 1)
                sp.dma_start(W1[:, j, :], t["L0_ffn_W1"][bass.ds(e, 1), :, :].squeeze(0)).then_inc(b_w1[j], 16)
                if not first:
                    sp.wait_ge(b_w2h, e - 1)
                    sp.wait_ge(b_w2l, e - 1)
                sp.dma_start(W2[:, j], t["L0_ffn_W2"][bass.ds(e, 1), :, :].squeeze(0).rearrange("(c p) d -> p c d", p=P))\
                  .then_inc(b_w2[j], 16)

            def biases(e, j):
                sp.dma_start(b1[:, j, :], t["L0_ffn_b1_columns"][bass.ds(e, 1), :, :].squeeze(0)).then_inc(b_b1[j], 16)

            for j in range(2):
                weights(j, j, True)
                biases(j, j)
            sp.wait_ge(b_ct, HALVES)
            sp.dma_start(c0_dram, CT8[:]).then_inc(b_cs, 16)
            sp.wait_ge(b_cs, 16)

            def pair(p, first, last):
                for j in range(2):
                    e = p * 2 + j
                    if not first:
                        sp.wait_ge(b_hl, (e - 1) * BLK0)
                    if not (first and j == 0):
                        sp.dma_start(CE[:, j, :], c0_dram[bass.ds(e, 1), :].squeeze(0).partition_broadcast(P))\
                          .then_inc(b_ce[j], 16)
                    if not first:
                        biases(e, j)
                    if not last:
                        weights(e + 2, j, False)

            over_pairs(sp, NP0, pair)

        @block.sync
        def _(sp):
            sp.dma_start(ident[:], t["c_ident"]).then_inc(s_id, 16)
            for b in range(NB):
                sp.dma_start(X[:, b * TPB:(b + 1) * TPB, :], rows_of(b)).then_inc(s_x[b], 16)
            for r, name in enumerate(("L0_xattn_bq", "L0_xattn_bk", "L1_xattn_q_b", "L1_xattn_v_b",
                                      "L1_ffn_attn_norm_w", "L1_ffn_ffn_norm_w")):
                sp.dma_start(rows[r:r + 1, :], t[name].unsqueeze(0)).then_inc(s_w0, 16)
            for i, name in enumerate(("L0_xattn_bv", "L0_xattn_bv", "L1_xattn_v_b", "L1_xattn_v_b")):
                sp.dma_start(bias_v[:, i, :], t[name].partition_broadcast(LC)).then_inc(s_b0, 16)
            sp.dma_start(gate_in[:, 0:2], t["g_xattn"].partition_broadcast(P)).then_inc(s_b0, 16)
            sp.dma_start(gate_in[:, 2:4], t["g_ffn"].partition_broadcast(P)).then_inc(s_b0, 16)

            for dst, src in ((wg0[:], t["L0_ffn_Wg"]), (bg0[:], t["L0_ffn_bg"].partition_broadcast(P)),
                             (rev0[:], t["c_rev"].partition_broadcast(P)), (b2[:], t["L0_ffn_b2"])):
                sp.dma_start(dst, src).then_inc(s_rl, 16)
            for dst, src in ((head_cols[:], t["c_head_cols"]), (repeat_ctx[:], t["c_repeat_ctx"]),
                             (own_head[:], t["c_own_head"]), (ob[:], t["L1_xattn_o_b"].partition_broadcast(P))):
                sp.dma_start(dst, src).then_inc(s_cc, 16)
            load_mixture0(sp)

            sp.wait_ge(b_dn, E0 * BLK0)
            sp.wait_ge(c_vb, 4 * NB)
            for dst, src in ((cosT, t["c_cos"]), (sinT, t["c_sin"]), (window, t["c_window"]),
                             (w_raw[:, GW:GW + KD], t["L1_ffn_qkv_w"][:, QD + KD:]),
                             (proj_w, t["L1_ffn_proj_w"].rearrange("(c p) d -> p c d", p=P)),
                             (qkv_bias[:], t["qkv_b_groups"]),
                             (v_bias[:], t["L1_ffn_qkv_b"][QD + KD:].partition_broadcast(P)),
                             (proj_b[:], t["L1_ffn_proj_b"].partition_broadcast(P)),
                             (sink[:], t["L1_ffn_attn_sink"].partition_broadcast(P))):
                sp.dma_start(dst, src).then_inc(d_cl, 16)

            def group_weights(G):
                if G:
                    sp.wait_ge(d_wh, G)
                    sp.wait_ge(d_wl, G)
                sp.dma_start(w_raw[:, 0:GW], t["qkv_w_groups"][G % KV]).then_inc(d_wg, 16)

            def stack_queries(n):
                r = BLOCK_OF["q", n]
                sp.wait_ge(d_hi, r + 1)
                if n >= 4:
                    sp.wait_ge(d_s, TPB * (n - 3))
                h = DH
                for k, (dst, src) in enumerate(((UQ[n % 4][0:h, 0, :], QH[0:h, n % 4, :]),
                                                (UQ[n % 4][h:P, 1, :], QH[h:P, n % 4, :]),
                                                (UQ[n % 4][h:P, 0, :], QL[0:h, n % 2, :]),
                                                (UQ[n % 4][0:h, 1, :], QL[h:P, n % 2, :]))):
                    if k == 2:
                        sp.wait_ge(d_lo, r + 1)
                    sp.dma_start(dst.bitcast(F32), src.bitcast(F32)).then_inc(d_u[n % 2], 16)

            group_weights(0)
            sp.wait_ge(c_n, NT)
            for r in range(3 * NG):
                kind, n = rope_block(r)
                if kind == "q":
                    if n % 2 and n // 2 + 1 < NG:
                        group_weights(n // 2 + 1)
                    stack_queries(n)

            for dst, src in ((gate_w[:], t["L1_ffn_gate_w"]), (gate_b[:], t["L1_ffn_gate_b"].partition_broadcast(P)),
                             (experts[:], t["c_experts"].partition_broadcast(P))):
                sp.dma_start(dst, src).then_inc(e_cl, 16)

            def up_weights(e, s):
                sp.dma_start(ZU[0][:, s, :], t["L1_ffn_W_up"][bass.ds(e, 1), :, :].squeeze(0)).then_inc(e_wu[s], 16)

            def down_weights(e, s):
                sp.dma_start(ZD[0][:, s, :], t["L1_ffn_W_down"][bass.ds(e, 1), :, :].squeeze(0)).then_inc(e_wd[s], 16)

            def expert(e, s):
                sp.wait_ge(e_wh, e - 3)
                sp.wait_ge(e_wl, e - 3)
                up_weights(e, s)
                down_weights(e, s)

            sp.wait_ge(d_wh, NG)
            sp.wait_ge(d_wl, NG)
            sp.wait_ge(d_vl, 1)
            for s in range(QUAD):
                up_weights(s, s)
            sp.wait_ge(d_x1, NB)
            for s in range(QUAD):
                down_weights(s, s)
            sp.wait_ge(e_ct, HALVES)
            sp.dma_start(c1_dram, CT1).then_inc(e_cs, 16)
            sp.wait_ge(e_cs, 16)

            def quad_loads(p, first, last):
                for s in range(QUAD):
                    e = p * QUAD + s
                    if not first:
                        sp.wait_ge(e_c, (e - 3) * HALVES)
                    if not (first and s == 0):
                        sp.dma_start(CZ[s], c1_dram[bass.ds(e, 1), :].squeeze(0).partition_broadcast(P))\
                          .then_inc(e_ce[s], 16)
                    if not last:
                        expert(e + QUAD, s)

            over_pairs(sp, E1 // QUAD, quad_loads)

            for b in range(NB):
                sp.wait_ge(s_xu, NT * 3 + TPB * (b + 1))
                sp.dma_start(out[b].rearrange("(t p) d -> p t d", p=P),
                             X[:, b * TPB:(b + 1) * TPB, :]).then_inc(s_st1, 16)
            sp.wait_ge(s_st1, 16 * NB)

        SETUP_W, SETUP_ROWS = 16 * 4, 16 * 6
        SETUP_B = 16 * 6

        @block.gpsimd
        def _(pool):
            pool.memset(minus_half[:], -0.5).then_inc(s_mh, 1)
            for dst, name in ((vw1, "L1_xattn_v_w"), (qw1, "L1_xattn_q_w"), (ow1, "L1_xattn_o_w")):
                pool.dma_start(dst[:], t[name]).then_inc(s_w2, 16)

            def inverse_roots(stage, b, src):
                u = slice(b * TPB, (b + 1) * TPB)
                pool.wait_ge(s_mv, NT * stage + TPB * (b + 1))
                pool.tensor_scalar(ve[:, u], src, EPS, None, ALU.add).then_inc(s_ve, 1)
                pool.wait_ge(s_ve, NB * stage + b + 1)
                pool.tensor_tensor(rstd[:, u], ve[:, u], minus_half[:, u], ALU.pow).then_inc(s_rs, 1)

            pool.wait_ge(s_mh, 1)
            for b in range(NB):
                inverse_roots(0, b, mv[:, b * TPB:(b + 1) * TPB, 1])

            def low1(e, j, first):
                pool.wait_ge(b_w1h, e + 1)
                if not first:
                    pool.wait_ge(b_up, (e - 1) * BLK0)
                pool.tensor_tensor(W1L[:, j, :], W1[:, j, :], W1H[:, j, :].bitcast(F32), ALU.subtract)\
                    .then_inc(b_w1l, 1)

            def low2(e, j, first):
                pool.wait_ge(b_w2h, e + 1)
                if not first:
                    pool.wait_ge(b_dn, (e - 1) * BLK0)
                pool.tensor_tensor(W2L[:, j], W2[:, j], W2H[:, j].bitcast(F32), ALU.subtract).then_inc(b_w2l, 1)

            def values_by_head(b):
                for part in range(2):
                    src = (V1TH[:, b * LC:(b + 1) * LC].bitcast(F32), V1TL[:, b * LC:(b + 1) * LC])[part]
                    pool.tensor_tensor((VTH, VTL)[part][:, b, :].rearrange("p (h k) -> p h k", k=LC),
                                       spread(src, 1, H1), spread(head_cols[:], 2, LC), ALU.mult).then_inc(c_vt, 1)

            for b in range(NB):
                inverse_roots(1, b, mv[:, b * TPB:(b + 1) * TPB, 1])
            low1(0, 0, True)
            low2(0, 0, True)
            pool.wait_ge(s_cc, 64)
            pool.wait_ge(c_vh, 2)
            values_by_head(0)

            def pair(p, first, last):
                for j in range(2):
                    e = p * 2 + j
                    for k, i in enumerate(POOL0):
                        if not (last and j == 1):
                            (low1, low2)[k](e + 1, 1 - j, first and j == 0)
                        n = e * BLK0 + i
                        pool.wait_ge(b_si, n + 1)
                        wait_weights0(pool, p, j, i, first)
                        if not (first and j * BLK0 + i < H_RING):
                            pool.wait_ge(b_hl, n + 1 - H_RING)
                        pool.tensor_tensor(HC[:, i % H_RING, :], HA[:, i % H_RING, :],
                                           CE[:, j, (i % HALVES) * 512:(i % HALVES + 1) * 512], ALU.mult)\
                            .then_inc(b_mp, 1)

            over_pairs(pool, NP0, pair)
            values_by_head(1)
            pool.wait_ge(s_g, 1)
            pool.tensor_scalar(ob[:], ob[:], gate[:, 1:2], None, ALU.mult).then_inc(c_ob, 1)
            for b in range(NB):
                inverse_roots(2, b, mv[:, b * TPB:(b + 1) * TPB, 1])
            pool.wait_ge(c_ob, 1)
            for u in range(NT):
                pool.wait_ge(s_xn, 2 * NT + u + 1)
                pool.tensor_tensor(X[:, u, :], X[:, u, :], ob[:], ALU.add).then_inc(c_xb, 1)

            def rms_roots(before, b, mean_square):
                u = slice(b * TPB, (b + 1) * TPB)
                steps = mean_square(u)
                pool.tensor_scalar(rms[:, u], rms[:, u], EPS, None, ALU.add).then_inc(s_rr, 1)
                pool.wait_ge(s_rr, before + steps + 1)
                pool.tensor_tensor(rms[:, u], rms[:, u], minus_half[:, u], ALU.pow).then_inc(s_rr, 1)

            pool.wait_ge(b_dn, E0 * BLK0)
            pool.wait_ge(c_xb, NT)
            pool.memset(KL[0][DH:P].bitcast(F32), 0.0)
            pool.memset(KL[1][0:DH].bitcast(F32), 0.0).then_inc(d_kz, 1)
            pool.wait_ge(d_kz, 1)
            def low_group(G):
                pool.wait_ge(d_wh, G + 1)
                if G:
                    pool.wait_ge(d_qp, 3 * G)
                pool.tensor_tensor(WL[:, 0:GW], w_raw[:, 0:GW], WH[:, 0:GW].bitcast(F32), ALU.subtract)\
                    .then_inc(d_wl, 1)

            def norm_roots(b):
                inverse_roots(3, b, mv[:, b * TPB:(b + 1) * TPB, 1])

                def of_normed(u):
                    pool.wait_ge(s_rs, NB * 3 + b + 1)
                    pool.tensor_tensor(rms[:, u], mv[:, u, 1], rstd[:, u], ALU.mult).then_inc(s_rr, 1)
                    pool.wait_ge(s_rr, 4 * b + 1)
                    pool.tensor_tensor(rms[:, u], rms[:, u], rstd[:, u], ALU.mult).then_inc(s_rr, 1)
                    pool.wait_ge(s_rr, 4 * b + 2)
                    return 2

                rms_roots(4 * b, b, of_normed)

            def square_roots(b):
                def of_squares(u):
                    pool.wait_ge(e_sq, TPB * (b + 1))
                    pool.tensor_scalar(rms[:, u], rms[:, u], 1.0 / D, None, ALU.mult).then_inc(s_rr, 1)
                    pool.wait_ge(s_rr, 4 * NB + 3 * b + 1)
                    return 1

                rms_roots(4 * NB + 3 * b, b, of_squares)

            norm_roots(0)
            pool.wait_ge(d_cl, 16 * 9)
            pool.wait_ge(d_vw, 1)
            pool.tensor_tensor(WL[:, GW:GW + KD], w_raw[:, GW:GW + KD], WH[:, GW:GW + KD].bitcast(F32),
                               ALU.subtract).then_inc(d_vl, 1)
            pool.tensor_scalar(nsink[:], sink[:], -1.0, None, ALU.mult).then_inc(d_ns, 1)
            low_group(0)
            for r in range(3 * NG):
                kind, n = rope_block(r)
                if r >= NDVE:
                    pool.wait_ge(d_t, 2 * r + 2)
                    pool.wait_ge(d_hi, r - 1)
                    pool.wait_ge(d_lo, r - 1)
                    pool.tensor_tensor(TS[:, r % 2], T1[:, r % 2], T2[:, r % 2], ALU.add).then_inc(d_ts, 1)
                pool.wait_ge(d_hi, r + 1)
                if kind == "q":
                    if n >= 2:
                        pool.wait_ge(d_u[n % 2], 64 * (n // 2))
                    pool.tensor_tensor(QL[:, n % 2], TS[:, r % 2], QH[:, n % 4].bitcast(F32), ALU.subtract)\
                        .then_inc(d_lo, 1)
                else:
                    if n >= 2:
                        pool.wait_ge(d_s, 8 * (n - 1))
                    for q in range(2):
                        rows_ = slice(q * DH, (q + 1) * DH)
                        ins = pool.tensor_tensor(KL[q][rows_, n % 2], TS[rows_, r % 2],
                                                 KHH[rows_, n % 2].bitcast(F32), ALU.subtract)
                    ins.then_inc(d_lo, 1)
                    pool.wait_ge(d_lo, r + 1)
                if kind == "q" and n % 2 and n // 2 + 1 < NG:
                    low_group(n // 2 + 1)
                if r == ROOTS_AT:
                    norm_roots(1)
                if r == 3 * NG - 4:
                    square_roots(0)
                if r in (2, 5):
                    b = r // 3
                    pool.wait_ge(s_xn, NT * 3 + TPB * (b + 1))
                    u = slice(b * TPB, (b + 1) * TPB)
                    pool.tensor_tensor(X1[:, u, :], XN[:, u, :], spread(proj_b[:], 1, TPB), ALU.add)\
                        .then_inc(d_x0, 1)

            square_roots(1)

            def quad(p, first, last):
                for k in range(QUAD * HALVES):
                    n, s, h = p * QUAD * HALVES + k, k // HALVES, k % HALVES
                    pool.wait_ge(e_si, n + 1)
                    if first and k < HALVES:
                        pool.wait_ge(e_z0, HALVES + h + 1)
                    elif h == 0 and s == 0:
                        pool.wait_ge(e_ce[0], 16 * p)
                    elif h == 0:
                        pool.wait_ge(e_ce[s], 16 * (p + 1))
                    if not (first and k < H_RING):
                        pool.wait_ge(e_hl, n + 1 - H_RING)
                    pool.tensor_tensor(HC[:, k % H_RING, :], HA[:, k % H_RING, :], CZ[s][:, h * 512:(h + 1) * 512],
                                       ALU.mult).then_inc(e_c, 1)

            over_pairs(pool, E1 // QUAD, quad)

        @block.tensor
        def _(pe):
            pe.wait_ge(s_id, 16)
            pe.wait_ge(s_w1, SETUP_W)
            pe.wait_ge(s_w0, SETUP_ROWS)
            for b in range(NB):
                pe.transpose(bank[2][0:DC, b * LC:(b + 1) * LC], ctx_rows[:, b, :], ident[0:LC, 0:LC])
            pe.transpose(bank[2][:, 256:256 + NROWS], rows[:], ident[0:NROWS, 0:NROWS]).then_inc(s_p1, 1)
            pe.wait_ge(s_w2, 16 * 3)
            for i, w in enumerate((wq0, qw1, ow1)):
                pe.transpose(bank[3][:, i * D:(i + 1) * D], w[:], ident[:])
            pe.transpose(bank[3][0:DC, 3 * D:4 * D], vw1[:], ident[:]).then_inc(s_p1, 1)
            pe.wait_ge(s_e1, 3)
            pe.wait_ge(s_vw, 1)
            pe.matmul(bank[4][:, 0:NB * LC], wk0[:], ctxT[:], start=True, stop=True).then_inc(s_p2, 1)
            pe.matmul(bank[5][:, 0:NB * LC], WT[0:DC, 3, :], ctxT[:], start=True, stop=True).then_inc(s_p2, 1)
            for b in range(NB):
                cb = ctxT[:, b * LC:(b + 1) * LC]
                pe.matmul(bank[6][0:LC, b * D:(b + 1) * D], cb, wv0[:], start=True, stop=True)
            for b in range(NB):
                cb = ctxT[:, b * LC:(b + 1) * LC]
                mm = pe.matmul(bank[6][0:LC, (2 + b) * D:(3 + b) * D], cb, WT[0:DC, 3, :], start=True, stop=True)
            mm.then_inc(s_p2, 1)
            pe.wait_ge(s_kt, 1)
            pe.matmul(bank[7][:, 0:NB * LC], WT[:, 0, :], KT0[:], start=True, stop=True).then_inc(s_p3, 1)

            def transpose_tokens(ready, before, src, dst, batches=range(NB)):
                for b in batches:
                    for i in range(TPB):
                        u = b * TPB + i
                        pe.wait_ge(ready, NT * before + u + 1)
                        mm = pe.transpose(dst[b][:, i * P:(i + 1) * P], src[:, u, :], ident[:])
                    mm.then_inc(s_xtp, 1)

            transpose_tokens(s_xn, 0, XN, bank)
            pe.wait_ge(s_bq, 1)
            pe.wait_ge(s_e3, 1)
            pe.wait_ge(s_e2, 2)
            for b in range(NB):
                pe.wait_ge(s_xt, b + 1)
                cb = slice(b * LC, (b + 1) * LC)
                for i in range(TPB):
                    o = bank[2 + b][:, i * LC:(i + 1) * LC]
                    u = b * TPB + i
                    pe.matmul(o, BQW[:], KT0[:, cb], start=True, stop=False)
                    mm = pe.matmul(o, XT[:, u * P:(u + 1) * P], KA[:, cb], start=False, stop=True)
                mm.then_inc(sa_s, 1)
            for b in range(NB):
                pe.wait_ge(sa_e, b + 1)
                for i in range(TPB):
                    mm = pe.transpose(bank[4 + b][0:LC, i * P:(i + 1) * P], SA[:, b * TPB + i, :], ident[:])
                mm.then_inc(sa_t, 1)
            for b in range(NB):
                pe.wait_ge(sa_p, b + 1)
                for i in range(TPB):
                    mm = pe.matmul(bank[6 + b][:, i * D:(i + 1) * D], PTA[:, b * TPB + i, :],
                                   VV[:, 0, b, :], start=True, stop=True)
                mm.then_inc(sa_o, 1)

            pe.wait_ge(s_xt, NB)
            transpose_tokens(s_xn, 1, XN, bank)
            pe.wait_ge(s_rl, 64)
            for b in range(NB):
                pe.wait_ge(s_xt, NB + b + 1)
                for i in range(TPB):
                    u = b * TPB + i
                    mm = pe.matmul(bank[6][:, u * E0:(u + 1) * E0], XT[:, u * P:(u + 1) * P], wg0[:],
                                   start=True, stop=True)
            mm.then_inc(b_lg, 1)
            pe.wait_ge(s_xtl, NB)

            def up(e, j, i, first):
                n = e * BLK0 + i
                if i == 0:
                    pe.wait_ge(b_w1l, e + 1)
                if not first:
                    pe.wait_ge(b_si, n + 1 - UP_RING)
                c, h = i // HALVES, i % HALVES
                o = bank[2 + i % UP_RING][:, :]
                wc, tk = slice(c * P, (c + 1) * P), slice(h * 512, (h + 1) * 512)
                pe.matmul(o, W1H[:, j, wc], XTH[:, tk], start=True, stop=False)
                pe.matmul(o, W1H[:, j, wc], XTL[:, tk], start=False, stop=False)
                pe.matmul(o, W1L[:, j, wc], XTH[:, tk], start=False, stop=True).then_inc(b_up, 1)

            def down(e, j, i):
                n = e * BLK0 + i
                if i == 0:
                    pe.wait_ge(b_w2l, e + 1)
                pe.wait_ge(b_hl, n + 1)
                c, h = i // HALVES, i % HALVES
                o, r = bank[6 + h][:, :], i % H_RING
                pe.matmul(o, W2H[:, j, c], HH[:, r, :], start=False, stop=False, skip_group_check=True)
                pe.matmul(o, W2H[:, j, c], HL[:, r, :], start=False, stop=False, skip_group_check=True)
                pe.matmul(o, W2L[:, j, c], HH[:, r, :], start=False, stop=True, skip_group_check=True)\
                    .then_inc(b_dn, 1)

            for i in range(2):
                up(0, 0, i, True)
            pe.wait_ge(b_cm, 1)
            for b in range(NB):
                for i in range(TPB):
                    mm = pe.transpose(bank[b][0:E0, i * P:(i + 1) * P], CM[:, b * TPB + i, :], ident[:])
                mm.then_inc(b_ctp, 1)
            for i in range(2, UP_RING):
                up(0, 0, i, True)
            pe.wait_ge(e_r0, 1)
            for h in range(HALVES):
                pe.wait_ge(b_ct, h + 1)
                pe.matmul(bank[h][:, :], row0[0:E0, :], CT8[:, h * 512:(h + 1) * 512], start=True, stop=True)\
                    .then_inc(e_z0p, 1)
            for h in range(HALVES):
                pe.wait_ge(b_ct, h + 1)
                pe.matmul(bank[6 + h][:, :], b2[:], CT8[:, h * 512:(h + 1) * 512], start=True, stop=False,
                          skip_group_check=True)

            for i in range(UP_RING, LEAD0):
                up(0, 0, i, False)

            def pair0(p, first, last):
                for k in range(2 * BLK0):
                    j, i = k // BLK0, k % BLK0
                    m = k + LEAD0
                    if not (last and m >= 2 * BLK0):
                        up(p * 2 + m // BLK0, m // BLK0 % 2, m % BLK0, False)
                    down(p * 2 + j, j, i)

            over_pairs(pe, NP0, pair0)

            def transpose_back(done, count):
                for b in range(NB):
                    pe.wait_ge(done, count + b + 1)
                    for i in range(TPB):
                        u = b * TPB + i
                        mm = pe.transpose(bank[b][:, i * P:(i + 1) * P], YT[:, u * P:(u + 1) * P], ident[:])
                    mm.then_inc(b_yp, 1)

            transpose_back(b_yt, 0)

            pe.wait_ge(s_xu, 2 * NT)
            transpose_tokens(s_xn, 2, XN, bank)
            for b in range(NB):
                pe.wait_ge(s_xt, 2 * NB + b + 1)
                pe.matmul(bank[5 + b][:, :], WT[:, 1, :], XT[:, b * 512:(b + 1) * 512], start=True, stop=True)\
                    .then_inc(c_q, 1)

            def values_repeated(q, dst):
                b, g = q // 3, q % 3
                for j in range(4 * g, min(4 * g + 4, NCH)):
                    mm = pe.matmul(dst[:, (j - 4 * g) * D:(j - 4 * g + 1) * D], repeat_ctx[:, j * P:(j + 1) * P],
                                   VV[:, 1, b, :], start=True, stop=True)
                mm.then_inc(c_vp, 1)

            for q in range(3):
                if q == 2:
                    pe.wait_ge(c_vb, NB + 1)
                values_repeated(q, bank[q % 2])

            def scores(u):
                b = u // TPB
                pe.wait_ge(c_ql, b + 1)
                pe.wait_ge(c_vt, 2 * (b + 1))
                tk = slice(u * P, (u + 1) * P)
                for g, (h0, n) in enumerate(GROUPS):
                    if u:
                        pe.wait_ge(c_c, 3 * (u - 1) + g + 1)
                    o, hk = bank[2 + g][:, 0:n * LC], slice(h0 * LC, (h0 + n) * LC)
                    pe.matmul(o, XTH[:, tk], VTH[:, b, hk], start=True, stop=False)
                    pe.matmul(o, XTH[:, tk], VTL[:, b, hk], start=False, stop=False)
                    pe.matmul(o, XTL[:, tk], VTH[:, b, hk], start=False, stop=True).then_inc(c_s, 1)

            def chunk_rows(j):
                return min(P, HK - j * P)

            def probs_transposed(u):
                pe.wait_ge(c_e, u + 1)
                for g in range(3):
                    if u:
                        pe.wait_ge(c_p, 3 * (u - 1) + g + 1)
                    for j in range(4 * g, min(4 * g + 4, NCH)):
                        mm = pe.transpose(bank[5 + g][0:chunk_rows(j), (j - 4 * g) * P:(j - 4 * g + 1) * P],
                                          SCS[u % 3][:, j * P:j * P + chunk_rows(j)], ident[:])
                    mm.then_inc(c_tp, 1)

            def attend(u):
                pe.wait_ge(c_p, 3 * (u + 1))
                pe.wait_ge(c_vb, NB + 3 * (u // TPB + 1))
                if u:
                    pe.wait_ge(c_n, u)
                for j in range(NCH):
                    mm = pe.matmul(bank[0][:, 0:DEN], PTC[0:chunk_rows(j), j, :],
                                   VBD[0:chunk_rows(j), u // TPB, j, :], start=(j == 0), stop=(j == NCH - 1))
                mm.then_inc(c_o, 1)

            def rows_transposed(b):
                pe.wait_ge(c_n, TPB * (b + 1))
                if b:
                    pe.wait_ge(s_xu, 2 * NT + TPB * b)
                for h in range(H1):
                    mm = pe.transpose(bank[1][:, h * AA:(h + 1) * AA], OA[:, b, h].rearrange("a s d -> a (s d)"),
                                      ident[0:AA, 0:AA])
                mm.then_inc(c_otp, 1)

            def project(b):
                pe.wait_ge(c_ot, b + 1)
                for i in range(TPB):
                    mm = pe.matmul(bank[1][:, i * P:(i + 1) * P], OT[:, b, i * P:(i + 1) * P], WT[:, 2, :],
                                   start=True, stop=True)
                mm.then_inc(c_y, 1)

            scores(0)
            scores(1)
            for u in range(NT):
                if u and u % TPB == 0:
                    rows_transposed(u // TPB - 1)
                probs_transposed(u)
                if u + 2 < NT:
                    scores(u + 2)
                if u and u % TPB == 0:
                    project(u // TPB - 1)
                attend(u)
                if u < 3:
                    pe.wait_ge(c_vb, NB + 3 + u)
                    values_repeated(3 + u, bank[1])
            pe.wait_ge(c_n, NT)
            transpose_tokens(s_xr, 0, XR, bank, [0])
            rows_transposed(NB - 1)


            def values(u):
                o, tk = V_BANK[u // 2][:, u % 2 * KD:(u % 2 + 1) * KD], slice(u * P, (u + 1) * P)
                pe.matmul(o, XTH[:, tk], WH[:, GW:GW + KD], start=True, stop=False)
                pe.matmul(o, XTL[:, tk], WH[:, GW:GW + KD], start=False, stop=False)
                mm = pe.matmul(o, XTH[:, tk], WL[:, GW:GW + KD], start=False, stop=True)
                if u % 2:
                    mm.then_inc(d_vp, 1)

            def rope_products(r, outT):
                kind, n = rope_block(r)
                G = n if kind == "k" else n // 2
                b = G // KV
                tk = slice(b * 512, (b + 1) * 512)
                pe.wait_ge(d_wl, G + 1)
                if r >= 2 and r != 3:
                    pe.wait_ge(d_t, 2 * r - 3)
                if outT and r % 2 == 0:
                    pe.wait_ge(d_yc, outT)
                w0 = 2 * P if kind == "k" else n % 2 * P
                wc, o = slice(w0, w0 + P), rope_bank(r)[:, :]
                pe.matmul(o, WH[:, wc], XTH[:, tk], start=True, stop=False)
                pe.matmul(o, WH[:, wc], XTL[:, tk], start=False, stop=False)
                pe.matmul(o, WL[:, wc], XTH[:, tk], start=False, stop=True).then_inc(d_qp, 1)

            def scores_d(q):
                n, i = q // TPB, q % TPB
                G = n // 2
                if i == 0:
                    pe.wait_ge(d_u[n % 2], 64 * (n // 2 + 1))
                    pe.wait_ge(d_lo, BLOCK_OF["k", G] + 1)
                    if q == 0:
                        pe.wait_ge(d_kz, 1)
                if q < 2:
                    pe.wait_ge(d_v, q + 1)
                else:
                    pe.wait_ge(d_m, q - 1)
                k0 = max(i - 1, 0)
                keys, tk = slice(k0 * P, (i + 1) * P), slice(i * P, (i + 1) * P)
                for hd in range(2):
                    o = bank[2 + q % 2][:, hd * 256 + (128 if i == 0 else 0):(hd + 1) * 256]
                    pe.matmul(o, UQ[n % 4][:, hd, tk], KHH[:, G % 2, keys], start=True, stop=False)
                    mm = pe.matmul(o, QH[:, n % 4, tk], KL[hd][:, G % 2, keys], start=False, stop=True)
                mm.then_inc(d_s, 1)

            def probs_transposed_d(q):
                pe.wait_ge(d_e, q + 1)
                if q >= 2:
                    pe.wait_ge(d_pt, q - 1)
                elif q == 0:
                    pe.wait_ge(d_t, 4)
                for hd in range(2):
                    for kb in range(2):
                        if q % TPB or kb:
                            at = slice((2 * hd + kb) * P, (2 * hd + kb + 1) * P)
                            mm = pe.transpose(bank[4 + q % 2][:, at], SM[:, q % 4, at], ident[:])
                mm.then_inc(d_tp, 1)

            def attend_d(q):
                n, i = q // TPB, q % TPB
                b, g = n // PAIRS, n % PAIRS // 2
                pe.wait_ge(d_pt, q + 1)
                if i == 0 and n:
                    pe.wait_ge(d_ys, n)
                for hd in range(2):
                    o = bank[6][:, i * P + hd * DH:i * P + (hd + 1) * DH]
                    for kb in range(2):
                        if i or kb:
                            mm = pe.matmul(o, PT[:, q % 2, (2 * hd + kb) * P:(2 * hd + kb + 1) * P],
                                           VS[:, b * TPB + i - 1 + kb, g * DH:(g + 1) * DH],
                                           start=(kb == 0 or i == 0), stop=(kb == 1))
                mm.then_inc(d_y, 1)

            LOGITS = (bank[1], bank[5])

            def logits(b):
                pe.wait_ge(e_cl, 48)
                pe.wait_ge(s_xt, 4 * NB + b + 1)
                if b == 0:
                    pe.wait_ge(s_xtl, 2 * NB + 1)
                for u in range(b * TPB, (b + 1) * TPB):
                    mm = pe.matmul(LOGITS[b][:, u * E1:(u + 1) * E1], XT[:, u * P:(u + 1) * P], gate_w[:],
                                   start=True, stop=True)
                mm.then_inc(e_lg, 1)

            def weights_transposed(b, dst):
                pe.wait_ge(e_r, 10 * (b + 1))
                for i in range(TPB):
                    mm = pe.transpose(dst[0:E1, i * P:(i + 1) * P], GZ[:, b * TPB + i, :], ident[:])
                mm.then_inc(e_ctp, 1)

            def out_transposed(m, ropes):
                pe.wait_ge(d_ys, m + 1)
                pe.wait_ge(d_t, 2 * ((ropes - 1) // 2 * 2) + 1)
                if m:
                    pe.wait_ge(d_yc, m)
                for i in range(TPB):
                    mm = pe.transpose(bank[0][:, i * P:(i + 1) * P], YS[:, m % 2, i * P:(i + 1) * P], ident[:])
                mm.then_inc(d_yt, 1)

            def project_d(m):
                b, c = m // PAIRS, m % PAIRS
                pe.wait_ge(d_yc, m + 1)
                if m == 0:
                    pe.wait_ge(d_v, 4)
                if b and c == 0:
                    pe.wait_ge(d_x1, b)
                for i in range(TPB):
                    mm = pe.matmul(bank[7][:, i * P:(i + 1) * P], YTC[:, m % 2, i * P:(i + 1) * P], proj_w[:, c, :],
                                   start=(c == 0 and i == 0), stop=(c == PAIRS - 1), skip_group_check=True)
                mm.then_inc(d_pr, 1)

            pe.wait_ge(s_xtl, NB + 1)
            rope_products(0, 0)
            rope_products(1, 0)
            project(NB - 1)
            pe.wait_ge(d_vl, 1)
            for u in range(TPB):
                values(u)
            rope_products(2, 0)
            pe.wait_ge(s_xu, 3 * NT)
            ropes = 3
            for q in range(NQ + 2 * TPB):
                if q < NQ:
                    scores_d(q)
                if q == 3:
                    transpose_tokens(s_xr, 0, XR, (None, bank[7]), [1])
                if q == 7:
                    pe.wait_ge(s_xtl, 2 * NB)
                if q == 9:
                    pe.wait_ge(d_v, 3)
                if q in (7, 9):
                    values(q - 3)
                    values(q - 2)
                if q in ROPE_AT:
                    rope_products(ropes, max(0, (q - 6) // 4))
                    ropes += 1
                if T_LAG <= q < NQ + T_LAG:
                    probs_transposed_d(q - T_LAG)
                if T_LAG < q <= NQ + T_LAG:
                    attend_d(q - T_LAG - 1)
                if q == NQ - 8:
                    pe.wait_ge(d_t, 2 * 3 * NG - 1)
                    transpose_tokens(s_xr, 1, XR, (bank[1], None), [0])
                if q == NQ - 4:
                    logits(0)
                if q == NQ + 6:
                    weights_transposed(0, bank[1])
                m, k = (q - 5) // 4 - 1, (q - 5) % 4
                if 0 <= m < NU and k == 0:
                    out_transposed(m, ropes)
                if 0 <= m < NU and k == 2:
                    project_d(m)

            pe.wait_ge(d_x1, NB)
            transpose_tokens(s_xr, 1, XR, (None, bank[0]), [1])
            logits(1)
            pe.wait_ge(s_xtl, 3 * NB)

            def three_passes(o, wh, wl, xh, xl, start):
                pe.matmul(o, wh, xh, start=start, stop=False, skip_group_check=not start)
                pe.matmul(o, wh, xl, start=False, stop=False, skip_group_check=not start)
                return pe.matmul(o, wl, xh, start=False, stop=True, skip_group_check=not start)

            def gate_block(e, n, k, first):
                s, tk = k // HALVES % QUAD, slice(k % HALVES * 512, (k % HALVES + 1) * 512)
                if k % HALVES == 0:
                    pe.wait_ge(e_ul, e + 1)
                if not first:
                    pe.wait_ge(e_si, n - 3)
                three_passes(bank[k % 4][:, :], ZU[1][:, s, P:2 * P], ZU[2][:, s, P:2 * P], XTH[:, tk], XTL[:, tk],
                             True).then_inc(e_g, 1)

            def up_block(n, k, first):
                s, tk = k // HALVES % QUAD, slice(k % HALVES * 512, (k % HALVES + 1) * 512)
                if not first:
                    pe.wait_ge(e_mu, n - 1)
                three_passes(bank[4 + k % 2][:, :], ZU[1][:, s, 0:P], ZU[2][:, s, 0:P], XTH[:, tk], XTL[:, tk],
                             True).then_inc(e_u, 1)

            def down_block(e, n, k):
                s, r = k // HALVES, k % H_RING
                if k % HALVES == 0:
                    pe.wait_ge(e_wl, e + 1)
                pe.wait_ge(e_hl, n + 1)
                three_passes(bank[6 + k % HALVES][:, :], ZD[1][:, s, :], ZD[2][:, s, :], HH[:, r, :], HL[:, r, :],
                             False).then_inc(e_dn, 1)

            gate_block(0, 0, 0, True)
            up_block(0, 0, True)
            pe.wait_ge(e_ct, 1)
            gate_block(0, 1, 1, True)
            gate_block(1, 2, 2, True)
            pe.wait_ge(e_r, 11)
            up_block(1, 1, True)
            weights_transposed(1, bank[3])
            pe.wait_ge(e_r0, 1)
            for h in range(HALVES):
                pe.wait_ge(e_ct, h + 1)
                pe.matmul(bank[7 - 4 * h][:, :], row0[:], CT1[:, h * 512:(h + 1) * 512], start=True, stop=True)\
                    .then_inc(e_z0p, 1)
            pe.wait_ge(e_z0, 2 * HALVES)
            for u in range(NT):
                pe.matmul(bank[6 + u // TPB][:, u % TPB * P:(u % TPB + 1) * P], X1[:, u, :], ident[:],
                          start=(u % TPB == 0), stop=False, skip_group_check=True)

            def quad(p, first, last):
                for k in range(QUAD * HALVES):
                    n = p * QUAD * HALVES + k
                    if not (last and k + 2 >= QUAD * HALVES):
                        up_block(n + 2, k + 2, False)
                    if not (last and k + 3 >= QUAD * HALVES):
                        gate_block(p * QUAD + (k + 3) // HALVES, n + 3, k + 3, first and k + 3 < 4)
                    down_block(p * QUAD + k // HALVES, n, k)

            over_pairs(pe, E1 // QUAD, quad)
            transpose_back(b_yt, NB)

        @block.scalar
        def _(act):
            act.dma_start(ctx_rows[:], t["ctx_768"].rearrange("b c d -> c b d")).then_inc(s_w1, 16)
            for dst, name in ((wk0, "L0_xattn_Wk"), (wq0, "L0_xattn_Wq"), (wv0, "L0_xattn_Wv")):
                act.dma_start(dst[:], t[name]).then_inc(s_w1, 16)
            act.wait_ge(s_p1, 1)
            act.copy(ctxT[:], bank[2][0:DC, 0:NB * LC]).then_inc(s_e1, 1)
            act.copy(cols[:], bank[2][:, 256:256 + NROWS]).then_inc(s_e1, 1)
            act.wait_ge(s_p1, 2)
            act.copy(WT[:, 0:3, :], bank[3][:, 0:3 * D]).then_inc(s_e1, 1)
            act.wait_ge(s_p2, 1)
            act.wait_ge(s_e1, 3)
            act.activation(KT0[:], bank[4][:, 0:NB * LC], ACT.Identity, bias=cols[:, BK:BK + 1]).then_inc(s_kt, 1)
            act.wait_ge(s_p3, 1)
            act.copy(KA[:], bank[7][:, 0:NB * LC]).then_inc(s_e3, 1)
            for b in range(NB):
                act.wait_ge(s_xtp, b + 1)
                act.copy(XT[:, b * 512:(b + 1) * 512], bank[b][:, :]).then_inc(s_xt, 1)
            act.wait_ge(s_b0, SETUP_B)
            act.activation(gate[:], gate_in[:], ACT.Tanh).then_inc(s_g, 1)
            for b in range(NB):
                act.wait_ge(sa_c, b + 1)
                sc = SA[:, b * TPB:(b + 1) * TPB, :]
                act.activation(sc, sc, ACT.Exp, scale=float(D) ** -0.5).then_inc(sa_e, 1)
            for b in range(NB):
                act.wait_ge(sa_t, b + 1)
                act.copy(PTA[:, b * TPB:(b + 1) * TPB, :], bank[4 + b][0:LC, :]).then_inc(sa_p, 1)


            def split_tokens(kth, scale, batches=range(NB), src=bank):
                for b in batches:
                    act.wait_ge(s_xtp, NB * kth + b + 1)
                    tk = slice(b * 512, (b + 1) * 512)
                    act.activation(XTH[:, tk], src[b][:, :], ACT.Copy, scale=scale).then_inc(s_xth, 1)
                    act.activation(XT[:, tk], src[b][:, :], ACT.Copy, scale=scale).then_inc(s_xt, 1)

            def high1(e, j, first, p):
                act.wait_ge(b_w1[j], 16 * (p + 1))
                if not first:
                    act.wait_ge(b_up, (e - 1) * BLK0)
                act.copy(W1H[:, j, :], W1[:, j, :]).then_inc(b_w1h, 1)

            def high2(e, j, first, p):
                act.wait_ge(b_w2[j], 16 * (p + 1))
                if not first:
                    act.wait_ge(b_dn, (e - 1) * BLK0)
                act.copy(W2H[:, j], W2[:, j]).then_inc(b_w2h, 1)

            high1(0, 0, True, 0)
            high2(0, 0, True, 0)
            split_tokens(1, 1.0)
            act.wait_ge(b_d, 3)
            act.activation(GL[:], GL[:], ACT.Exp).then_inc(b_ex, 1)
            for h in range(HALVES):
                act.wait_ge(e_z0p, h + 1)
                act.copy(CE[:, 0, h * 512:(h + 1) * 512], bank[h][:, :]).then_inc(e_z0, 1)

            HI_LAG = 2

            def high(e, i, k, first):
                n = e * BLK0 + i
                if i in POOL0:
                    act.wait_ge(b_mp, e * len(POOL0) + POOL0.index(i) + 1)
                else:
                    act.wait_ge(b_mv, e * len(VEC0) + VEC0.index(i) + 1)
                if not first:
                    act.wait_ge(b_dn, n + 1 - H_RING)
                act.copy(HH[:, i % H_RING, :], HC[:, i % H_RING, :]).then_inc(b_hh, 1)

            def pair0(p, first, last):
                for k in range(2 * BLK0):
                    j, i = k // BLK0, k % BLK0
                    e = p * 2 + j
                    n = e * BLK0 + i
                    act.wait_ge(b_up, n + 1)
                    if not (first and k < H_RING):
                        act.wait_ge(b_hl, n + 1 - H_RING)
                    if i == 0:
                        act.wait_ge(b_b1[j], 16 * (p + 1))
                    act.activation(HA[:, i % H_RING, :], bank[2 + i % UP_RING][:, :], ACT.Silu,
                                   bias=b1[:, j, i // HALVES:i // HALVES + 1]).then_inc(b_si, 1)
                    if not (last and j == 1):
                        if i == 0:
                            high1(e + 1, 1 - j, first and j == 0, p + j)
                        if i == BLK0 - 2:
                            high2(e + 1, 1 - j, first and j == 0, p + j)
                    if k >= HI_LAG or not first:
                        m = k - HI_LAG
                        high(p * 2 + m // BLK0, m % BLK0, m, first and m < H_RING)
                if last:
                    for m in range(2 * BLK0 - HI_LAG, 2 * BLK0):
                        high(p * 2 + m // BLK0, m % BLK0, m, False)

            over_pairs(act, NP0, pair0)
            for h in range(HALVES):
                act.wait_ge(b_dn, E0 * BLK0 - HALVES + h + 1)
                act.copy(YT[:, h * 512:(h + 1) * 512], bank[6 + h][:, :]).then_inc(b_yt, 1)

            for b in range(NB):
                act.wait_ge(s_xtp, 2 * NB + b + 1)
                act.copy(XT[:, b * 512:(b + 1) * 512], bank[b][:, :]).then_inc(s_xt, 1)
            for b in range(NB):
                tk = slice(b * 512, (b + 1) * 512)
                act.wait_ge(c_q, b + 1)
                by_s = bank[5 + b][:, :].rearrange("p (a s) -> p s a", s=STR)
                for dst, done in ((XTH, c_qh), (YT, c_qt)):
                    act.activation(dst[:, tk].rearrange("p (s a) -> p s a", s=STR), by_s, ACT.Identity,
                                   bias=cols[:, QB:QB + 1]).then_inc(done, 1)

            def exp_c(u):
                act.wait_ge(c_c, 3 * (u + 1))
                act.activation(SCS[u % 3][:, :], SCS[u % 3][:, :], ACT.Exp, scale=float(DH1) ** -0.5).then_inc(c_e, 1)

            def out_c(b):
                act.wait_ge(c_otp, b + 1)
                act.copy(OT[:, b, :], bank[1][:, :]).then_inc(c_ot, 1)

            def high_group(G):
                act.wait_ge(d_wg, 16 * (G + 1))
                if G:
                    act.wait_ge(d_qp, 3 * G)
                act.copy(WH[:, 0:GW], w_raw[:, 0:GW]).then_inc(d_wh, 1)

            exp_c(0)
            for u in range(NT):
                if u and u % TPB == 0:
                    out_c(u // TPB - 1)
                if u == NT - 2:
                    act.wait_ge(d_cl, 16 * 9)
                    act.copy(WH[:, GW:GW + KD], w_raw[:, GW:GW + KD]).then_inc(d_vw, 1)
                    high_group(0)
                for g in range(3):
                    act.wait_ge(c_tp, 3 * u + g + 1)
                    if u and g == 0:
                        act.wait_ge(c_o, u)
                    nj = min(4, NCH - 4 * g)
                    act.copy(PTC[:, 4 * g:4 * g + nj, :], bank[5 + g][:, 0:nj * P]).then_inc(c_p, 1)
                if u + 1 < NT:
                    exp_c(u + 1)
            split_tokens(3, cols[:, ATTN_W:ATTN_W + 1], [0])
            out_c(NB - 1)


            def high_qk(r):
                kind, n = rope_block(r)
                wait_rope_sum(act, r)
                if kind == "q":
                    if n >= 4:
                        act.wait_ge(d_s, TPB * (n - 3))
                        act.wait_ge(d_u[n % 2], 64 * ((n - 4) // 2 + 1))
                    act.copy(QH[:, n % 4], TS[:, r % 2]).then_inc(d_hi, 1)
                else:
                    if n >= 2:
                        act.wait_ge(d_s, 8 * (n - 1))
                    act.copy(KHH[:, n % 2], TS[:, r % 2]).then_inc(d_hi, 1)
                if kind == "q" and n % 2 and n // 2 + 1 < NG:
                    high_group(n // 2 + 1)

            for r in range(3):
                high_qk(r)
            highs = 3

            def squares(b):
                act.wait_ge(d_x1, b + 1)
                for i in range(TPB):
                    u = b * TPB + i
                    act.activation(XR[:, u, :], X1[:, u, :], ACT.Square, accum_out=rms[:, u:u + 1]).then_inc(e_sq, 1)

            def high_up(s, p):
                act.wait_ge(e_wu[s], LOADS0[s] + 16 * (p + 1))
                act.copy(ZU[1][:, s, :], ZU[0][:, s, :]).then_inc(e_uh, 1)

            def router_exp(b):
                act.wait_ge(e_r, 10 * b + 2)
                w = wt[:, b * TPB:(b + 1) * TPB, :]
                act.activation(w, w, ACT.Exp).then_inc(e_ex, 1)

            for q in range(NQ + 2 * TPB):
                if T_LAG <= q < NQ + T_LAG:
                    y = q - T_LAG
                    act.wait_ge(d_tp, y + 1)
                    if y >= 2:
                        act.wait_ge(d_y, y - 1)
                    h = slice(0, 2) if y % TPB else slice(1, 2)
                    act.copy(PT[:, y % 2].rearrange("p (h k j) -> p h k j", h=2, k=2)[:, :, h, :],
                             bank[4 + y % 2][:, :].rearrange("p (h k j) -> p h k j", h=2, k=2)[:, :, h, :])\
                       .then_inc(d_pt, 1)
                if q < NQ:
                    n, i = q // TPB, q % TPB
                    act.wait_ge(d_nm, q + 1)
                    if n >= 2 and i == 0:
                        act.wait_ge(d_dn, n - 1)
                    for hd in range(2):
                        pr = SM[:, q % 4, hd * 256 + (128 if i == 0 else 0):(hd + 1) * 256]
                        ins = act.activation(pr, pr, ACT.Exp, bias=nm[:, n % 2, i, hd:hd + 1], scale=DH ** -0.5,
                                             accum_out=lD[:, n % 2, i, hd:hd + 1])
                    ins.then_inc(d_e, 1)
                if q == 4:
                    split_tokens(3, cols[:, ATTN_W:ATTN_W + 1], [1], (None, bank[7]))
                if q == SQ_AT:
                    squares(0)
                if q == NQ - 7:
                    split_tokens(4, cols[:, FFN_W:FFN_W + 1], [0], (bank[1], None))
                if q == NQ:
                    router_exp(0)
                if NQ + 1 <= q < NQ + 4:
                    if q == NQ + 1:
                        act.wait_ge(d_qp, 3 * NG)
                        act.wait_ge(d_vp, NT // 2)
                    high_up(q - NQ - 1, 0)
                m, k = q // 4 - 1, q % 4
                if k == 0 and 0 <= m < NU:
                    act.wait_ge(d_zs, m + 1)
                    act.activation(den[:, m % 2], zs[:, m % 2], ACT.Exp).then_inc(d_es, 1)
                m, k = (q - 6) // 4 - 1, (q - 6) % 4
                if k == 0 and 0 <= m < NU:
                    act.wait_ge(d_yt, m + 1)
                    if m >= 2:
                        act.wait_ge(d_pr, m - 1)
                    act.copy(YTC[:, m % 2], bank[0][:, :]).then_inc(d_yc, 1)
                if q - 1 in ROPE_AT:
                    high_qk(highs)
                    highs += 1

            squares(1)

            def high_down(s, p):
                act.wait_ge(e_wd[s], LOADS1[s] + 16 * (p + 1))
                act.copy(ZD[1][:, s, :], ZD[0][:, s, :]).then_inc(e_wh, 1)

            split_tokens(4, cols[:, FFN_W:FFN_W + 1], [1], (None, bank[0]))
            for s in range(2):
                high_down(s, 0)
            router_exp(1)
            for h in range(HALVES):
                act.wait_ge(e_z0p, HALVES + h + 1)
                act.copy(CZ[0][:, h * 512:(h + 1) * 512], bank[7 - 4 * h][:, :]).then_inc(e_z0, 1)

            def high_e(n, k, first):
                act.wait_ge(e_mu, n + 1)
                if not first:
                    act.wait_ge(e_dn, n + 1 - H_RING)
                act.copy(HH[:, k % H_RING, :], HC[:, k % H_RING, :]).then_inc(e_hh, 1)

            HI1 = 2

            def quad(p, first, last):
                for k in range(QUAD * HALVES):
                    n, s, h = p * QUAD * HALVES + k, k // HALVES, k % HALVES
                    if not first or k >= HI1:
                        high_e(n - HI1, (k - HI1) % H_RING, first and k - HI1 < H_RING)
                    act.wait_ge(e_g, n + 1)
                    if not (first and k < H_RING):
                        act.wait_ge(e_c, n + 1 - H_RING)
                    act.activation(HA[:, k % H_RING, :], bank[k % 4][:, :], ACT.Silu).then_inc(e_si, 1)
                    if h == 0 and not (last and s >= 1):
                        if not (first and s < 1):
                            act.wait_ge(e_u, n)
                        high_up((s + 3) % QUAD, p + (s + 3) // QUAD)
                    if h == 0 and not (last and s >= 2):
                        if not (first and s < 2):
                            act.wait_ge(e_dn, n - HALVES)
                        high_down((s + 2) % QUAD, p + (s + 2) // QUAD)
                if last:
                    for k in range(QUAD * HALVES - HI1, QUAD * HALVES):
                        high_e(p * QUAD * HALVES + k, k, False)

            over_pairs(act, E1 // QUAD, quad)
            for h in range(HALVES):
                act.wait_ge(e_dn, NB1 - HALVES + h + 1)
                act.copy(YT[:, h * 512:(h + 1) * 512], bank[6 + h][:, :]).then_inc(b_yt, 1)

        @block.vector
        def _(dve):
            def row_means(stage, b):
                for i in range(TPB):
                    u = b * TPB + i
                    if stage:
                        dve.wait_ge(s_xu, NT * (stage - 1) + u + 1)
                    dve.bn_stats(stats[:, u, :], X[:, u, :]).then_inc(s_st, 1)
                for i in range(TPB):
                    u = b * TPB + i
                    dve.wait_ge(s_st, NT * stage + u + 1)
                    dve.bn_aggr(mv[:, u, :], stats[:, u, :]).then_inc(s_mv, 1)

            def normalise(stage, b):
                dve.wait_ge(s_rs, NB * stage + b + 1)
                for i in range(TPB):
                    u = b * TPB + i
                    dve.tensor_scalar(XN[:, u, :], X[:, u, :], mv[:, u, 0:1], rstd[:, u:u + 1],
                                      ALU.subtract, ALU.mult).then_inc(s_xn, 1)

            for b in range(NB):
                dve.wait_ge(s_x[b], 16)
                row_means(0, b)
            for b in range(NB):
                normalise(0, b)
            dve.wait_ge(s_id, 16)
            dve.tensor_copy(row0[:], ident[0:E1, 0:1].broadcast_to([E1, P])).then_inc(e_r0, 1)
            dve.wait_ge(s_e1, 3)
            dve.tensor_copy(WT[0:DC, 3, :], bank[3][0:DC, 3 * D:4 * D]).then_inc(s_vw, 1)
            dve.tensor_copy(BQW[:], cols[:, BQ:BQ + 1].broadcast_to([P, P])).then_inc(s_bq, 1)
            dve.wait_ge(s_p2, 2)
            dve.tensor_scalar(V1T[:], bank[5][:, 0:NB * LC], cols[:, VB:VB + 1], None, ALU.add).then_inc(s_e2, 1)
            dve.wait_ge(s_p2, 3)
            dve.wait_ge(s_b0, SETUP_B)
            dve.tensor_tensor(VV[:].rearrange("k l b d -> k (l b d)"), bank[6][0:LC, :],
                              bias_v[:].rearrange("k l d -> k (l d)"), ALU.add).then_inc(s_e2, 1)

            dve.wait_ge(s_e2, 1)
            dve.tensor_copy(V1TH[:], V1T[:]).then_inc(c_vh, 1)
            dve.wait_ge(c_vh, 1)
            dve.tensor_tensor(V1TL[:], V1T[:], V1TH[:].bitcast(F32), ALU.subtract).then_inc(c_vh, 1)

            for b in range(NB):
                u = slice(b * TPB, (b + 1) * TPB)
                sc = bank[2 + b][:, 0:TPB * LC].rearrange("p (i k) -> p i k", k=LC)
                dve.wait_ge(sa_s, b + 1)
                dve.tensor_reduce(mA[:, u], sc, AX.X, ALU.max).then_inc(sa_m, 1)
                dve.wait_ge(sa_m, b + 1)
                dve.tensor_tensor(SA[:, u, :], sc, spread(mA[:, u], 2, LC), ALU.subtract).then_inc(sa_c, 1)
            for b in range(NB):
                u = slice(b * TPB, (b + 1) * TPB)
                dve.wait_ge(sa_e, b + 1)
                dve.tensor_reduce(lA[:, u], SA[:, u, :], AX.X, ALU.add).then_inc(sa_l, 1)
                dve.wait_ge(sa_l, b + 1)
                dve.reciprocal(rA[:, u], lA[:, u]).then_inc(sa_r, 1)
                dve.wait_ge(sa_r, b + 1)
                dve.wait_ge(s_g, 1)
                dve.tensor_scalar(rA[:, u], rA[:, u], gate[:, 0:1], None, ALU.mult).then_inc(sa_g, 1)
            for b in range(NB):
                dve.wait_ge(sa_o, b + 1)
                dve.wait_ge(sa_g, b + 1)
                for i in range(TPB):
                    u = b * TPB + i
                    dve.scalar_tensor_tensor(X[:, u, :], bank[6 + b][:, i * D:(i + 1) * D], rA[:, u:u + 1],
                                             X[:, u, :], ALU.mult, ALU.add).then_inc(s_xu, 1)


            def low_tokens(kth, batches=range(NB)):
                for b in batches:
                    dve.wait_ge(s_xt, NB * kth + b + 1)
                    tk = slice(b * 512, (b + 1) * 512)
                    dve.tensor_tensor(XTL[:, tk], XT[:, tk], XTH[:, tk].bitcast(F32), ALU.subtract).then_inc(s_xtl, 1)

            for b in range(NB):
                row_means(1, b)
            for b in range(NB):
                normalise(1, b)
            low_tokens(1)
            dve.wait_ge(b_lg, 1)
            dve.tensor_tensor(GL[:], bank[6][:, 0:NT * E0].rearrange("p (u e) -> p u e", e=E0),
                              spread(bg0[:], 1, NT), ALU.add).then_inc(b_d, 1)
            dve.wait_ge(b_d, 1)
            dve.tensor_reduce(gm[:], GL[:], AX.X, ALU.max).then_inc(b_d, 1)
            dve.wait_ge(b_d, 2)
            dve.tensor_tensor(GL[:], GL[:], spread(gm[:], 2, E0), ALU.subtract).then_inc(b_d, 1)
            dve.wait_ge(b_ex, 1)
            dve.tensor_reduce(gs[:], GL[:], AX.X, ALU.add).then_inc(b_d, 1)
            dve.wait_ge(b_d, 4)
            dve.reciprocal(gs[:], gs[:]).then_inc(b_d, 1)
            dve.wait_ge(b_d, 5)
            dve.tensor_tensor(GL[:], GL[:], spread(gs[:], 2, E0), ALU.mult).then_inc(b_d, 1)
            dve.wait_ge(b_d, 6)
            dve.tensor_reduce(gm[:], GL[:], AX.X, ALU.max).then_inc(b_d, 1)
            dve.wait_ge(b_d, 7)
            dve.tensor_tensor(EQ[:], GL[:], spread(gm[:], 2, E0), ALU.is_equal).then_inc(b_d, 1)
            dve.wait_ge(b_d, 8)
            dve.tensor_tensor(EQ[:], EQ[:], spread(rev0[:], 1, NT), ALU.mult).then_inc(b_d, 1)
            dve.wait_ge(b_d, 9)
            dve.tensor_reduce(gm[:], EQ[:], AX.X, ALU.max).then_inc(b_d, 1)
            dve.wait_ge(b_d, 10)
            dve.tensor_tensor(EQ[:], EQ[:], spread(gm[:], 2, E0), ALU.is_equal).then_inc(b_d, 1)
            dve.wait_ge(b_d, 11)
            dve.tensor_tensor(CM[:], EQ[:], GL[:], ALU.mult).then_inc(b_cm, 1)

            for b in range(NB):
                dve.wait_ge(b_ctp, b + 1)
                dve.tensor_copy(CT8[:, b * 512:(b + 1) * 512], bank[b][0:E0, :]).then_inc(b_ct, 1)

            dve.wait_ge(s_cc, 64)
            for b in range(NB):
                dve.tensor_copy(VBD[:, b, :, D:DEN], own_head[:, :, D:DEN]).then_inc(c_vb, 1)

            LO_LAG = 2

            def low(e, i, first):
                n = e * BLK0 + i
                dve.wait_ge(b_hh, n + 1)
                if not first:
                    dve.wait_ge(b_dn, n + 1 - H_RING)
                r = i % H_RING
                dve.tensor_tensor(HL[:, r, :], HC[:, r, :], HH[:, r, :].bitcast(F32), ALU.subtract).then_inc(b_hl, 1)

            def pair0(p, first, last):
                for k in range(2 * BLK0):
                    j, i = k // BLK0, k % BLK0
                    n = (p * 2 + j) * BLK0 + i
                    if i in VEC0:
                        dve.wait_ge(b_si, n + 1)
                        wait_weights0(dve, p, j, i, first)
                        if not (first and k < H_RING):
                            dve.wait_ge(b_hl, n + 1 - H_RING)
                        dve.tensor_tensor(HC[:, i % H_RING, :], HA[:, i % H_RING, :],
                                          CE[:, j, (i % HALVES) * 512:(i % HALVES + 1) * 512], ALU.mult)\
                            .then_inc(b_mv, 1)
                    if k >= LO_LAG or not first:
                        m = k - LO_LAG
                        low(p * 2 + m // BLK0, m % BLK0, first and m < H_RING)
                if last:
                    for m in range(2 * BLK0 - LO_LAG, 2 * BLK0):
                        low(p * 2 + m // BLK0, m % BLK0, False)

            over_pairs(dve, NP0, pair0)

            def add_back(kth, g, batches=range(NB)):
                for b in batches:
                    dve.wait_ge(b_yp, NB * kth + b + 1)
                    for i in range(TPB):
                        u = b * TPB + i
                        dve.scalar_tensor_tensor(X[:, u, :], bank[b][:, i * P:(i + 1) * P], gate[:, g:g + 1],
                                                 X[:, u, :], ALU.mult, ALU.add).then_inc(s_xu, 1)

            for b in range(NB):
                add_back(0, 2, [b])
                row_means(2, b)

            for b in range(NB):
                normalise(2, b)
            for b in range(NB):
                tk = slice(b * 512, (b + 1) * 512)
                dve.wait_ge(c_qt, b + 1)
                dve.tensor_tensor(XTL[:, tk], YT[:, tk], XTH[:, tk].bitcast(F32), ALU.subtract).then_inc(c_ql, 1)

            def values_own(q, src):
                b, g = q // 3, q % 3
                n = min(4, NCH - 4 * g)
                dve.wait_ge(c_vp, q + 1)
                dve.tensor_tensor(VBD[:, b, 4 * g:4 * g + n, 0:D], src[:, 0:n * D].rearrange("p (j d) -> p j d", d=D),
                                  own_head[:, 4 * g:4 * g + n, 0:D], ALU.mult).then_inc(c_vb, 1)

            for q in range(3):
                values_own(q, bank[q % 2])

            def centre(u):
                for g, (h0, n) in enumerate(GROUPS):
                    sc = bank[2 + g][:, 0:n * LC].rearrange("p (h k) -> p h k", k=LC)
                    m = mC[:, u % 2, h0:h0 + n]
                    dve.wait_ge(c_s, 3 * u + g + 1)
                    dve.tensor_reduce(m, sc, AX.X, ALU.max).then_inc(c_m, 1)
                    dve.wait_ge(c_m, 3 * u + g + 1)
                    if u >= 3 and g == 0:
                        dve.wait_ge(c_tp, 3 * (u - 2))
                    dve.tensor_tensor(SCS[u % 3][:, h0 * LC:(h0 + n) * LC].rearrange("p (h k) -> p h k", k=LC),
                                      sc, spread(m, 2, LC), ALU.subtract).then_inc(c_c, 1)

            def update(b):
                dve.wait_ge(c_y, b + 1)
                for i in range(TPB):
                    u = b * TPB + i
                    dve.wait_ge(c_xb, u + 1)
                    dve.scalar_tensor_tensor(X[:, u, :], bank[1][:, i * P:(i + 1) * P], gate[:, 1:2], X[:, u, :],
                                             ALU.mult, ALU.add).then_inc(s_xu, 1)

            def norm_twice(b):
                normalise(3, b)
                dve.wait_ge(s_rr, 4 * (b + 1))
                for i in range(TPB):
                    u = b * TPB + i
                    dve.wait_ge(s_xn, NT * 3 + u + 1)
                    dve.tensor_scalar(XR[:, u, :], XN[:, u, :], rms[:, u:u + 1], None, ALU.mult).then_inc(s_xr, 1)

            centre(0)
            centre(1)
            for u in range(NT):
                if u + 2 < NT:
                    centre(u + 2)
                dve.wait_ge(c_o, u + 1)
                dve.reciprocal(rC[:, u % 2, :], bank[0][:, D:DEN]).then_inc(c_r, 1)
                dve.wait_ge(c_r, u + 1)
                b, i = u // TPB, u % TPB
                for k in range(P // AA):
                    q = slice(k * AA, (k + 1) * AA)
                    ins = dve.tensor_tensor(OA[:, b, :, i * (P // AA) + k, :],
                                            bank[0][q, 0:D].rearrange("p (h d) -> p h d", d=DH1),
                                            spread(rC[q, u % 2, :], 2, DH1), ALU.mult)
                ins.then_inc(c_n, 1)
                if u < 3:
                    values_own(3 + u, bank[1])
                if u and i == 0:
                    update(b - 1)
                if u == TPB + 1:
                    row_means(3, 0)
                if u == TPB + 2:
                    norm_twice(0)
            low_tokens(3, [0])

            def rope_terms(r):
                kind, n = rope_block(r)
                G = n if kind == "k" else n // 2
                col = 2 * (G % KV * 3 + (2 if kind == "k" else n % 2))
                dve.wait_ge(d_qp, r + 1)
                if r >= 2:
                    wait_rope_sum(dve, r - 2)
                dve.stream_shuffle(T2[:, r % 2], rope_bank(r)[:, :], [c ^ 1 for c in range(32)]).then_inc(d_sh, 1)
                dve.scalar_tensor_tensor(T1[:, r % 2], rope_bank(r)[:, :], qkv_bias[:, col:col + 1], cosT,
                                         ALU.add, ALU.mult).then_inc(d_t, 1)
                dve.wait_ge(d_sh, r + 1)
                dve.scalar_tensor_tensor(T2[:, r % 2], T2[:, r % 2], qkv_bias[:, col + 1:col + 2], sinT,
                                         ALU.add, ALU.mult).then_inc(d_t, 1)
                if r < NDVE:
                    dve.wait_ge(d_t, 2 * r + 2)
                    if r >= 2:
                        dve.wait_ge(d_hi, r - 1)
                        dve.wait_ge(d_lo, r - 1)
                    dve.tensor_tensor(TS[:, r % 2], T1[:, r % 2], T2[:, r % 2], ALU.add).then_inc(d_ts0, 1)

            dve.wait_ge(d_cl, 16 * 9)
            for r in range(2):
                rope_terms(r)
            update(NB - 1)
            row_means(3, 1)
            dve.wait_ge(d_vl, 1)
            def values_out(k):
                dve.wait_ge(d_vp, k + 1)
                dve.tensor_tensor(VS[:, 2 * k:2 * k + 2], V_BANK[k][:, :].rearrange("p (u d) -> p u d", u=2),
                                  spread(v_bias[:], 1, 2), ALU.add).then_inc(d_v, 1)

            values_out(0)
            values_out(1)
            rope_terms(2)
            ropes = 3
            def unit_tokens(b):
                dve.wait_ge(s_rr, 4 * NB + 3 * (b + 1))
                for i in range(TPB):
                    u = b * TPB + i
                    dve.tensor_scalar(XR[:, u, :], X1[:, u, :], rms[:, u:u + 1], None, ALU.mult).then_inc(s_xr, 1)

            def low_up(e, s):
                dve.wait_ge(e_uh, e + 1)
                dve.tensor_tensor(ZU[2][:, s, :], ZU[0][:, s, :], ZU[1][:, s, :].bitcast(F32), ALU.subtract)\
                   .then_inc(e_ul, 1)

            def low_down(e, s):
                dve.wait_ge(e_wh, e + 1)
                dve.tensor_tensor(ZD[2][:, s, :], ZD[0][:, s, :], ZD[1][:, s, :].bitcast(F32), ALU.subtract)\
                   .then_inc(e_wl, 1)

            def router(b):
                us, us_ = slice(b * TPB, (b + 1) * TPB), range(b * TPB, (b + 1) * TPB)
                n, w = 10 * b, wt[:, us, :]
                logits_bank = (bank[1], bank[5])[b]

                def top():
                    dve.wait_ge(e_lg, b + 1)
                    dve.wait_ge(e_cl, 48)
                    dve.tensor_tensor(GZ[:, us, :], logits_bank[:, b * TPB * E1:(b + 1) * TPB * E1]
                                      .rearrange("p (u e) -> p u e", e=E1), spread(gate_b[:], 1, TPB), ALU.add)\
                       .then_inc(e_r, 1)
                    dve.wait_ge(e_r, n + 1)
                    for u in us_:
                        ins = dve.max(m8[:, u, :], GZ[:, u, :])
                    ins.then_inc(e_cm, 1)
                    dve.wait_ge(e_cm, b + 1)
                    dve.tensor_tensor(w, m8[:, us, 0:TOPK], m8[:, us, 0:1].broadcast_to([P, TPB, TOPK]),
                                      ALU.subtract).then_inc(e_r, 1)
                    for u in us_:
                        ins = dve.max_index(i8[:, u, :], m8[:, u, :], GZ[:, u, :])
                    ins.then_inc(e_r, 1)

                def softmax():
                    dve.wait_ge(e_r, n + 3)
                    dve.tensor_copy(if8[:, us, :], i8[:, us, 0:TOPK]).then_inc(e_r, 1)
                    dve.wait_ge(e_ex, b + 1)
                    dve.tensor_reduce(wsum[:, us], w, AX.X, ALU.add).then_inc(e_r, 1)
                    dve.wait_ge(e_r, n + 5)
                    dve.reciprocal(wsum[:, us], wsum[:, us]).then_inc(e_r, 1)
                    dve.wait_ge(e_r, n + 6)
                    dve.tensor_tensor(w, w, spread(wsum[:, us], 2, TOPK), ALU.mult).then_inc(e_r, 1)
                    dve.tensor_tensor(EQ4[:, us], spread(spread(experts[:], 1, TPB), 3, TOPK),
                                      spread(if8[:, us, :], 2, E1), ALU.is_equal).then_inc(e_r, 1)

                def combine():
                    dve.wait_ge(e_r, n + 8)
                    dve.tensor_tensor(EQ4[:, us], EQ4[:, us], spread(w, 2, E1), ALU.mult).then_inc(e_r, 1)
                    dve.wait_ge(e_r, n + 9)
                    dve.tensor_reduce(GZ[:, us, :], EQ4[:, us], AX.X, ALU.add).then_inc(e_r, 1)

                return top, softmax, combine

            dve.wait_ge(d_ns, 1)
            for q in range(NQ + TPB):
                if q < NQ:
                    n, i = q // TPB, q % TPB
                    dve.wait_ge(d_s, q + 1)
                    if q >= 4:
                        dve.wait_ge(d_tp, q - 3)
                    k0 = 128 if i == 0 else 0
                    for hd in range(2):
                        at = slice(hd * 256 + k0, (hd + 1) * 256)
                        ins = dve.tensor_tensor_reduce(SM[:, q % 4, at], bank[2 + q % 2][:, at], window[:, k0:256],
                                                       1.0, -3e38, ALU.add, ALU.max, mD[:, q % 4, hd:hd + 1])
                    ins.then_inc(d_m, 1)
                    c = n % PAIRS
                    dve.wait_ge(d_m, q + 1)
                    dve.scalar_tensor_tensor(nm[:, n % 2, i, :], mD[:, q % 4, :], -DH ** -0.5,
                                             nsink[:, 2 * c:2 * c + 2], ALU.mult, ALU.min).then_inc(d_nm, 1)
                if q == 1:
                    norm_twice(1)
                if q == 6:
                    low_tokens(3, [1])
                if q in (8, 10):
                    values_out((q - 4) // 2)
                if q in ROPE_AT:
                    rope_terms(ropes)
                    ropes += 1
                if q == SQ_AT + 5:
                    unit_tokens(0)
                if q == NQ - 6:
                    low_tokens(4, [0])
                if q in (NQ - 2, NQ + 1, NQ + 2):
                    router(0)[{NQ - 2: 0, NQ + 1: 1, NQ + 2: 2}[q]]()
                if q < NQ and i == TPB - 1:
                    if n >= 2:
                        dve.wait_ge(d_es, n - 1)
                    dve.wait_ge(d_nm, q + 1)
                    dve.tensor_tensor(zs[:, n % 2], nm[:, n % 2], spread(sink[:, 2 * c:2 * c + 2], 1, TPB), ALU.add)\
                        .then_inc(d_zs, 1)
                m, k = q // 4 - 1, q % 4
                if k == 3 and 0 <= m < NU:
                    dve.wait_ge(d_es, m + 1)
                    dve.wait_ge(d_e, TPB * (m + 1))
                    dve.tensor_tensor(den[:, m % 2], den[:, m % 2], lD[:, m % 2], ALU.add).then_inc(d_dn, 1)
                    dve.wait_ge(d_dn, m + 1)
                    dve.reciprocal(den[:, m % 2], den[:, m % 2]).then_inc(d_rc, 1)
                    dve.wait_ge(d_rc, m + 1)
                    dve.wait_ge(d_y, TPB * (m + 1))
                    if m >= 2:
                        dve.wait_ge(d_yt, m - 1)
                    dve.tensor_tensor(YS[:, m % 2].rearrange("p (x d) -> p x d", d=DH),
                                      bank[6][:, :].rearrange("p (x d) -> p x d", d=DH),
                                      spread(den[:, m % 2].rearrange("p i h -> p (i h)"), 2, DH), ALU.mult)\
                        .then_inc(d_ys, 1)
                if q == TPB * (PAIRS + 2):
                    dve.wait_ge(d_x0, NB)
                    dve.wait_ge(d_pr, PAIRS)
                    dve.tensor_tensor(X1[:, 0:TPB, :].rearrange("p i d -> p (i d)"),
                                      X1[:, 0:TPB, :].rearrange("p i d -> p (i d)"), bank[7][:, :], ALU.add)\
                        .then_inc(d_x1, 1)
            dve.wait_ge(d_pr, NU)
            dve.tensor_tensor(X1[:, TPB:, :].rearrange("p i d -> p (i d)"),
                              X1[:, TPB:, :].rearrange("p i d -> p (i d)"), bank[7][:, :], ALU.add).then_inc(d_x1, 1)

            unit_tokens(1)
            low_tokens(4, [1])
            for s in range(3):
                low_up(s, s)
            for s in range(2):
                low_down(s, s)
            def weights_out(b):
                dve.wait_ge(e_ctp, b + 1)
                dve.tensor_copy(CT1[:, b * 512:(b + 1) * 512], bank[1 + 2 * b][0:E1, :]).then_inc(e_ct, 1)

            weights_out(0)
            for part in router(1):
                part()
            weights_out(1)

            def low_e(n, k, first):
                dve.wait_ge(e_hh, n + 1)
                if not first:
                    dve.wait_ge(e_dn, n + 1 - H_RING)
                r = k % H_RING
                dve.tensor_tensor(HL[:, r, :], HC[:, r, :], HH[:, r, :].bitcast(F32), ALU.subtract).then_inc(e_hl, 1)

            LO1 = 1

            def quad(p, first, last):
                for k in range(QUAD * HALVES):
                    n, s, h = p * QUAD * HALVES + k, k // HALVES, k % HALVES
                    dve.wait_ge(e_u, n + 1)
                    dve.wait_ge(e_c, n + 1)
                    dve.tensor_tensor(HC[:, k % H_RING, :], bank[4 + k % 2][:, :], HC[:, k % H_RING, :], ALU.mult)\
                       .then_inc(e_mu, 1)
                    if not first or k >= LO1:
                        low_e(n - LO1, (k - LO1) % H_RING, first and k - LO1 < H_RING)
                    if h == 0 and not (last and s >= 2):
                        low_down(p * QUAD + s + 2, (s + 2) % QUAD)
                    if h == 1 and not (last and s >= 1):
                        low_up(p * QUAD + s + 3, (s + 3) % QUAD)
                if last:
                    for k in range(QUAD * HALVES - LO1, QUAD * HALVES):
                        low_e(p * QUAD * HALVES + k, k, False)

            over_pairs(dve, E1 // QUAD, quad)
            add_back(1, 3)


_NAMES = ("x", "ctx_768", "g_xattn", "g_ffn", "L0_xattn_Wq", "L0_xattn_bq", "L0_xattn_Wk", "L0_xattn_bk",
          "L0_xattn_Wv", "L0_xattn_bv", "L0_ffn_Wg", "L0_ffn_bg", "L0_ffn_W1", "L0_ffn_b1", "L0_ffn_W2", "L0_ffn_b2",
          "L1_xattn_q_w", "L1_xattn_q_b", "L1_xattn_k_w", "L1_xattn_k_b", "L1_xattn_v_w", "L1_xattn_v_b",
          "L1_xattn_o_w", "L1_xattn_o_b", "L1_ffn_attn_norm_w", "L1_ffn_ffn_norm_w", "L1_ffn_qkv_w", "L1_ffn_qkv_b",
          "L1_ffn_proj_w", "L1_ffn_proj_b", "L1_ffn_attn_sink", "L1_ffn_gate_w", "L1_ffn_gate_b", "L1_ffn_W_up",
          "L1_ffn_W_down")
_UNUSED = ("L1_xattn_k_w", "L1_xattn_k_b")


def kernel(**inputs):
    import concourse.bacc as bacc
    from concourse.bass_utils import run_bass_kernel_spmd

    nc = bacc.Bacc("TRN2", target_bir_lowering=False, num_devices=1)
    arrays = {name: np.ascontiguousarray(inputs[name]) for name in _NAMES if name not in _UNUSED}
    arrays.update(constants())
    arrays.update(qkv_by_group(arrays["L1_ffn_qkv_w"], arrays["L1_ffn_qkv_b"]))
    b1 = arrays.pop("L0_ffn_b1")
    arrays["L0_ffn_b1_columns"] = np.ascontiguousarray(b1.reshape(len(b1), -1, P).transpose(0, 2, 1))
    t, named = {}, {}
    for name, a in arrays.items():
        named[f"in_{name}_dram"] = a
        t[name] = nc.dram_tensor(f"in_{name}_dram", a.shape, mybir.dt.from_np(a.dtype), kind="ExternalInput").ap()
    out = nc.dram_tensor("out_0_dram", arrays["x"].shape, F32, kind="ExternalOutput").ap()
    flamingo_two_layers(nc, t, out)
    r = run_bass_kernel_spmd(nc, [named], core_ids=[0])
    return r.results[0]["out_0_dram"]
```
